# Optimizing a Trainium2 kernel written in Bass

```python
import numpy as np
import jax
import jax.numpy as jnp

def _softmax(x, axis=-1):
    return jax.nn.softmax(x, axis=axis)

def _gelu(x):
    return jax.nn.gelu(x, approximate=True)

def _silu(x):
    return jax.nn.silu(x)

def _sigmoid(x):
    return jax.nn.sigmoid(x)

def _layernorm(x, axis=-1, eps=1e-05):
    m = jnp.mean(x, axis=axis, keepdims=True)
    v = jnp.var(x, axis=axis, keepdims=True)
    return (x - m) / jnp.sqrt(v + eps)

def _scatter_add(tgt, idx, src, axis=0):
    return tgt.at[idx].add(src)

def _segment_sum(src, seg, n):
    return jax.ops.segment_sum(src, seg, n)
kernel_name = 'mk_xattn_ffn_d4_seqx_r8_db995e'

def setup_inputs(seed: int=0):
    np.random.seed(seed)
    _w = jnp.asarray

    def _rec_inputs():
        import jax
        import jax.numpy as jnp
        _rk = jax.random.key(seed)
        x = 7.22e-05 + 1 * jax.random.normal(jax.random.fold_in(_rk, 1), (16, 64, 128), jnp.float32)
        _lenS = 64 - jax.random.randint(jax.random.fold_in(_rk, 7), (16,), 0, max(1, 64 // 4) + 1, jnp.int32)
        _lenS2 = 64 - jax.random.randint(jax.random.fold_in(_rk, 8), (16,), 0, max(1, 64 // 4) + 1, jnp.int32)
        _ctx_1024P = jax.random.normal(jax.random.fold_in(_rk, 11), (16, 16, 128), jnp.float32)
        _ctx_1024c = jax.random.dirichlet(jax.random.fold_in(_rk, 511), 0.3 * jnp.ones((16,), jnp.float32), (16, 64))
        _ctx_1024t = jnp.einsum('bsk,bkd->bsd', _ctx_1024c, _ctx_1024P)
        _ctx_1024t = _ctx_1024t * jax.lax.rsqrt(jnp.mean(jnp.square(_ctx_1024t)) + 1e-12) * 0.953939
        ctx_1024 = 4.13588e-05 + 0.999923 * (_ctx_1024t + 0.3 * jax.random.normal(jax.random.fold_in(_rk, 611), (16, 64, 128), jnp.float32))
        fside_BxSxS2_0 = -1.47943e-05 + 1.00017 * jax.random.normal(jax.random.fold_in(_rk, 14), (16, 64, 64), jnp.float32)
        _validS = jnp.arange(64)[None, :] < _lenS[:, None]
        _validS2 = jnp.arange(64)[None, :] < _lenS2[:, None]
        _causal = jnp.tril(jnp.ones((64, 64), dtype=bool))
        mask_Bx1xS2_bf1 = jnp.ones((16, 1, 64), dtype=bool)
        mask_BxS2_bf1 = jnp.ones((16, 64), dtype=bool)
        return (x, ctx_1024, fside_BxSxS2_0, mask_Bx1xS2_bf1, mask_BxS2_bf1)
    x, ctx_1024, fside_BxSxS2_0, mask_Bx1xS2_bf1, mask_BxS2_bf1 = _rec_inputs()

    def _L0_xattn_setup():
        import jax, jax.numpy as jnp
        import numpy as np
        D_MODEL = 128
        N_HEADS = 16
        D_K = D_MODEL // N_HEADS
        key = jax.random.key(seed)
        ks = jax.random.split(key, 12)
        B, S, D = (4, 256, D_MODEL)
        s = 1.0 / np.sqrt(D)
        return {'Q': jax.random.normal(ks[0], (B, S, D), jnp.float32), 'K': jax.random.normal(ks[1], (B, S, D), jnp.float32), 'V': jax.random.normal(ks[2], (B, S, D), jnp.float32), 'mask': jnp.ones((B, 1, S), dtype=bool), 'Wq': jax.random.normal(ks[3], (D, D), jnp.float32) * s, 'bq': jnp.zeros((D,), jnp.float32), 'Wk': jax.random.normal(ks[4], (D, D), jnp.float32) * s, 'bk': jnp.zeros((D,), jnp.float32), 'Wv': jax.random.normal(ks[5], (D, D), jnp.float32) * s, 'bv': jnp.zeros((D,), jnp.float32), 'Wo': jax.random.normal(ks[6], (D, D), jnp.float32) * s, 'bo': jnp.zeros((D,), jnp.float32)}
    _L0_xattn_all = _L0_xattn_setup()
    _L0_xattn_in = {k: v for k, v in _L0_xattn_all.items() if k in ('Wq', 'bq', 'Wk', 'bk', 'Wv', 'bv', 'Wo', 'bo')}
    del _L0_xattn_all

    def _L0_ffn_setup():
        import jax, jax.numpy as jnp
        import numpy as np
        E, K, H, F, R = (8, 2, 128, 256, 64)
        B, S = (2, 256)
        key = jax.random.key(seed)
        k0, k1, k2, k3, k4 = jax.random.split(key, 5)
        return {'hidden_states': jax.random.normal(k0, (B, S, H), dtype=jnp.float32), 'W_A': jax.random.normal(k1, (E, R, H), dtype=jnp.float32) * 0.02, 'W_B': jax.random.normal(k2, (E, F, R), dtype=jnp.float32) * 0.02, 'W_up': jax.random.normal(k3, (E, F, H), dtype=jnp.float32) * 0.02, 'W_down': jax.random.normal(k4, (E, H, F), dtype=jnp.float32) * 0.02}
    _L0_ffn_all = _L0_ffn_setup()
    _L0_ffn_in = {k: v for k, v in _L0_ffn_all.items() if k in ('W_A', 'W_B', 'W_up', 'W_down')}
    del _L0_ffn_all

    def _L1_xattn_setup():
        import jax, jax.numpy as jnp
        import numpy as np
        B, N, HID, HEADS, TOPK = (2, 256, 128, 16, 64)
        DHEAD = HID // HEADS

        def _split_heads(x):
            b, n, _ = x.shape
            return x.reshape(b, n, HEADS, DHEAD).transpose(0, 2, 1, 3)
        key = jax.random.key(seed)
        ks = jax.random.split(key, 12)
        s = 1.0 / np.sqrt(HID)
        inp = {'q': jax.random.normal(ks[0], (B, N, HID), jnp.float32), 'k': jax.random.normal(ks[1], (B, N, HID), jnp.float32), 'v': jax.random.normal(ks[2], (B, N, HID), jnp.float32), 'mask': jnp.ones((B, N), jnp.bool_), 'topk': TOPK, 'wq_w': jax.random.normal(ks[3], (HID, HID), jnp.float32) * s, 'wq_b': jnp.zeros((HID,), jnp.float32), 'wk_w': jax.random.normal(ks[4], (HID, HID), jnp.float32) * s, 'wk_b': jnp.zeros((HID,), jnp.float32), 'wv_w': jax.random.normal(ks[5], (HID, HID), jnp.float32) * s, 'wv_b': jnp.zeros((HID,), jnp.float32), 'wo_w': jax.random.normal(ks[6], (HID, HID), jnp.float32) * s, 'wo_b': jnp.zeros((HID,), jnp.float32)}
        return inp
    _L1_xattn_all = _L1_xattn_setup()
    _L1_xattn_in = {k: v for k, v in _L1_xattn_all.items() if k in ('wq_w', 'wq_b', 'wk_w', 'wk_b', 'wv_w', 'wv_b', 'wo_w', 'wo_b')}
    del _L1_xattn_all

    def _L1_ffn_setup():
        import jax, jax.numpy as jnp
        import numpy as np
        E = 8
        TOPK = 2

        def _moe_forward(x, Wg, W1, W2, W3):
            B, S, D = x.shape
            xt = x.reshape(-1, D)
            T = xt.shape[0]
            logits = xt @ Wg.T
            scores = jax.nn.softmax(logits, axis=-1)
            w, idx = jax.lax.top_k(scores, TOPK)
            w = w / (w.sum(axis=-1, keepdims=True) + 1e-20)
            cw = jnp.zeros((T, E), xt.dtype).at[jnp.arange(T)[:, None], idx].add(w)
            h = jax.nn.silu(jnp.einsum('td,ehd->teh', xt, W1)) * jnp.einsum('td,ehd->teh', xt, W3)
            out = jnp.einsum('teh,edh->ted', h, W2)
            y = jnp.einsum('te,ted->td', cw, out)
            return y.reshape(B, S, D)
        key = jax.random.key(seed)
        k0, k1, k2, k3, k4 = jax.random.split(key, 5)
        B, S, D, H = (1, 256, 128, 352)
        scale = 0.02
        x = jax.random.normal(k0, (B, S, D), jnp.float32)
        Wg = jax.random.normal(k1, (E, D), jnp.float32) * scale
        W1 = jax.random.normal(k2, (E, H, D), jnp.float32) * scale
        W2 = jax.random.normal(k3, (E, D, H), jnp.float32) * scale
        W3 = jax.random.normal(k4, (E, H, D), jnp.float32) * scale
        return {'x': x, 'Wg': Wg, 'W1': W1, 'W2': W2, 'W3': W3}
    _L1_ffn_all = _L1_ffn_setup()
    _L1_ffn_in = {k: v for k, v in _L1_ffn_all.items() if k in ('Wg', 'W1', 'W2', 'W3')}
    del _L1_ffn_all

    def _L2_xattn_setup():
        import jax, jax.numpy as jnp
        import numpy as np
        D_K = 128
        HEADS = 16
        HK = 64
        HV = 64
        key = jax.random.key(seed)
        ks = jax.random.split(key, 12)
        B, S = (4, 256)
        sc_in = 1.0 / np.sqrt(D_K)
        sc_u = 1.0 / np.sqrt(HV * HEADS)
        return {'q': jax.random.normal(ks[0], (B, S, D_K), jnp.float32), 'k': jax.random.normal(ks[1], (B, S, D_K), jnp.float32), 'v': jax.random.normal(ks[2], (B, S, D_K), jnp.float32), 'Wq': jax.random.normal(ks[3], (D_K, HK * HEADS), jnp.float32) * sc_in, 'bq': jax.random.normal(ks[4], (HK * HEADS,), jnp.float32) * sc_in, 'Wk': jax.random.normal(ks[5], (D_K, HK * HEADS), jnp.float32) * sc_in, 'bk': jax.random.normal(ks[6], (HK * HEADS,), jnp.float32) * sc_in, 'Wv': jax.random.normal(ks[7], (D_K, HV * HEADS), jnp.float32) * sc_in, 'bv': jax.random.normal(ks[8], (HV * HEADS,), jnp.float32) * sc_in, 'Wu': jax.random.normal(ks[9], (HV * HEADS, D_K), jnp.float32) * sc_u, 'bu': jax.random.normal(ks[10], (D_K,), jnp.float32) * sc_u}
    _L2_xattn_all = _L2_xattn_setup()
    _L2_xattn_in = {k: v for k, v in _L2_xattn_all.items() if k in ('Wq', 'bq', 'Wk', 'bk', 'Wv', 'bv', 'Wu', 'bu')}
    del _L2_xattn_all

    def _L2_ffn_setup():
        import jax, jax.numpy as jnp
        import numpy as np
        NEG_INF = -1e+30

        def _moe_forward(x, router_w, router_b, w1, b1, w2, b2, top_k=2):
            B, S, D = x.shape
            E = router_w.shape[1]
            logits = jnp.einsum('bsd,de->bse', x, router_w) + router_b
            top_vals, top_idx = jax.lax.top_k(logits, top_k)
            keep = jax.nn.one_hot(top_idx, E, dtype=logits.dtype).sum(-2) > 0
            sparse_logits = jnp.where(keep, logits, NEG_INF)
            gating = jax.nn.softmax(sparse_logits, axis=-1)
            xf = x.reshape(-1, D)
            gf = gating.reshape(-1, E)
            h = jax.nn.relu(jnp.einsum('td,edh->eth', xf, w1) + b1[:, None, :])
            y = jnp.einsum('eth,ehd->etd', h, w2) + b2[:, None, :]
            out = jnp.einsum('etd,te->td', y, gf)
            return out.reshape(B, S, D)
        key = jax.random.key(seed)
        ks = jax.random.split(key, 5)
        B, S, D, E, H = (2, 256, 128, 8, 512)
        scale = 0.02
        return {'x': jax.random.normal(ks[0], (B, S, D), dtype=jnp.float32), 'router_w': jax.random.normal(ks[1], (D, E), dtype=jnp.float32) * scale, 'router_b': jnp.zeros((E,), dtype=jnp.float32), 'w1': jax.random.normal(ks[2], (E, D, H), dtype=jnp.float32) * scale, 'b1': jnp.zeros((E, H), dtype=jnp.float32), 'w2': jax.random.normal(ks[3], (E, H, D), dtype=jnp.float32) * scale, 'b2': jnp.zeros((E, D), dtype=jnp.float32)}
    _L2_ffn_all = _L2_ffn_setup()
    _L2_ffn_in = {k: v for k, v in _L2_ffn_all.items() if k in ('router_w', 'router_b', 'w1', 'b1', 'w2', 'b2')}
    del _L2_ffn_all

    def _L3_xattn_setup():
        import jax, jax.numpy as jnp
        import numpy as np
        B, N, DIM, H = (4, 256, 128, 8)
        HD = DIM // H
        SCALE = HD ** (-0.5)
        key = jax.random.key(seed)
        ks = jax.random.split(key, 9)
        inp = {'q': jax.random.normal(ks[0], (B, N, DIM), dtype=jnp.float32), 'k': jax.random.normal(ks[1], (B, N, DIM), dtype=jnp.float32), 'v': jax.random.normal(ks[2], (B, N, DIM), dtype=jnp.float32), 'trans_mat': jax.random.normal(ks[3], (B, N, N), dtype=jnp.float32), 'Wq': jax.random.normal(ks[4], (DIM, DIM), dtype=jnp.float32) * DIM ** (-0.5), 'Wk': jax.random.normal(ks[5], (DIM, DIM), dtype=jnp.float32) * DIM ** (-0.5), 'Wv': jax.random.normal(ks[6], (DIM, DIM), dtype=jnp.float32) * DIM ** (-0.5), 'Wp': jax.random.normal(ks[7], (DIM, DIM), dtype=jnp.float32) * DIM ** (-0.5), 'bp': jax.random.normal(ks[8], (DIM,), dtype=jnp.float32) * 0.01}
        return inp
    _L3_xattn_all = _L3_xattn_setup()
    _L3_xattn_in = {k: v for k, v in _L3_xattn_all.items() if k in ('Wq', 'Wk', 'Wv', 'Wp', 'bp')}
    del _L3_xattn_all

    def _L3_ffn_setup():
        import jax, jax.numpy as jnp
        import numpy as np
        N_EMBD = 128
        N_EXP = 8
        TOP_K = 2
        CAPACITY = 512
        D_FF = 3 * N_EMBD
        key = jax.random.key(seed)
        k1, k2, k3, k4 = jax.random.split(key, 4)
        x = jax.random.normal(k1, (8, 256, N_EMBD), dtype=jnp.float32)
        w_gate = jax.random.normal(k2, (N_EMBD, N_EXP), dtype=jnp.float32) * 0.02
        c_fc = jax.random.normal(k3, (N_EXP, N_EMBD, D_FF), dtype=jnp.float32) * 0.02
        c_proj = jax.random.normal(k4, (N_EXP, D_FF // 2, N_EMBD), dtype=jnp.float32) * 0.02
        return {'x': x, 'w_gate': w_gate, 'c_fc': c_fc, 'c_proj': c_proj}
    _L3_ffn_all = _L3_ffn_setup()
    _L3_ffn_in = {k: v for k, v in _L3_ffn_all.items() if k in ('w_gate', 'c_fc', 'c_proj')}
    del _L3_ffn_all
    return {'x': x, 'ctx_1024': ctx_1024, 'fside_BxSxS2_0': fside_BxSxS2_0, 'mask_Bx1xS2_bf1': mask_Bx1xS2_bf1, 'mask_BxS2_bf1': mask_BxS2_bf1, 'L0_xattn_Wq': _L0_xattn_in['Wq'], 'L0_xattn_bq': _L0_xattn_in['bq'], 'L0_xattn_Wk': _L0_xattn_in['Wk'], 'L0_xattn_bk': _L0_xattn_in['bk'], 'L0_xattn_Wv': _L0_xattn_in['Wv'], 'L0_xattn_bv': _L0_xattn_in['bv'], 'L0_xattn_Wo': _L0_xattn_in['Wo'], 'L0_xattn_bo': _L0_xattn_in['bo'], 'L0_ffn_W_A': _L0_ffn_in['W_A'], 'L0_ffn_W_B': _L0_ffn_in['W_B'], 'L0_ffn_W_up': _L0_ffn_in['W_up'], 'L0_ffn_W_down': _L0_ffn_in['W_down'], 'L1_xattn_wq_w': _L1_xattn_in['wq_w'], 'L1_xattn_wq_b': _L1_xattn_in['wq_b'], 'L1_xattn_wk_w': _L1_xattn_in['wk_w'], 'L1_xattn_wk_b': _L1_xattn_in['wk_b'], 'L1_xattn_wv_w': _L1_xattn_in['wv_w'], 'L1_xattn_wv_b': _L1_xattn_in['wv_b'], 'L1_xattn_wo_w': _L1_xattn_in['wo_w'], 'L1_xattn_wo_b': _L1_xattn_in['wo_b'], 'L1_ffn_Wg': _L1_ffn_in['Wg'], 'L1_ffn_W1': _L1_ffn_in['W1'], 'L1_ffn_W2': _L1_ffn_in['W2'], 'L1_ffn_W3': _L1_ffn_in['W3'], 'L2_xattn_Wq': _L2_xattn_in['Wq'], 'L2_xattn_bq': _L2_xattn_in['bq'], 'L2_xattn_Wk': _L2_xattn_in['Wk'], 'L2_xattn_bk': _L2_xattn_in['bk'], 'L2_xattn_Wv': _L2_xattn_in['Wv'], 'L2_xattn_bv': _L2_xattn_in['bv'], 'L2_xattn_Wu': _L2_xattn_in['Wu'], 'L2_xattn_bu': _L2_xattn_in['bu'], 'L2_ffn_router_w': _L2_ffn_in['router_w'], 'L2_ffn_router_b': _L2_ffn_in['router_b'], 'L2_ffn_w1': _L2_ffn_in['w1'], 'L2_ffn_b1': _L2_ffn_in['b1'], 'L2_ffn_w2': _L2_ffn_in['w2'], 'L2_ffn_b2': _L2_ffn_in['b2'], 'L3_xattn_Wq': _L3_xattn_in['Wq'], 'L3_xattn_Wk': _L3_xattn_in['Wk'], 'L3_xattn_Wv': _L3_xattn_in['Wv'], 'L3_xattn_Wp': _L3_xattn_in['Wp'], 'L3_xattn_bp': _L3_xattn_in['bp'], 'L3_ffn_w_gate': _L3_ffn_in['w_gate'], 'L3_ffn_c_fc': _L3_ffn_in['c_fc'], 'L3_ffn_c_proj': _L3_ffn_in['c_proj']}

def reference(x, ctx_1024, fside_BxSxS2_0, mask_Bx1xS2_bf1, mask_BxS2_bf1, L0_xattn_Wq, L0_xattn_bq, L0_xattn_Wk, L0_xattn_bk, L0_xattn_Wv, L0_xattn_bv, L0_xattn_Wo, L0_xattn_bo, L0_ffn_W_A, L0_ffn_W_B, L0_ffn_W_up, L0_ffn_W_down, L1_xattn_wq_w, L1_xattn_wq_b, L1_xattn_wk_w, L1_xattn_wk_b, L1_xattn_wv_w, L1_xattn_wv_b, L1_xattn_wo_w, L1_xattn_wo_b, L1_ffn_Wg, L1_ffn_W1, L1_ffn_W2, L1_ffn_W3, L2_xattn_Wq, L2_xattn_bq, L2_xattn_Wk, L2_xattn_bk, L2_xattn_Wv, L2_xattn_bv, L2_xattn_Wu, L2_xattn_bu, L2_ffn_router_w, L2_ffn_router_b, L2_ffn_w1, L2_ffn_b1, L2_ffn_w2, L2_ffn_b2, L3_xattn_Wq, L3_xattn_Wk, L3_xattn_Wv, L3_xattn_Wp, L3_xattn_bp, L3_ffn_w_gate, L3_ffn_c_fc, L3_ffn_c_proj):
    import jax
    import jax.numpy as jnp

    def _L0_xattn_ref(Q, K, V, mask, Wq, bq, Wk, bk, Wv, bv, Wo, bo):
        import jax, jax.numpy as jnp
        import numpy as np
        D_MODEL = 128
        N_HEADS = 16
        D_K = D_MODEL // N_HEADS
        B, S, D = Q.shape
        H, dk = (N_HEADS, D_K)
        q = (Q @ Wq + bq).reshape(B, S, H, dk).transpose(0, 2, 1, 3)
        k = (K @ Wk + bk).reshape(B, S, H, dk).transpose(0, 2, 1, 3)
        v = (V @ Wv + bv).reshape(B, S, H, dk).transpose(0, 2, 1, 3)
        scores = jnp.einsum('bhqd,bhkd->bhqk', q, k) / jnp.sqrt(jnp.float32(dk))
        m = mask[:, None, :, :]
        scores = jnp.where(m, scores, jnp.float32(-1000000000.0))
        att = jax.nn.softmax(scores, axis=-1)
        out = jnp.einsum('bhqk,bhkd->bhqd', att, v)
        out = out.transpose(0, 2, 1, 3).reshape(B, S, D)
        return out @ Wo + bo

    def _L0_ffn_ref(hidden_states, W_A, W_B, W_up, W_down):
        import jax, jax.numpy as jnp
        import numpy as np
        E, K, H, F, R = (8, 2, 128, 256, 64)
        B, S = (2, 256)
        orig_shape = hidden_states.shape
        x = hidden_states.reshape(-1, orig_shape[-1])
        num_experts = W_A.shape[0]
        gate_hidden = jnp.einsum('nh,erh->ner', x, W_A)
        scores = jnp.sqrt(jnp.sum(gate_hidden * gate_hidden, axis=-1))
        topk_scores, topk_idx = jax.lax.top_k(scores, K)
        topk_w = jax.nn.softmax(topk_scores, axis=-1)
        w_full = jnp.sum(jax.nn.one_hot(topk_idx, num_experts, dtype=topk_w.dtype) * topk_w[..., None], axis=1)
        g = jnp.einsum('ner,efr->nef', gate_hidden, W_B)
        up = jnp.einsum('nh,efh->nef', x, W_up)
        y = jnp.einsum('nef,ehf->neh', jax.nn.silu(g) * up, W_down)
        out = jnp.einsum('neh,ne->nh', y, w_full)
        return out.reshape(orig_shape)

    def _L1_xattn_ref(q, k, v, mask, topk, wq_w, wq_b, wk_w, wk_b, wv_w, wv_b, wo_w, wo_b):
        import jax, jax.numpy as jnp
        import numpy as np
        B, N, HID, HEADS, TOPK = (2, 256, 128, 16, 64)
        DHEAD = HID // HEADS

        def _split_heads(x):
            b, n, _ = x.shape
            return x.reshape(b, n, HEADS, DHEAD).transpose(0, 2, 1, 3)
        qh = _split_heads(q @ wq_w.T + wq_b)
        kh = _split_heads(k @ wk_w.T + wk_b)
        vh = _split_heads(v @ wv_w.T + wv_b)
        scores = jnp.einsum('bhqd,bhkd->bhqk', qh, kh) / np.sqrt(DHEAD)
        neg = jnp.finfo(scores.dtype).min
        scores = jnp.where(mask[:, None, None, :], scores, neg)
        if topk and 0 < topk < scores.shape[-1]:
            vals, idx = jax.lax.top_k(scores, topk)
            b, h, nq, _ = scores.shape
            bI = jnp.arange(b)[:, None, None, None]
            hI = jnp.arange(h)[None, :, None, None]
            qI = jnp.arange(nq)[None, None, :, None]
            scores = jnp.full_like(scores, neg).at[bI, hI, qI, idx].set(vals)
        probs = jax.nn.softmax(scores, axis=-1)
        ctx = jnp.einsum('bhqk,bhkd->bhqd', probs, vh)
        ctx = ctx.transpose(0, 2, 1, 3).reshape(q.shape[0], q.shape[1], HID)
        return ctx @ wo_w.T + wo_b

    def _L1_ffn_ref(x, Wg, W1, W2, W3):
        import jax, jax.numpy as jnp
        import numpy as np
        E = 8
        TOPK = 2

        def _moe_forward(x, Wg, W1, W2, W3):
            B, S, D = x.shape
            xt = x.reshape(-1, D)
            T = xt.shape[0]
            logits = xt @ Wg.T
            scores = jax.nn.softmax(logits, axis=-1)
            w, idx = jax.lax.top_k(scores, TOPK)
            w = w / (w.sum(axis=-1, keepdims=True) + 1e-20)
            cw = jnp.zeros((T, E), xt.dtype).at[jnp.arange(T)[:, None], idx].add(w)
            h = jax.nn.silu(jnp.einsum('td,ehd->teh', xt, W1)) * jnp.einsum('td,ehd->teh', xt, W3)
            out = jnp.einsum('teh,edh->ted', h, W2)
            y = jnp.einsum('te,ted->td', cw, out)
            return y.reshape(B, S, D)
        return _moe_forward(x, Wg, W1, W2, W3)

    def _L2_xattn_ref(q, k, v, Wq, bq, Wk, bk, Wv, bv, Wu, bu):
        import jax, jax.numpy as jnp
        import numpy as np
        D_K = 128
        HEADS = 16
        HK = 64
        HV = 64
        B, S, _ = q.shape
        qh = (q @ Wq + bq).reshape(B, S, HEADS, HK).transpose(0, 2, 1, 3)
        kh = (k @ Wk + bk).reshape(B, S, HEADS, HK).transpose(0, 2, 1, 3)
        vh = (v @ Wv + bv).reshape(B, S, HEADS, HV).transpose(0, 2, 1, 3)
        scores = jnp.einsum('bhqd,bhkd->bhqk', qh, kh) / jnp.sqrt(jnp.asarray(HK, qh.dtype))
        attn = jax.nn.softmax(scores, axis=-1)
        out = jnp.einsum('bhqk,bhkd->bhqd', attn, vh)
        merged = out.transpose(0, 2, 1, 3).reshape(B, S, HEADS * HV)
        return merged @ Wu + bu

    def _L2_ffn_ref(x, router_w, router_b, w1, b1, w2, b2):
        import jax, jax.numpy as jnp
        import numpy as np
        NEG_INF = -1e+30

        def _moe_forward(x, router_w, router_b, w1, b1, w2, b2, top_k=2):
            B, S, D = x.shape
            E = router_w.shape[1]
            logits = jnp.einsum('bsd,de->bse', x, router_w) + router_b
            top_vals, top_idx = jax.lax.top_k(logits, top_k)
            keep = jax.nn.one_hot(top_idx, E, dtype=logits.dtype).sum(-2) > 0
            sparse_logits = jnp.where(keep, logits, NEG_INF)
            gating = jax.nn.softmax(sparse_logits, axis=-1)
            xf = x.reshape(-1, D)
            gf = gating.reshape(-1, E)
            h = jax.nn.relu(jnp.einsum('td,edh->eth', xf, w1) + b1[:, None, :])
            y = jnp.einsum('eth,ehd->etd', h, w2) + b2[:, None, :]
            out = jnp.einsum('etd,te->td', y, gf)
            return out.reshape(B, S, D)
        return _moe_forward(x, router_w, router_b, w1, b1, w2, b2, top_k=2)

    def _L3_xattn_ref(q, k, v, trans_mat, Wq, Wk, Wv, Wp, bp):
        import jax, jax.numpy as jnp
        import numpy as np
        B, N, DIM, H = (4, 256, 128, 8)
        HD = DIM // H
        SCALE = HD ** (-0.5)
        Bq, Nq, C = q.shape
        qh = (q @ Wq.T).reshape(Bq, Nq, H, HD).transpose(0, 2, 1, 3)
        kh = (k @ Wk.T).reshape(Bq, -1, H, HD).transpose(0, 2, 1, 3)
        vh = (v @ Wv.T).reshape(Bq, -1, H, HD).transpose(0, 2, 1, 3)
        scores = jnp.einsum('bhqd,bhkd->bhqk', qh, kh) * SCALE
        gated = scores * trans_mat[:, None, :, :]
        sm = jax.nn.softmax(gated, axis=-1)
        attn = jnp.where(gated != 0, sm, jnp.zeros((), dtype=sm.dtype))
        x = jnp.einsum('bhqk,bhkd->bhqd', attn, vh)
        x = x.transpose(0, 2, 1, 3).reshape(Bq, Nq, C)
        return x @ Wp.T + bp

    def _L3_ffn_ref(x, w_gate, c_fc, c_proj):
        import jax, jax.numpy as jnp
        import numpy as np
        N_EMBD = 128
        N_EXP = 8
        TOP_K = 2
        CAPACITY = 512
        D_FF = 3 * N_EMBD
        B, T, d = x.shape
        N = B * T
        xf = x.reshape(N, d)
        scores = jax.nn.softmax(xf @ w_gate, axis=-1)
        weights, idx = jax.lax.top_k(scores, TOP_K)
        flat_e = idx.reshape(-1)
        tok = jnp.repeat(jnp.arange(N), TOP_K)
        oh = jax.nn.one_hot(flat_e, N_EXP, dtype=jnp.int32)
        pos = (jnp.cumsum(oh, axis=0) * oh).sum(-1) - 1
        valid = pos < CAPACITY
        pos_c = jnp.where(valid, pos, 0)
        vmask = valid.astype(x.dtype)[:, None]
        exp_x = jnp.zeros((N_EXP, CAPACITY, d), x.dtype)
        exp_x = exp_x.at[flat_e, pos_c].add(xf[tok] * vmask)
        h = jnp.einsum('ecd,edf->ecf', exp_x, c_fc)
        a, g = jnp.split(h, 2, axis=-1)
        h = jax.nn.silu(a) * g
        exp_out = jnp.einsum('ecf,efd->ecd', h, c_proj)
        gathered = exp_out[flat_e, pos_c]
        w = weights.reshape(-1)[:, None] * vmask
        out = (gathered * w).reshape(N, TOP_K, d).sum(axis=1)
        return out.reshape(B, T, d)
    x = x + _L0_xattn_ref(_layernorm(x, axis=-1), ctx_1024, ctx_1024, mask_Bx1xS2_bf1, L0_xattn_Wq, L0_xattn_bq, L0_xattn_Wk, L0_xattn_bk, L0_xattn_Wv, L0_xattn_bv, L0_xattn_Wo, L0_xattn_bo)
    x = x + _L0_ffn_ref(_layernorm(x, axis=-1), L0_ffn_W_A, L0_ffn_W_B, L0_ffn_W_up, L0_ffn_W_down)
    x = x + _L1_xattn_ref(_layernorm(x, axis=-1), ctx_1024, ctx_1024, mask_BxS2_bf1, 64, L1_xattn_wq_w, L1_xattn_wq_b, L1_xattn_wk_w, L1_xattn_wk_b, L1_xattn_wv_w, L1_xattn_wv_b, L1_xattn_wo_w, L1_xattn_wo_b)
    x = x + _L1_ffn_ref(_layernorm(x, axis=-1), L1_ffn_Wg, L1_ffn_W1, L1_ffn_W2, L1_ffn_W3)
    x = x + _L2_xattn_ref(_layernorm(x, axis=-1), ctx_1024, ctx_1024, L2_xattn_Wq, L2_xattn_bq, L2_xattn_Wk, L2_xattn_bk, L2_xattn_Wv, L2_xattn_bv, L2_xattn_Wu, L2_xattn_bu)
    x = x + _L2_ffn_ref(_layernorm(x, axis=-1), L2_ffn_router_w, L2_ffn_router_b, L2_ffn_w1, L2_ffn_b1, L2_ffn_w2, L2_ffn_b2)
    x = x + _L3_xattn_ref(_layernorm(x, axis=-1), ctx_1024, ctx_1024, fside_BxSxS2_0, L3_xattn_Wq, L3_xattn_Wk, L3_xattn_Wv, L3_xattn_Wp, L3_xattn_bp)
    x = x + _L3_ffn_ref(_layernorm(x, axis=-1), L3_ffn_w_gate, L3_ffn_c_fc, L3_ffn_c_proj)
    return x

_drawn_inputs = setup_inputs


def setup_inputs(seed=0):
    import zlib

    import numpy as np

    out = dict(_drawn_inputs(seed))
    spreads = {'L0_xattn_bq': (0.0, 0.382),
     'L0_xattn_bk': (0.0, 2.0),
     'L0_xattn_bv': (0.0, 0.1),
     'L0_xattn_bo': (0.0, 0.1),
     'L1_xattn_wq_b': (0.0, 0.366),
     'L1_xattn_wk_b': (0.0, 2.0),
     'L1_xattn_wv_b': (0.0, 0.1),
     'L1_xattn_wo_b': (0.0, 0.1),
     'L2_ffn_router_b': (0.0, 0.594),
     'L2_ffn_b1': (0.0, 2.0),
     'L2_ffn_b2': (0.0, 0.751)}
    factors = {'L0_ffn_W_A': 8.0,
     'L0_ffn_W_B': 8.0,
     'L0_ffn_W_up': 8.0,
     'L0_ffn_W_down': 8.0,
     'L1_ffn_Wg': 8.0,
     'L1_ffn_W1': 8.0,
     'L1_ffn_W2': 8.0,
     'L1_ffn_W3': 8.0,
     'L2_xattn_bq': 18.014,
     'L2_xattn_bk': 64.0,
     'L3_xattn_bp': 45.828,
     'L3_ffn_w_gate': 8.0,
     'L3_ffn_c_fc': 8.0,
     'L3_ffn_c_proj': 8.0,
     'L2_xattn_bv': 4.178,
     'L2_xattn_bu': 5.729,
     'L2_ffn_router_w': 2.863,
     'L2_ffn_w1': 6.039,
     'L2_ffn_w2': 2.969}
    for name, (base, spread) in spreads.items():
        noise = np.random.default_rng([zlib.crc32(name.encode()), seed]).standard_normal(out[name].shape)
        drawn = base * np.exp(spread * noise) if base else spread * noise
        out[name] = jnp.asarray(drawn.astype(out[name].dtype))
    for name, factor in factors.items():
        out[name] = (out[name] * factor).astype(out[name].dtype)
    return out
```

```python
from contextlib import ExitStack

import numpy as np
import concourse.bass as bass
from concourse import mybir

F32 = mybir.dt.float32
BF16 = mybir.dt.bfloat16
U8 = mybir.dt.uint8
ALU = mybir.AluOpType
ACT = mybir.ActivationFunctionType
AX = mybir.AxisListType

P = 128
D = 128
B, S = 16, 64
T = B * S // P
N = B * S
HALF = 512
E = 8
CAPACITY = 512
EPS = 1e-5
MASKED = 2.0 ** 100

LAYERS = 4
HEADS = [16, 16, 16, 8]
DK = [8, 8, 64, 16]
EXP_SCALE = [8 ** -0.5, 8 ** -0.5, 64 ** -0.5, 1.0]
Q_SCALE3 = 16 ** -0.5
HIDDEN = [256, 352, 512, 192]


def row_tiles(h):
    return [min(P, h - r) for r in range(0, h, P)]


CHUNKS = [2 * len(row_tiles(h)) for h in HIDDEN]
CHUNK_BASE = [E * sum(CHUNKS[:l]) for l in range(LAYERS)]
BUFS = [2, 2, 4, 2]
PACK = [HIDDEN[0] * 3, HIDDEN[1] * 2 + 3 * P, HIDDEN[2] + 4 * P + 4, HIDDEN[3] * 2 + 2 * P]
PACK_MAX = max(PACK)

CONSTS, PARAMS = {}, {}


def columns(table, items):
    at = 0
    for name, n in items:
        table[name] = (at, at + n)
        at += n
    return at


N_CONST = columns(CONSTS, [("ident", P), ("hmask8", 16), ("hmask16", 8), ("vmask8", P), ("vmask16", P),
                           ("tri", 64), ("before", P), ("sel", E * P), ("bsel", P), ("half", 2)])
N_PARAM = columns(PARAMS, [("w0", 4 * P), ("w1", 4 * P), ("w3", 4 * P), ("wa", 4 * P),
                           ("bq0", 1), ("bk0", 1), ("bv0", 1), ("bq1", 1), ("bk1", 1), ("bv1", 1),
                           ("bq2", 8), ("bk2", 8), ("bv2", 8), ("bo", 4 * P),
                           ("wg1", E), ("wg2", E), ("wg3", E), ("rb2", E), ("b2", P)])
N_WIDE = 4 * 1024


def n_small(l):
    return T * (l if l < 3 else 2)


def build(nc, x, ctxT, gate, mask0, mask1, consts, params, wide, packs, out, stages=8):
    with ExitStack() as ctx:
        def sb(name, shape, dt=F32):
            return ctx.enter_context(nc.sbuf_tensor(name, shape, dt))

        def sem(name):
            return ctx.enter_context(nc.semaphore(name))

        X = sb("X", [P, T, D])
        XC = sb("XC", [P, T, D])
        SQ = sb("SQ", [P, T * D])
        stat = sb("stat", [P, 4, T])
        xnT = sb("xnT", [P, N])
        con = sb("con", [P, N_CONST])
        par = sb("par", [P, N_PARAM])
        wid = sb("wid", [P, N_WIDE])
        identb = sb("identb", [P, P], BF16)
        beforeb = sb("beforeb", [P, P], BF16)
        onesb = sb("onesb", [P, P], BF16)
        selb = sb("selb", [3 * E, E * P], BF16)
        bselb = sb("bselb", [2, P], BF16)
        mrow = sb("mrow", [2, 2, T * S], U8)
        mbias = sb("mbias", [2, 2, T, S], BF16)
        gat = sb("gat", [P, T, S])
        ctk = sb("ctk", [P, 2, 2 * S])
        ctv = sb("ctv", [P, 2, 2 * S])
        kt = sb("kt", [P, P])
        qt = sb("qt", [P, P])
        km = sb("km", [P, 2, 1024])
        v2 = sb("v2", [P, T, 2, P])
        diff = sb("diff", [P, 1024])
        gated = sb("gated", [P, 512])
        prob = sb("prob", [P, 1024])
        pnorm = sb("pnorm", [P, 1024])
        mx = sb("mx", [P, 16])
        sm = sb("sm", [P, 2, 16])
        probT = sb("probT", [P, 8, P])
        on = sb("on", [P, P])
        oT = sb("oT", [P, 8, P])
        kt2 = sb("kt2", [P, 8, P])
        qt2 = sb("qt2", [P, 8, P])
        va2 = sb("va2", [P, 2, 8, 64])
        R = [sb(f"r{i}", [P, T, E]) for i in range(6)]
        cmp1 = sb("cmp1", [P, T, E, E])
        cmp2 = sb("cmp2", [P, T, E, E])
        rs = sb("rs", [P, 2, T])
        wts = sb("wts", [P, T, E])
        wres = sb("wres", [P, 2, T, E])
        w3 = sb("w3", [P, T, 3, E], BF16)
        keepb = sb("keepb", [P, T, E], BF16)
        cumb = sb("cumb", [P, T, E], BF16)
        wT3 = sb("wT3", [3 * E, N], BF16)
        wT = sb("wT", [E, N])
        ghT = sb("ghT", [P, 4, N])
        pack = [sb(f"pack{u}", [P, PACK_MAX]) for u in range(2)]
        xe = [sb(f"xe{u}", [P, N]) for u in range(2)]
        act_s = [sb(f"act_s{i}", [P, HALF]) for i in range(4)]
        hid = [sb(f"hid{i}", [P, HALF]) for i in range(4)]
        yT = sb("yT", [P, N])

        PS = ctx.enter_context(nc.psum_tensor("PS", [P, 8, 512], F32))
        psS = PS[:, 0:2, :]
        psT2 = PS[:, 2:4, :]
        psA = PS[:, 4, :]
        psV = PS[:, 5, :]
        psO = PS[:, 6, :]
        psM = PS[:, 7, :]
        psKV = PS[:, 4:6, :]
        psO2 = PS[:, 6:8, :]
        psH = PS[:, 0:4, :]
        psY = PS[:, 4:6, :]
        psW = PS[:, 6:8, :]

        names = """load_x load_con load_par load_wide load_gate load_mask ctk_loaded ctv_loaded
            pack0_loaded pack1_loaded consts_ready mbias_ready dve_step
            centred squared var_ready std_ready xn_ready xnT_done xnT_ready bo_added
            qkv_done kq_ready v2_ready km_ready s_done sub_done exp_done pt_done pt_ready pv_done
            on_ready ot_done ot_ready out_done resid_done pn_ready nz_ready ot2_ready
            k2_done k2_ready q2_done q2_ready va_done va_ready
            gh_done gh_ready root_ready route_done ex_in ex_done wsplit wT_done wT_ready cum_in cum_done
            y_started wb_done xe_ready gu_done act_done h_done down_done y_done yT_ready xt_done x_ready
            stored""".split()
        s = {n: sem(n) for n in names}

        def c(name, rows=P):
            a, b = CONSTS[name]
            return con[0:rows, a:b]

        def p(name, rows=P):
            a, b = PARAMS[name]
            return par[0:rows, a:b]

        def attn_w(l, i):
            a = PARAMS[f"w{l}"][0] + i * P
            return par[:, a:a + P]

        def tile(ap, t):
            return ap[:, bass.ds(t * P, P)]

        n_attn = (stages + 1) // 2
        n_ffn = stages // 2

        def steps(eng, body):
            body(0, None, 0, 1)
            body(1, 0, 1, 2)
            with eng.Fori(2, T - 1) as i:
                body(i, i - 1, i, i + 1)
            body(T - 1, T - 2, T - 1, None)
            body(T, T - 1, None, None)

        block = ctx.enter_context(nc.Block())

        @block.sync
        def _(sp):
            sp.dma_start(X[:, :, :], x.rearrange("(t p) d -> p t d", p=P)).then_inc(s["load_x"], 16)
            sp.dma_start(con[:, :], consts).then_inc(s["load_con"], 16)
            sp.dma_start(par[:, :], params).then_inc(s["load_par"], 16)
            sp.dma_start(mrow[:, 0, :], mask0).then_inc(s["load_mask"], 16)
            sp.dma_start(mrow[:, 1, :], mask1).then_inc(s["load_mask"], 16)
            sp.dma_start(wid[:, :], wide).then_inc(s["load_wide"], 16)
            sp.dma_start(gat[:, :, :], gate.rearrange("(t p) k -> p t k", p=P)).then_inc(s["load_gate"], 16)
            for l in range(LAYERS):
                if l < n_attn:
                    n0 = l * T

                    def load_ctk(t, first=False):
                        if not first:
                            if l == 2:
                                sp.wait_ge(s["k2_done"], t)
                            else:
                                sp.wait_ge(s["qkv_done"], n_small(l) + t)
                        sp.dma_start(ctk[:, :, :].rearrange("p b k -> p (b k)"), ctxT[bass.ds(t, 1), :, :].rearrange("a p k -> (a p) k")).then_inc(s["ctk_loaded"], 16)

                    def load_ctv(t, first=False):
                        if not first:
                            sp.wait_ge(s["va_done"], t)
                        sp.dma_start(ctv[:, :, :].rearrange("p b k -> p (b k)"), ctxT[bass.ds(t, 1), :, :].rearrange("a p k -> (a p) k")).then_inc(s["ctv_loaded"], 16)
                    if l > 0:
                        if l == 3:
                            sp.wait_ge(s["k2_done"], T)
                        else:
                            sp.wait_ge(s["qkv_done"], n_small(l))
                    load_ctk(0, True)
                    if l == 2:
                        load_ctk(1)
                        load_ctv(0, True)
                        with sp.Fori(2, T) as i:
                            load_ctk(i)
                            load_ctv(i - 1)
                        load_ctv(T - 1)
                    else:
                        with sp.Fori(1, T) as i:
                            load_ctk(i)
                if l < n_ffn:
                    q0 = CHUNK_BASE[l]

                    def load_pack(e, u):
                        sp.dma_start(pack[u][:, 0:PACK[l]], packs[l][e, :, :]).then_inc(s[f"pack{u}_loaded"], 16)
                    for u in range(2):
                        if l > 0:
                            sp.wait_ge(s["down_done"], q0)
                        load_pack(u, u)
                    with sp.Fori(1, E // 2) as i:
                        for u in range(2):
                            sp.wait_ge(s["down_done"], q0 + (i * 2 + (u - 1)) * CHUNKS[l])
                            load_pack(i * 2 + u, u)
            if stages % 2:
                sp.wait_ge(s["resid_done"], n_attn * T)
            else:
                sp.wait_ge(s["x_ready"], n_ffn)
            sp.dma_start(out.rearrange("(t p) d -> p t d", p=P), X[:, :, :]).then_inc(s["stored"], 16)
            sp.wait_ge(s["stored"], 16)

        @block.gpsimd
        def _(pool):
            pool.wait_ge(s["load_con"], 16)
            pool.tensor_copy(identb[:, :], c("ident"))
            pool.tensor_copy(beforeb[:, :], c("before"))
            pool.tensor_copy(selb[:, :], c("sel", 3 * E))
            pool.tensor_copy(bselb[:, :], c("bsel", 2))
            pool.memset(onesb[:, :], 1.0).then_inc(s["consts_ready"], 1)
            pool.wait_ge(s["load_par"], 16)
            for l in range(n_attn):
                pool.wait_ge(s["centred"], 2 * l + 1)
                a = PARAMS["bo"][0] + l * P
                pool.tensor_tensor(X[:, :, :], X[:, :, :],
                                   par[:, a:a + P].unsqueeze(1).to_broadcast([P, T, P]),
                                   ALU.add).then_inc(s["bo_added"], 1)
                if l == 2:
                    continue
                H = HEADS[l]
                n0 = n_small(l)
                hm = c(f"hmask{DK[l]}")

                def mask_keys(t):
                    n = n0 + t
                    pool.wait_ge(s["kq_ready"], 2 * n + 1)
                    if l or not isinstance(t, int) or t > 0:
                        pool.wait_ge(s["s_done"], l * T + t)
                    for b in range(2):
                        pool.tensor_tensor(
                            km[:, b, 0:H * S].rearrange("p (h k) -> p h k", h=H),
                            kt[:, b * S:(b + 1) * S].unsqueeze(1).to_broadcast([P, H, S]),
                            hm.unsqueeze(2).to_broadcast([P, H, S]), ALU.mult).then_inc(s["km_ready"], 1)

                mask_keys(0)
                with pool.Fori(1, T) as i:
                    mask_keys(i)

        @block.tensor
        def _(pe):
            pe.wait_ge(s["load_con"], 16)
            pe.wait_ge(s["load_par"], 16)
            pe.wait_ge(s["consts_ready"], 1)

            def norm_transpose(k):
                pe.wait_ge(s["xn_ready"], k + 1)
                for t in range(T):
                    mm = pe.transpose(psT2[:, t // 4, (t % 4) * P:(t % 4 + 1) * P], XC[:, t, :], c("ident"))
                mm.then_inc(s["xnT_done"], 1)

            def small_attention(l):
                H, dk = HEADS[l], DK[l]
                G = H * S // 512
                n0, a0 = n_small(l), l * T

                def project(t):
                    n = n0 + t
                    pe.wait_ge(s["ctk_loaded"], (a0 + t + 1) * 16)
                    if l == 0 and isinstance(t, int) and t == 0:
                        pass
                    else:
                        pe.wait_ge(s["kq_ready"], 2 * n)
                        pe.wait_ge(s["v2_ready"], n)
                    pe.matmul(psA[:, 0:P].rearrange("p (b k) -> p b k", b=2), attn_w(l, 1), ctk[:, :, 0:S], start=True, stop=True)
                    pe.matmul(psA[:, P:2 * P], attn_w(l, 0), tile(xnT, t), start=True, stop=True)
                    for b in range(2):
                        mm = pe.matmul(psV[:, b * P:(b + 1) * P],
                                       ctk[:, b, :],
                                       attn_w(l, 2), start=True, stop=True)
                    mm.then_inc(s["qkv_done"], 1)

                def scores(t):
                    n = n0 + t
                    pe.wait_ge(s["km_ready"], 2 * n + 2)
                    pe.wait_ge(s["kq_ready"], 2 * n + 2)
                    if l or not isinstance(t, int) or t > 0:
                        pe.wait_ge(s["sub_done"], a0 + t)
                    for g in range(G):
                        for b in range(2):
                            mm = pe.matmul(psS[b * S:(b + 1) * S, g, :], qt[:, b * S:(b + 1) * S],
                                           km[:, b, g * 512:(g + 1) * 512], start=True, stop=(l == 3),
                                           skip_group_check=True)
                        if l < 3:
                            mm = pe.matmul(psS[:, g, :].rearrange("p (h k) -> p h k", h=8), bselb[:, :],
                                           mbias[:, l, bass.ds(t, 1), :].to_broadcast([2, 8, S]),
                                           start=False, stop=True, skip_group_check=True)
                    mm.then_inc(s["s_done"], 1)

                def transpose_probs(t):
                    a = a0 + t
                    pe.wait_ge(s["exp_done"], a + 1)
                    if l == 3:
                        pe.wait_ge(s["nz_ready"], t + 1)
                    if l or not isinstance(t, int) or t > 0:
                        pe.wait_ge(s["pt_ready"], 2 * a)
                    src = pnorm if l == 3 else prob
                    for g in range(G):
                        for j in range(4):
                            k = (4 * g + j) * P
                            mm = pe.transpose(psT2[:, g, j * P:(j + 1) * P], src[:, k:k + P], c("ident"))
                        mm.then_inc(s["pt_done"], 2 // G)

                def weigh_values(t):
                    n, a = n0 + t, a0 + t
                    pe.wait_ge(s["pt_ready"], 2 * a + 2)
                    pe.wait_ge(s["v2_ready"], n + 1)
                    if n0 or not isinstance(t, int) or t > 0:
                        pe.wait_ge(s["on_ready"], n)
                    for j in range(H // 2):
                        mm = pe.matmul(psO[:, 4 * dk * j:4 * dk * (j + 1)].rearrange("p (b c) -> p b c", b=2),
                                       probT[:, j, :],
                                       v2[:, bass.ds(t, 1), :, 2 * dk * j:2 * dk * (j + 1)].rearrange("p a b c -> p (a b) c"),
                                       start=True, stop=True, skip_group_check=True)
                    mm.then_inc(s["pv_done"], 1)

                def output(t):
                    n, a = n0 + t, a0 + t
                    pe.wait_ge(s["on_ready"], n + 1)
                    if l or not isinstance(t, int) or t > 0:
                        pe.wait_ge(s["resid_done"], a)
                    pe.transpose(psM[:, 0:P], on[:, :], c("ident")).then_inc(s["ot_done"], 1)
                    pe.wait_ge(s["ot_ready"], n + 1)
                    pe.matmul(psM[:, P:2 * P], oT[:, 0, :], attn_w(l, 3), start=True,
                              stop=True).then_inc(s["out_done"], 1)

                def body(_, fin, sc, pre):
                    if sc is not None:
                        scores(sc)
                    if fin is not None:
                        transpose_probs(fin)
                        weigh_values(fin)
                    if pre is not None:
                        project(pre)
                    if fin is not None:
                        output(fin)

                pe.wait_ge(s["xnT_ready"], 2 * l + 1)
                if l == 0:
                    pe.wait_ge(s["mbias_ready"], 1)
                project(0)
                steps(pe, body)

            def wide_attention():
                l, a0 = 2, 2 * T

                def keys(t):
                    pe.wait_ge(s["ctk_loaded"], (a0 + t + 1) * 16)
                    if isinstance(t, int) and t == 0:
                        pe.wait_ge(s["v2_ready"], 2 * T)
                    else:
                        pe.wait_ge(s["q2_ready"], t)
                    for j in range(8):
                        mm = pe.matmul(psKV[:, j // 4, (j % 4) * P:(j % 4 + 1) * P].rearrange("p (b k) -> p b k", b=2),
                                       wid[:, 1024 + j * P:1024 + (j + 1) * P], ctk[:, :, 0:S],
                                       start=True, stop=True)
                    mm.then_inc(s["k2_done"], 1)

                def queries(t, v_before):
                    pe.wait_ge(s["k2_ready"], t + 1)
                    if v_before is not None:
                        pe.wait_ge(s["va_ready"], v_before + 1)
                    for j in range(8):
                        mm = pe.matmul(psKV[:, j // 4, (j % 4) * P:(j % 4 + 1) * P],
                                       wid[:, j * P:(j + 1) * P], tile(xnT, t), start=True, stop=True)
                    mm.then_inc(s["q2_done"], 1)

                def values(t, k_before):
                    pe.wait_ge(s["ctv_loaded"], (t + 1) * 16)
                    if k_before is not None:
                        pe.wait_ge(s["k2_ready"], k_before + 1)
                    for b in range(2):
                        for par_ in range(2):
                            mm = pe.matmul(psKV[par_ * S:(par_ + 1) * S, b, :], ctv[:, b, 0:S],
                                           wid[:, 2048 + par_ * 512:2048 + (par_ + 1) * 512],
                                           start=True, stop=True, skip_group_check=True)
                    mm.then_inc(s["va_done"], 1)

                def scores(t):
                    pe.wait_ge(s["q2_ready"], t + 1)
                    pe.wait_ge(s["k2_ready"], t + 1)
                    pe.wait_ge(s["sub_done"], a0 + t)
                    for j in range(8):
                        for b in range(2):
                            for h in range(2):
                                rows = slice(h * S, (h + 1) * S)
                                m = 2 if j == b == h == 0 else 1
                                mm = pe.matmul(psS[b * S:(b + m) * S, h, j * S:(j + 1) * S],
                                               qt2[rows, j, b * S:(b + m) * S],
                                               kt2[rows, j, b * S:(b + 1) * S],
                                               start=True, stop=True, skip_group_check=True)
                    mm.then_inc(s["s_done"], 1)

                def transpose_probs(t):
                    pe.wait_ge(s["pn_ready"], t + 1)
                    pe.wait_ge(s["pt_ready"], 2 * (a0 + t))
                    for g in range(2):
                        for j in range(4):
                            k = (4 * g + j) * P
                            mm = pe.transpose(psT2[:, g, j * P:(j + 1) * P], pnorm[:, k:k + P], c("ident"))
                        mm.then_inc(s["pt_done"], 1)

                def weigh_values(t):
                    pe.wait_ge(s["pt_ready"], 2 * (a0 + t) + 2)
                    pe.wait_ge(s["va_ready"], t + 1)
                    if not isinstance(t, int) or t > 0:
                        pe.wait_ge(s["resid_done"], a0 + t)
                    for j in range(8):
                        for b in range(2):
                            for h in range(2):
                                rows = slice(h * S, (h + 1) * S)
                                m = 2 if j == b == h == 0 else 1
                                mm = pe.matmul(psO2[h * S:(h + m) * S, b, j * S:(j + 1) * S],
                                               va2[rows, b, j:j + m, :].rearrange("p j d -> p (j d)"), probT[rows, j, b * S:(b + 1) * S],
                                               start=True, stop=True, skip_group_check=True)
                    mm.then_inc(s["pv_done"], 1)

                def output(t):
                    pe.wait_ge(s["ot2_ready"], 2 * t + 2)
                    for j in range(8):
                        mm = pe.matmul(psO2[:, 0, 0:P], oT[:, j, :], wid[:, 3072 + j * P:3072 + (j + 1) * P],
                                       start=(j == 0), stop=(j == 7))
                    mm.then_inc(s["out_done"], 1)

                def body(_, fin, sc, pre):
                    if sc is not None:
                        scores(sc)
                    if pre is not None:
                        keys(pre)
                    if fin is not None:
                        transpose_probs(fin)
                        values(fin, pre)
                    if pre is not None:
                        queries(pre, fin)
                    if fin is not None:
                        weigh_values(fin)
                        output(fin)

                pe.wait_ge(s["xnT_ready"], 2 * l + 1)
                pe.wait_ge(s["load_wide"], 16)
                keys(0)
                queries(0, None)
                steps(pe, body)

            def route(l):
                pe.wait_ge(s["xnT_ready"], 2 * l + 2)
                pe.wait_ge(s["resid_done"], (l + 1) * T)
                if l == 0:
                    for k in range(4):
                        if k >= 2:
                            pe.wait_ge(s["gh_ready"], 2 * (k - 1))
                        for h in range(2):
                            a = PARAMS["wa"][0] + k * P
                            mm = pe.matmul(psH[:, (2 * k + h) % 4, :], par[:, a:a + P],
                                           xnT[:, h * HALF:(h + 1) * HALF], start=True, stop=True)
                        mm.then_inc(s["gh_done"], 1)
                    pe.wait_ge(s["gh_ready"], 8)
                    for t in range(T):
                        for k in range(4):
                            mm = pe.matmul(psW[:, 0, t * E + 2 * k:t * E + 2 * k + 2],
                                           ghsq(k)[:, t * P:(t + 1) * P], c("half"), start=True, stop=True)
                    mm.then_inc(s["route_done"], 1)
                else:
                    for t in range(T):
                        mm = pe.matmul(psW[:, 0, t * E:(t + 1) * E], xnT[:, t * P:(t + 1) * P], p(f"wg{l}"),
                                       start=True, stop=True)
                    mm.then_inc(s["route_done"], 1)
                for t in range(T):
                    mm = pe.matmul(psY[:, t // 4, (t % 4) * P:(t % 4 + 1) * P], X[:, t, :], c("ident"),
                                   start=(t % 4 == 0), stop=False, skip_group_check=True)
                mm.then_inc(s["y_started"], 1)
                if l == 3:
                    pe.wait_ge(s["cum_in"], 1)
                    pe.matmul(psW[:, 1, 0:T * E], beforeb[:, :], keepb[:, :, :].rearrange("p t e -> p (t e)"),
                              start=True, stop=False)
                    pe.matmul(psW[:, 1, 0:T * E], onesb[:, :], cumb[:, :, :].rearrange("p t e -> p (t e)"),
                              start=False, stop=True).then_inc(s["cum_done"], 1)
                pe.wait_ge(s["wsplit"], l + 1)
                psWb = psH[:, 0, :].bitcast(BF16)
                for t in range(T):
                    mm = pe.transpose(psWb[0:3 * E, t * P:(t + 1) * P],
                                      w3[:, t, :, :].rearrange("p a e -> p (a e)"), identb[:, :])
                if l == 2:
                    for t in range(T):
                        mm = pe.transpose(psH[0:E, 1 + t // 4, (t % 4) * P:(t % 4 + 1) * P], wts[:, t, :], c("ident"))
                mm.then_inc(s["wT_done"], 1)

            def ghsq(k):
                return [xe[0], xe[1], yT, SQ][k][:, :]

            def experts(l):
                tiles = row_tiles(HIDDEN[l])
                C, bufs, q0 = CHUNKS[l], BUFS[l], CHUNK_BASE[l]
                hidn = HIDDEN[l]
                if l == 0:
                    off = (0, hidn, 2 * hidn)
                elif l == 2:
                    off = (0, None, hidn)
                else:
                    off = (0, hidn, 2 * hidn)

                def spread(e):
                    if not (l == 0 and isinstance(e, int) and e == 0):
                        pe.wait_ge(s["xe_ready"], l * E + e)
                    for h in range(2):
                        mm = pe.matmul(psW[:, h, :], selb[:, bass.ds(e * P, P)], wT3[:, h * HALF:(h + 1) * HALF],
                                       start=True, stop=True)
                    mm.then_inc(s["wb_done"], 1)

                def up(e, u, ch, first):
                    i, h = ch // 2, ch % 2
                    m = tiles[i]
                    q = e * C + (q0 + ch)
                    bank = ch % bufs
                    if ch == 0:
                        done = sum(16 * (E // 2) for _ in range(l))
                        pe.wait_ge(s[f"pack{u}_loaded"], (e - u) * 8 + (done + 16))
                        pe.wait_ge(s["xe_ready"], l * E + e + 1)
                    if not (first and ch < bufs):
                        pe.wait_ge(s["h_done"], q - bufs + 1)
                    if l == 0:
                        mm = pe.matmul(psH[0:m, bank, :], pack[u][:, off[0] + i * P:off[0] + i * P + m],
                                       ghT[:, bass.ds((e - u) // 2 if isinstance(e, int) else pair(e, u), 1),
                                           h * HALF:(h + 1) * HALF],
                                       start=True, stop=True)
                    else:
                        mm = pe.matmul(psH[0:m, bank, :], pack[u][:, off[0] + i * P:off[0] + i * P + m],
                                       xnT[:, h * HALF:(h + 1) * HALF], start=True, stop=True)
                    if l != 2:
                        mm = pe.matmul(psH[0:m, 2 + bank, :], pack[u][:, off[1] + i * P:off[1] + i * P + m],
                                       xe[u][:, h * HALF:(h + 1) * HALF], start=True, stop=True)
                    mm.then_inc(s["gu_done"], 1)

                pairs = {}

                def pair(e, u):
                    return pairs["now"]

                def down(e, u, ch):
                    i, h = ch // 2, ch % 2
                    q = e * C + (q0 + ch)
                    pe.wait_ge(s["h_done"], q + 1)
                    pe.matmul(psY[:, h, :], pack[u][0:tiles[i], off[2] + i * P:off[2] + (i + 1) * P],
                              hid[ch % bufs][0:tiles[i], :], start=False, stop=False,
                              skip_group_check=True).then_inc(s["down_done"], 1)

                lag = bufs - 1

                def expert_pair(i, first=False):
                    pairs["now"] = i
                    for u in range(2):
                        e = i * 2 + u
                        for ch in range(C + lag):
                            if ch < C:
                                up(e, u, ch, first and u == 0)
                            if ch == 1 and not (u == 1 and isinstance(i, int) and i == E // 2 - 1):
                                spread(e + 1)
                            if ch >= lag:
                                down(e, u, ch - lag)

                pe.wait_ge(s["wT_ready"], l + 1)
                spread(0)
                expert_pair(0, True)
                with pe.Fori(1, E // 2 - 1) as i:
                    expert_pair(i)
                expert_pair(E // 2 - 1)
                if l == 2:
                    for h in range(2):
                        mm = pe.matmul(psY[:, h, :], p("b2", E), wT[:, h * HALF:(h + 1) * HALF],
                                       start=False, stop=False, skip_group_check=True)
                    mm.then_inc(s["y_done"], 1)
                pe.wait_ge(s["yT_ready"], l + 1)
                for t in range(T):
                    mm = pe.transpose(psH[:, t // 4, (t % 4) * P:(t % 4 + 1) * P], yT[:, t * P:(t + 1) * P], c("ident"))
                mm.then_inc(s["xt_done"], 1)

            for l in range(LAYERS):
                if l < n_attn:
                    norm_transpose(2 * l)
                    if l == 2:
                        wide_attention()
                    else:
                        small_attention(l)
                if l < n_ffn:
                    norm_transpose(2 * l + 1)
                    route(l)
                    experts(l)

        @block.scalar
        def _(act):
            act.wait_ge(s["load_par"], 16)

            def norm(k):
                act.wait_ge(s["centred"], k + 1)
                act.activation(SQ[:, :], XC[:, :, :].rearrange("p t d -> p (t d)"),
                               ACT.Square).then_inc(s["squared"], 1)
                act.wait_ge(s["var_ready"], k + 1)
                act.activation(stat[:, 3, :], stat[:, 2, :], ACT.Sqrt).then_inc(s["std_ready"], 1)
                act.wait_ge(s["xnT_done"], k + 1)
                for h in range(2):
                    a = act.activation(xnT[:, h * HALF:(h + 1) * HALF], psT2[:, h, :], ACT.Copy)
                a.then_inc(s["xnT_ready"], 1)

            def probs_out(l, t, G):
                a = l * T + t
                for g in range(G):
                    act.wait_ge(s["pt_done"], 2 * a + (g + 1) * (2 // G))
                    if g == 0 and (l or not isinstance(t, int) or t > 0):
                        act.wait_ge(s["pv_done"], a)
                    act.activation(probT[:, 4 * g:4 * g + 4, :].rearrange("p j q -> p (j q)"), psT2[:, g, :],
                                   ACT.Copy).then_inc(s["pt_ready"], 2 // G)

            def small_attention(l):
                H = HEADS[l]
                G = H * S // 512
                n0, a0 = n_small(l), l * T

                def keys_queries(t):
                    n = n0 + t
                    act.wait_ge(s["qkv_done"], n + 1)
                    if not (l == 0 and isinstance(t, int) and t == 0):
                        act.wait_ge(s["km_ready"], 2 * n)
                        act.wait_ge(s["s_done"], a0 + t)
                    if l < 3:
                        act.activation(kt[:, :], psA[:, 0:P], ACT.Identity, bias=p(f"bk{l}")).then_inc(s["kq_ready"], 1)
                        act.activation(qt[:, :], psA[:, P:2 * P], ACT.Identity, bias=p(f"bq{l}")).then_inc(s["kq_ready"], 1)
                    else:
                        act.activation(kt[:, :], psA[:, 0:P], ACT.Copy).then_inc(s["kq_ready"], 1)
                        act.activation(qt[:, :], psA[:, P:2 * P], ACT.Copy, scale=Q_SCALE3).then_inc(s["kq_ready"], 1)

                def exps(t):
                    a = a0 + t
                    act.wait_ge(s["sub_done"], a + 1)
                    if l or not isinstance(t, int) or t > 0:
                        act.wait_ge(s["pt_done"], 2 * a)
                    act.activation(prob[:, 0:H * S], diff[:, 0:H * S], ACT.Exp,
                                   scale=EXP_SCALE[l]).then_inc(s["exp_done"], 1)

                def out_values(t):
                    n = n0 + t
                    act.wait_ge(s["ot_done"], n + 1)
                    if not (l == 0 and isinstance(t, int) and t == 0):
                        act.wait_ge(s["out_done"], a0 + t)
                    if l < 3:
                        act.activation(oT[:, 0, :], psM[:, 0:P], ACT.Identity, bias=p(f"bv{l}")).then_inc(s["ot_ready"], 1)
                    else:
                        act.activation(oT[:, 0, :], psM[:, 0:P], ACT.Copy).then_inc(s["ot_ready"], 1)

                def body(_, fin, sc, pre):
                    if fin is not None:
                        probs_out(l, fin, G)
                    if sc is not None:
                        exps(sc)
                    if pre is not None:
                        keys_queries(pre)
                    if fin is not None:
                        out_values(fin)

                keys_queries(0)
                steps(act, body)

            def wide_attention():
                a0 = 2 * T

                def exps(t):
                    act.wait_ge(s["sub_done"], a0 + t + 1)
                    act.wait_ge(s["pn_ready"], t)
                    act.activation(prob[:, :].rearrange("p (j h k) -> p h j k", j=8, h=2),
                                   diff[:, :].rearrange("p (h j k) -> p h j k", j=8, h=2), ACT.Exp,
                                   scale=EXP_SCALE[2]).then_inc(s["exp_done"], 1)

                def values_out(t):
                    act.wait_ge(s["va_done"], t + 1)
                    act.wait_ge(s["pv_done"], a0 + t)
                    for b in range(2):
                        a = act.activation(va2[:, b, :, :].rearrange("p j d -> p (j d)"), psKV[:, b, :], ACT.Copy)
                    a.then_inc(s["va_ready"], 1)

                def out_values(t):
                    act.wait_ge(s["pv_done"], a0 + t + 1)
                    act.wait_ge(s["out_done"], a0 + t)
                    src = psO2[:, :, :].rearrange("p b (j q) -> p j b q", j=8)
                    for g in range(2):
                        for j in range(4 * g, 4 * g + 4):
                            bv = PARAMS["bv2"][0] + j
                            a = act.activation(oT[:, j, :].rearrange("p (b q) -> p b q", b=2), src[:, j, :, :],
                                               ACT.Identity, bias=par[:, bv:bv + 1])
                        a.then_inc(s["ot2_ready"], 1)

                def body(_, fin, sc, pre):
                    if fin is not None:
                        probs_out(2, fin, 2)
                    if sc is not None:
                        exps(sc)
                    if fin is not None:
                        values_out(fin)
                        out_values(fin)

                steps(act, body)

            def route(l):
                if l == 0:
                    for k in range(4):
                        act.wait_ge(s["gh_done"], k + 1)
                        for h in range(2):
                            src = psH[:, (2 * k + h) % 4, :]
                            cols = slice(h * HALF, (h + 1) * HALF)
                            act.activation(ghT[:, k, cols], src, ACT.Copy)
                            act.activation([xe[0], xe[1], yT, SQ][k][:, cols], src,
                                           ACT.Square).then_inc(s["gh_ready"], 1)
                    act.wait_ge(s["route_done"], 1)
                    act.activation(R[2][:, :, :].rearrange("p t e -> p (t e)"), psW[:, 0, 0:T * E],
                                   ACT.Sqrt).then_inc(s["root_ready"], 1)
                act.wait_ge(s["ex_in"], l + 1)
                act.activation(R[1][:, :, :].rearrange("p t e -> p (t e)"), R[0][:, :, :].rearrange("p t e -> p (t e)"),
                               ACT.Exp).then_inc(s["ex_done"], 1)
                act.wait_ge(s["wT_done"], l + 1)
                a = act.activation(wT3[:, :], psH[0:3 * E, 0, :].bitcast(BF16), ACT.Copy)
                if l == 2:
                    for h in range(2):
                        a = act.activation(wT[:, h * HALF:(h + 1) * HALF], psH[0:E, 1 + h, :], ACT.Copy)
                a.then_inc(s["wT_ready"], 1)

            def experts(l):
                tiles = row_tiles(HIDDEN[l])
                C, bufs, q0 = CHUNKS[l], BUFS[l], CHUNK_BASE[l]

                def expert_pair(i, first=False):
                    for u in range(2):
                        e = i * 2 + u
                        for ch in range(C):
                            m = tiles[ch // 2]
                            q = e * C + (q0 + ch)
                            act.wait_ge(s["gu_done"], q + 1)
                            if not (first and u == 0 and ch < bufs):
                                act.wait_ge(s["h_done"], q - bufs + 1)
                            dst = act_s[ch % bufs][0:m, :]
                            src = psH[0:m, ch % bufs, :]
                            if l == 2:
                                b1 = HIDDEN[2] + 4 * P + ch // 2
                                a = act.activation(dst, src, ACT.Relu, bias=pack[u][:, b1:b1 + 1])
                            else:
                                a = act.activation(dst, src, ACT.Silu)
                            a.then_inc(s["act_done"], 1)

                expert_pair(0, True)
                with act.Fori(1, E // 2 - 1) as i:
                    expert_pair(i)
                expert_pair(E // 2 - 1)
                act.wait_ge(s["down_done"], q0 + E * C)
                if l == 2:
                    act.wait_ge(s["y_done"], 1)
                for h in range(2):
                    a = act.activation(yT[:, h * HALF:(h + 1) * HALF], psY[:, h, :], ACT.Copy)
                a.then_inc(s["yT_ready"], 1)

            for l in range(LAYERS):
                if l < n_attn:
                    norm(2 * l)
                    if l == 2:
                        wide_attention()
                    else:
                        small_attention(l)
                if l < n_ffn:
                    norm(2 * l + 1)
                    route(l)
                    experts(l)

        @block.vector
        def _(dve):
            step = {"n": 0}

            def link(ins):
                step["n"] = step["n"] + 1
                ins.then_inc(s["dve_step"], 1)
                dve.wait_ge(s["dve_step"], step["n"])

            def add_mask_bias():
                dve.wait_ge(s["load_mask"], 32)
                dve.tensor_scalar(mbias[:, :, :, :].rearrange("b l t k -> b (l t k)"),
                                  mrow[:, :, :].rearrange("b l n -> b (l n)"), MASKED, -MASKED,
                                  ALU.mult, ALU.add).then_inc(s["mbias_ready"], 1)

            def norm(k):
                link(dve.tensor_reduce(stat[:, 0, :], X[:, :, :], AX.X, ALU.add))
                link(dve.tensor_scalar(stat[:, 1, :], stat[:, 0, :], 1.0 / D, None, ALU.mult))
                if k:
                    dve.wait_ge(s["xnT_done"], k)
                dve.tensor_tensor(XC[:, :, :], X[:, :, :], stat[:, 1, :].unsqueeze(2).to_broadcast([P, T, D]),
                                  ALU.subtract).then_inc(s["centred"], 1)
                dve.wait_ge(s["squared"], k + 1)
                link(dve.tensor_reduce(stat[:, 2, :], SQ[:, :].rearrange("p (t d) -> p t d", t=T), AX.X, ALU.add))
                dve.tensor_scalar(stat[:, 2, :], stat[:, 2, :], 1.0 / D, EPS, ALU.mult, ALU.add).then_inc(s["var_ready"], 1)
                dve.wait_ge(s["std_ready"], k + 1)
                link(dve.reciprocal(stat[:, 3, :], stat[:, 3, :]))
                dve.tensor_tensor(XC[:, :, :], XC[:, :, :], stat[:, 3, :].unsqueeze(2).to_broadcast([P, T, D]),
                                  ALU.mult).then_inc(s["xn_ready"], 1)

            def loop_steps(body, links):
                body(0, None, 0, 1)
                body(1, 0, 1, 2)
                base = step["n"]
                with dve.Fori(2, T - 1) as i:
                    step["n"] = (i - 2) * links + base
                    body(i, i - 1, i, i + 1)
                step["n"] = base + (T - 3) * links
                body(T - 1, T - 2, T - 1, None)
                body(T, T - 1, None, None)

            def heads(ap, H):
                return ap.rearrange("p (h k) -> p h k", h=H)

            def small_attention(l):
                H, dk = HEADS[l], DK[l]
                G = H * S // 512
                n0, a0 = n_small(l), l * T
                W = H * S
                raw = psS[:, 0:G, :].rearrange("p g n -> p (g n)")

                def values(t):
                    n = n0 + t
                    dve.wait_ge(s["qkv_done"], n + 1)
                    dve.tensor_tensor(v2[:, bass.ds(t, 1), :, :].rearrange("p a b c -> p (a b) c"),
                                      psV[:, 0:2 * P].rearrange("p (b c) -> p b c", b=2),
                                      c(f"vmask{dk}").unsqueeze(1).to_broadcast([P, 2, P]),
                                      ALU.mult).then_inc(s["v2_ready"], 1)

                def softmax_in(t):
                    a = a0 + t
                    dve.wait_ge(s["s_done"], a + 1)
                    src = raw
                    if l == 3:
                        if not isinstance(t, int) or t > 0:
                            dve.wait_ge(s["nz_ready"], t)
                        link(dve.tensor_tensor(heads(gated[:, :], H), heads(raw, H),
                                               gat[:, bass.ds(t, 1), :].to_broadcast([P, H, S]), ALU.mult))
                        src = gated[:, :]
                    link(dve.tensor_reduce(mx[:, 0:H], heads(src, H), AX.X, ALU.max))
                    if l or not isinstance(t, int) or t > 0:
                        dve.wait_ge(s["exp_done"], a)
                    dve.tensor_tensor(heads(diff[:, 0:W], H), heads(src, H),
                                      mx[:, 0:H].unsqueeze(2).to_broadcast([P, H, S]),
                                      ALU.subtract).then_inc(s["sub_done"], 1)

                def normalise_out(t):
                    n = n0 + t
                    dve.wait_ge(s["pv_done"], a0 + t + 1)
                    if not (l == 0 and isinstance(t, int) and t == 0):
                        dve.wait_ge(s["ot_done"], n)
                    for b in range(2):
                        q = slice(b * S, (b + 1) * S)
                        ins = dve.tensor_tensor(
                            on[q, :].rearrange("p (j h d) -> p j h d", h=2, d=dk),
                            psO[q, 0:2 * P].rearrange("p (j b h d) -> p j b h d", b=2, h=2, d=dk)[:, :, b, :, :],
                            sm[q, 1, 0:H].rearrange("p (j h) -> p j h", h=2).unsqueeze(3)
                              .to_broadcast([S, H // 2, 2, dk]), ALU.mult)
                    ins.then_inc(s["on_ready"], 1)

                def sums(t):
                    a = a0 + t
                    dve.wait_ge(s["exp_done"], a + 1)
                    link(dve.tensor_reduce(sm[:, 0, 0:H], heads(prob[:, 0:W], H), AX.X, ALU.add))
                    link(dve.reciprocal(sm[:, 1, 0:H], sm[:, 0, 0:H]))
                    if l == 3:
                        dve.wait_ge(s["pt_done"], 2 * a)
                        dve.scalar_tensor_tensor(pnorm[:, 0:W], gated[:, :], 0.0, prob[:, 0:W],
                                                 ALU.not_equal, ALU.mult).then_inc(s["nz_ready"], 1)

                def residual(t):
                    a = a0 + t
                    dve.wait_ge(s["out_done"], a + 1)
                    dve.tensor_tensor(X[:, bass.ds(t, 1), :].rearrange("p a d -> p (a d)"),
                                      X[:, bass.ds(t, 1), :].rearrange("p a d -> p (a d)"),
                                      psM[:, P:2 * P], ALU.add).then_inc(s["resid_done"], 1)

                def body(_, fin, sc, pre):
                    if sc is not None:
                        softmax_in(sc)
                    if fin is not None:
                        normalise_out(fin)
                    if pre is not None:
                        values(pre)
                    if sc is not None:
                        sums(sc)
                    if fin is not None:
                        residual(fin)

                values(0)
                loop_steps(body, 4 if l == 3 else 3)

            def wide_attention():
                a0 = 2 * T

                def with_bias(dst, bias):
                    a = PARAMS[bias][0]
                    return dve.tensor_tensor(dst[:, :, :], psKV[:, :, :].rearrange("p g (j q) -> p (g j) q", j=4),
                                             par[:, a:a + 8].unsqueeze(2).to_broadcast([P, 8, P]), ALU.add)

                def keys(t):
                    dve.wait_ge(s["k2_done"], t + 1)
                    dve.wait_ge(s["s_done"], a0 + t)
                    with_bias(kt2, "bk2").then_inc(s["k2_ready"], 1)

                def queries(t):
                    dve.wait_ge(s["q2_done"], t + 1)
                    with_bias(qt2, "bq2").then_inc(s["q2_ready"], 1)

                def softmax_in(t):
                    a = a0 + t
                    dve.wait_ge(s["s_done"], a + 1)
                    src = psS[:, :, :].rearrange("p h (j k) -> p (h j) k", j=8)
                    link(dve.tensor_reduce(mx[:, :], src, AX.X, ALU.max))
                    dve.wait_ge(s["exp_done"], a)
                    dve.tensor_tensor(heads(diff[:, :], 16), src, mx[:, :].unsqueeze(2).to_broadcast([P, 16, S]),
                                      ALU.subtract).then_inc(s["sub_done"], 1)

                def normalise(t):
                    a = a0 + t
                    dve.wait_ge(s["exp_done"], a + 1)
                    link(dve.tensor_reduce(sm[:, 0, :], heads(prob[:, :], 16), AX.X, ALU.add))
                    link(dve.reciprocal(sm[:, 1, :], sm[:, 0, :]))
                    dve.wait_ge(s["pt_done"], 2 * a)
                    dve.tensor_tensor(heads(pnorm[:, :], 16), heads(prob[:, :], 16),
                                      sm[:, 1, :].unsqueeze(2).to_broadcast([P, 16, S]),
                                      ALU.mult).then_inc(s["pn_ready"], 1)

                def residual(t):
                    dve.wait_ge(s["out_done"], a0 + t + 1)
                    dve.tensor_tensor(X[:, bass.ds(t, 1), :].rearrange("p a d -> p (a d)"),
                                      X[:, bass.ds(t, 1), :].rearrange("p a d -> p (a d)"),
                                      psO2[:, 0, 0:P], ALU.add).then_inc(s["resid_done"], 1)

                def body(_, fin, sc, pre):
                    if sc is not None:
                        softmax_in(sc)
                    if pre is not None:
                        keys(pre)
                        queries(pre)
                    if sc is not None:
                        normalise(sc)
                    if fin is not None:
                        residual(fin)

                keys(0)
                queries(0)
                loop_steps(body, 3)

            def flat(ap):
                return ap[:, :, :].rearrange("p t e -> p (t e)")

            def over_experts(ap):
                return ap.unsqueeze(2).to_broadcast([P, T, E])

            def route(l):
                score, top, keep = R[2], rs[:, 0, :], R[3]
                dve.wait_ge(s["route_done"], l + 1)
                src = psW[:, 0, 0:T * E]
                if l == 0:
                    dve.wait_ge(s["root_ready"], 1)
                elif l == 2:
                    link(dve.tensor_tensor(score[:, :, :], src.rearrange("p (t e) -> p t e", t=T),
                                           p("rb2").unsqueeze(1).to_broadcast([P, T, E]), ALU.add))
                else:
                    link(dve.tensor_copy(flat(score), src))
                link(dve.tensor_reduce(top, score[:, :, :], AX.X, ALU.max))
                dve.tensor_tensor(R[0][:, :, :], score[:, :, :], over_experts(top),
                                  ALU.subtract).then_inc(s["ex_in"], 1)
                dve.wait_ge(s["ex_done"], l + 1)
                ex = R[1]
                if l in (1, 3):
                    link(dve.tensor_reduce(rs[:, 1, :], ex[:, :, :], AX.X, ALU.add))
                    link(dve.reciprocal(rs[:, 1, :], rs[:, 1, :]))
                    link(dve.tensor_tensor(ex[:, :, :], ex[:, :, :], over_experts(rs[:, 1, :]), ALU.mult))
                    score = ex
                other = score[:, :, :].unsqueeze(2).to_broadcast([P, T, E, E])
                own = score[:, :, :].unsqueeze(3).to_broadcast([P, T, E, E])
                dve.tensor_tensor(cmp1[:, :, :, :], other, own, ALU.is_gt)
                link(dve.tensor_tensor(cmp2[:, :, :, :], other, own, ALU.is_equal))
                link(dve.tensor_tensor(cmp2[:, :, :, :].rearrange("p t a b -> p t (a b)"),
                                       cmp2[:, :, :, :].rearrange("p t a b -> p t (a b)"),
                                       c("tri").unsqueeze(1).to_broadcast([P, T, E * E]), ALU.mult))
                link(dve.tensor_tensor(cmp1[:, :, :, :].rearrange("p t a b -> p (t a b)"),
                                       cmp1[:, :, :, :].rearrange("p t a b -> p (t a b)"),
                                       cmp2[:, :, :, :].rearrange("p t a b -> p (t a b)"), ALU.add))
                link(dve.tensor_reduce(flat(R[4]), cmp1[:, :, :, :].rearrange("p t a b -> p (t a) b"), AX.X, ALU.add))
                link(dve.tensor_scalar(flat(keep), flat(R[4]), 1.5, None, ALU.is_lt))
                if l == 3:
                    dve.tensor_copy(keepb[:, :, :], keep[:, :, :])
                    link(dve.memset(cumb[:, 0, :], 0.0))
                    for t in range(1, T):
                        ins = dve.tensor_tensor(cumb[:, t, :], cumb[:, t - 1, :], keep[:, t - 1, :], ALU.add)
                        if t < T - 1:
                            link(ins)
                    ins.then_inc(s["cum_in"], 1)
                if l == 3:
                    link(dve.tensor_tensor(wts[:, :, :], ex[:, :, :], keep[:, :, :], ALU.mult))
                    dve.wait_ge(s["cum_done"], 1)
                    link(dve.scalar_tensor_tensor(flat(wts), psW[:, 1, 0:T * E], CAPACITY - 0.5, flat(wts),
                                                  ALU.is_lt, ALU.mult))
                else:
                    link(dve.tensor_tensor(ex[:, :, :], ex[:, :, :], keep[:, :, :], ALU.mult))
                    link(dve.tensor_reduce(rs[:, 0, :], ex[:, :, :], AX.X, ALU.add))
                    if l == 1:
                        link(dve.tensor_scalar(rs[:, 0, :], rs[:, 0, :], 1e-20, None, ALU.add))
                    link(dve.reciprocal(rs[:, 1, :], rs[:, 0, :]))
                    link(dve.tensor_tensor(wts[:, :, :], ex[:, :, :], over_experts(rs[:, 1, :]), ALU.mult))
                link(dve.tensor_copy(w3[:, :, 0, :], wts[:, :, :]))
                link(dve.tensor_tensor(wres[:, 0, :, :], wts[:, :, :], w3[:, :, 0, :], ALU.subtract))
                link(dve.tensor_copy(w3[:, :, 1, :], wres[:, 0, :, :]))
                link(dve.tensor_tensor(wres[:, 1, :, :], wres[:, 0, :, :], w3[:, :, 1, :], ALU.subtract))
                dve.tensor_copy(w3[:, :, 2, :], wres[:, 1, :, :]).then_inc(s["wsplit"], 1)

            def experts(l):
                tiles = row_tiles(HIDDEN[l])
                C, bufs, q0 = CHUNKS[l], BUFS[l], CHUNK_BASE[l]

                def weighted_input(e, u, first=False):
                    dve.wait_ge(s["wb_done"], l * E + e + 1)
                    if not first:
                        dve.wait_ge(s["down_done"], q0 + (e - 1) * C)
                    w = psW[:, :, :].rearrange("p g n -> p (g n)")
                    if l == 2:
                        link_free = dve.tensor_copy(xe[u][:, :], w)
                    else:
                        link_free = dve.tensor_tensor(xe[u][:, :], xnT[:, :], w, ALU.mult)
                    link_free.then_inc(s["xe_ready"], 1)

                def expert_pair(i, first=False):
                    for u in range(2):
                        e = i * 2 + u
                        for ch in range(C):
                            m = tiles[ch // 2]
                            q = e * C + (q0 + ch)
                            dve.wait_ge(s["act_done"], q + 1)
                            if not (first and u == 0 and ch < bufs):
                                dve.wait_ge(s["down_done"], q - bufs + 1)
                            if l == 2:
                                other = xe[u][0:m, (ch % 2) * HALF:(ch % 2 + 1) * HALF]
                                if ch == 0:
                                    dve.wait_ge(s["xe_ready"], l * E + e + 1)
                            else:
                                other = psH[0:m, 2 + ch % bufs, :]
                            dve.tensor_tensor(hid[ch % bufs][0:m, :], act_s[ch % bufs][0:m, :], other,
                                              ALU.mult).then_inc(s["h_done"], 1)
                            if ch == 1 and not (u == 1 and isinstance(i, int) and i == E // 2 - 1):
                                weighted_input(e + 1, 1 - u, first and u == 0)

                weighted_input(0, 0, True)
                expert_pair(0, True)
                with dve.Fori(1, E // 2 - 1) as i:
                    expert_pair(i)
                expert_pair(E // 2 - 1)
                dve.wait_ge(s["xt_done"], l + 1)
                for h in range(2):
                    ins = dve.tensor_copy(X[:, 4 * h:4 * h + 4, :].rearrange("p t d -> p (t d)"), psH[:, h, :])
                ins.then_inc(s["x_ready"], 1)

            add_mask_bias()
            dve.wait_ge(s["load_x"], 16)
            dve.wait_ge(s["load_con"], 16)
            dve.wait_ge(s["load_par"], 16)
            dve.wait_ge(s["load_gate"], 16)
            for l in range(LAYERS):
                if l < n_attn:
                    if l:
                        dve.wait_ge(s["x_ready"], l)
                    norm(2 * l)
                    dve.wait_ge(s["bo_added"], l + 1)
                    if l == 2:
                        wide_attention()
                    else:
                        small_attention(l)
                if l < n_ffn:
                    dve.wait_ge(s["resid_done"], (l + 1) * T)
                    norm(2 * l + 1)
                    route(l)
                    experts(l)


def constants():
    con = np.zeros((P, N_CONST), np.float32)
    r = np.arange(P)

    def put(name, value):
        a, b = CONSTS[name]
        con[:value.shape[0], a:b] = value

    put("ident", np.eye(P))
    put("hmask8", (r[:, None] // 8 == np.arange(16)[None]))
    put("hmask16", (r[:, None] // 16 == np.arange(8)[None]))
    put("vmask8", (r[:, None] // S == (r[None] // 8) % 2))
    put("vmask16", (r[:, None] // S == (r[None] // 16) % 2))
    e = np.arange(E)
    put("tri", np.broadcast_to((e[None, :] < e[:, None]).reshape(1, E * E), (P, E * E)))
    put("before", (r[:, None] < r[None, :]))
    sel = (np.arange(3 * E)[:, None, None] % E == e[None, :, None]) * np.ones((1, 1, P))
    put("sel", sel.reshape(3 * E, E * P))
    put("bsel", (np.arange(2)[:, None] == r[None] // S))
    put("half", (r[:, None] // 64 == np.arange(2)[None]))
    return con


def kernel(**inputs):
    import concourse.bacc as _bacc
    from concourse.bass_utils import run_bass_kernel_spmd as _run
    i = {k: np.asarray(v) for k, v in inputs.items()}
    stages = STAGES

    par = np.zeros((P, N_PARAM), np.float32)

    def put(name, value):
        a, b = PARAMS[name]
        par[:value.shape[0], a:b] = value

    put("w0", np.concatenate([i["L0_xattn_Wq"], i["L0_xattn_Wk"], i["L0_xattn_Wv"], i["L0_xattn_Wo"]], 1))
    put("w1", np.concatenate([i["L1_xattn_wq_w"].T, i["L1_xattn_wk_w"].T, i["L1_xattn_wv_w"].T,
                              i["L1_xattn_wo_w"].T], 1))
    put("w3", np.concatenate([i["L3_xattn_Wq"].T, i["L3_xattn_Wk"].T, i["L3_xattn_Wv"].T, i["L3_xattn_Wp"].T], 1))
    put("wa", i["L0_ffn_W_A"].reshape(512, P).T)
    for n in "qkv":
        put(f"b{n}0", i[f"L0_xattn_b{n}"].reshape(P, 1))
        put(f"b{n}1", i[f"L1_xattn_w{n}_b"].reshape(P, 1))
        put(f"b{n}2", i[f"L2_xattn_b{n}"].reshape(8, P).T)
    bo = np.stack([i["L0_xattn_bo"], i["L1_xattn_wo_b"], i["L2_xattn_bu"], i["L3_xattn_bp"]]).reshape(1, 4 * P)
    put("bo", np.broadcast_to(bo, (P, 4 * P)))
    put("wg1", i["L1_ffn_Wg"].T)
    put("wg2", i["L2_ffn_router_w"])
    put("wg3", i["L3_ffn_w_gate"])
    put("rb2", np.broadcast_to(i["L2_ffn_router_b"].reshape(1, E), (P, E)))
    put("b2", i["L2_ffn_b2"])

    wide = np.zeros((P, N_WIDE), np.float32)
    wide[:, 0:1024] = i["L2_xattn_Wq"]
    wide[:, 1024:2048] = i["L2_xattn_Wk"]
    wide[:, 2048:3072] = i["L2_xattn_Wv"].reshape(P, 8, 2, 64).transpose(0, 2, 1, 3).reshape(P, 1024)
    wide[:, 3072:4096] = i["L2_xattn_Wu"].reshape(8, P, P).transpose(1, 0, 2).reshape(P, 1024)

    def down_tiles(w):
        e, h, d = w.shape
        t = -(-h // P)
        padded = np.zeros((e, t * P, d), np.float32)
        padded[:, :h] = w
        return padded.reshape(e, t, P, d).transpose(0, 2, 1, 3).reshape(e, P, t * d)

    wb = np.zeros((E, P, HIDDEN[0]), np.float32)
    for e in range(E):
        wb[e, 64 * (e % 2):64 * (e % 2) + 64] = i["L0_ffn_W_B"][e].T
    packs = [
        np.concatenate([wb, i["L0_ffn_W_up"].transpose(0, 2, 1), down_tiles(i["L0_ffn_W_down"].transpose(0, 2, 1))], 2),
        np.concatenate([i["L1_ffn_W1"].transpose(0, 2, 1), i["L1_ffn_W3"].transpose(0, 2, 1),
                        down_tiles(i["L1_ffn_W2"].transpose(0, 2, 1))], 2),
        np.concatenate([i["L2_ffn_w1"], down_tiles(i["L2_ffn_w2"]),
                        i["L2_ffn_b1"].reshape(E, 4, P).transpose(0, 2, 1)], 2),
        np.concatenate([i["L3_ffn_c_fc"], down_tiles(i["L3_ffn_c_proj"])], 2),
    ]
    arrays = {
        "x": i["x"].reshape(N, D),
        "ctxT": np.broadcast_to(i["ctx_1024"].reshape(T, 2, 1, S, D), (T, 2, 2, S, D)).reshape(T, 4 * S, D)
                  .transpose(0, 2, 1),
        "gate": i["fside_BxSxS2_0"].reshape(N, S),
        "mask0": i["mask_Bx1xS2_bf1"].reshape(T, 2, S).transpose(1, 0, 2).reshape(2, T * S).view(np.uint8),
        "mask1": i["mask_BxS2_bf1"].reshape(T, 2, S).transpose(1, 0, 2).reshape(2, T * S).view(np.uint8),
        "consts": constants(),
        "params": par,
        "wide": wide,
    }
    for l in range(LAYERS):
        arrays[f"pack{l}"] = packs[l]
    nc = _bacc.Bacc("TRN2", target_bir_lowering=False, num_devices=1)
    feed, aps = {}, {}
    for name, a in arrays.items():
        a = np.ascontiguousarray(a)
        feed[f"in_{name}"] = a
        aps[name] = nc.dram_tensor(f"in_{name}", a.shape, mybir.dt.from_np(a.dtype), kind="ExternalInput").ap()
    out = nc.dram_tensor("out", (N, D), F32, kind="ExternalOutput").ap()
    build(nc, aps["x"], aps["ctxT"], aps["gate"], aps["mask0"], aps["mask1"], aps["consts"], aps["params"],
          aps["wide"], [aps[f"pack{l}"] for l in range(LAYERS)], out, stages)
    r = _run(nc, [feed], core_ids=[0])
    return r.results[0]["out"].reshape(B, S, D)


STAGES = 8
```

```python
from contextlib import ExitStack

import numpy as np
import concourse.bass as bass
from concourse import mybir

F32 = mybir.dt.float32
BF16 = mybir.dt.bfloat16
I32 = mybir.dt.int32
U8 = mybir.dt.uint8
ALU = mybir.AluOpType
ACT = mybir.ActivationFunctionType
AX = mybir.AxisListType

P = 128
D = 128
B, S = 16, 64
T = B * S // P
N = B * S
HALF = 512
E = 8
CAPACITY = 512
EPS = 1e-5
MAGIC = 0x5F3759DF
MASKED = 2.0 ** 100

LAYERS = 4
HEADS = [16, 16, 16, 8]
DK = [8, 8, 64, 16]
EXP_SCALE = [8 ** -0.5, 8 ** -0.5, 64 ** -0.5, 1.0]
Q_SCALE3 = 16 ** -0.5
HIDDEN = [256, 352, 512, 192]


def row_tiles(h):
    return [min(P, h - r) for r in range(0, h, P)]


CHUNKS = [2 * len(row_tiles(h)) for h in HIDDEN]
CHUNK_BASE = [E * sum(CHUNKS[:l]) for l in range(LAYERS)]
BUFS = [2, 2, 4, 2]
PACK = [HIDDEN[0] * 3, HIDDEN[1] * 2 + 3 * P, HIDDEN[2] + 4 * P + 4, HIDDEN[3] * 2 + 2 * P]
PACK_MAX = max(PACK)

CONSTS, PARAMS = {}, {}


def columns(table, items):
    at = 0
    for name, n in items:
        table[name] = (at, at + n)
        at += n
    return at


N_CONST = columns(CONSTS, [("ident", P), ("hmask8", 16), ("hmask16", 8),
                           ("tri", 64), ("before", P), ("bsel", P), ("half", 2)])
N_PARAM = columns(PARAMS, [("w0", 4 * P), ("bq0", 1), ("bk0", 1), ("bv0", 1),
                           ("w1", 4 * P), ("w3", 4 * P), ("wa", 4 * P), ("bq1", 1), ("bk1", 1), ("bv1", 1),
                           ("bq2", 8), ("bk2", 8), ("bv2", 8), ("bo", 4 * P),
                           ("wg1", E), ("wg2", E), ("wg3", E), ("rb2", E), ("b2", P)])
PARAMS["first"] = (0, PARAMS["w1"][0])
PARAMS["rest"] = (PARAMS["w1"][0], N_PARAM)
N_WIDE = 4 * 1024


def n_small(l):
    return T * (l if l < 3 else 2)


def build(nc, x, ctxT, gate, mask0, mask1, consts, selc, params, wide, packs, out, stages=8):
    with ExitStack() as ctx:
        def sb(name, shape, dt=F32):
            return ctx.enter_context(nc.sbuf_tensor(name, shape, dt))

        def sem(name):
            return ctx.enter_context(nc.semaphore(name))

        X = sb("X", [P, T, D])
        XC = sb("XC", [P, T, D])
        SQ = sb("SQ", [P, T * D])
        bn = sb("bn", [P, 6])
        bns = sb("bns", [P, T, 6])
        xsum = sb("xsum", [P, P])
        stat = sb("stat", [P, T, 2])
        root = sb("root", [P, 4, T])
        xnT = sb("xnT", [P, N])
        con = sb("con", [P, N_CONST])
        sel = sb("sel", [3 * E, E * P])
        par = sb("par", [P, N_PARAM])
        wid = sb("wid", [P, N_WIDE])
        identb = sb("identb", [P, P], BF16)
        beforeb = sb("beforeb", [P, P], BF16)
        onesb = sb("onesb", [P, P], BF16)
        selb = sb("selb", [3 * E, E * P], BF16)
        bselb = sb("bselb", [2, P], BF16)
        mrow = sb("mrow", [2, 2, T * S], U8)
        mbias = sb("mbias", [2, 2, T, S], BF16)
        gat = sb("gat", [P, T, S])
        cx = sb("cx", [P, T, 2, 2 * S])
        ctv = sb("ctv", [P, P])
        kt = sb("kt", [P, N])
        qt = sb("qt", [P, P])
        km = sb("km", [P, 2, 1024])
        v2 = {dk: sb(f"v2_{dk}", [P, T, 2, P]) for dk in (8, 16)}
        diff = sb("diff", [P, 1024])
        gated = sb("gated", [P, 512])
        prob = sb("prob", [P, 1024])
        pnorm = sb("pnorm", [P, 1024])
        mx = sb("mx", [P, 16])
        sm = sb("sm", [P, 2, 16])
        probT = sb("probT", [P, 8, P])
        on = sb("on", [P, P])
        oT = sb("oT", [P, 8, P])
        kt2 = sb("kt2", [P, 8, P])
        qt2 = sb("qt2", [P, 8, P])
        va2 = sb("va2", [P, 2, 8, 64])
        R = [sb(f"r{i}", [P, T, E]) for i in range(6)]
        cmp1 = sb("cmp1", [P, T, E, E])
        cmp2 = sb("cmp2", [P, T, E, E])
        rs = sb("rs", [P, 2, T])
        wts = sb("wts", [P, T, E])
        wres = sb("wres", [P, 2, T, E])
        w3 = sb("w3", [P, T, 3, E], BF16)
        keepb = sb("keepb", [P, T, E], BF16)
        cumb = sb("cumb", [P, T, E], BF16)
        wT3 = sb("wT3", [3 * E, N], BF16)
        wT = sb("wT", [E, N])
        ghT = sb("ghT", [P, 4, N])
        pack = [sb(f"pack{u}", [P, PACK_MAX]) for u in range(2)]
        xe = [sb(f"xe{u}", [P, N]) for u in range(2)]
        act_s = [sb(f"act_s{i}", [P, HALF]) for i in range(4)]
        hid = [sb(f"hid{i}", [P, HALF]) for i in range(4)]
        yT = sb("yT", [P, N])

        PS = ctx.enter_context(nc.psum_tensor("PS", [P, 8, 512], F32))
        psS = PS[:, 0:2, :]
        psT2 = PS[:, 2:4, :]
        psA = PS[:, 4, :]
        psO = PS[:, 6, :]
        psM = PS[:, 7, :]
        psKV = PS[:, 4:6, :]
        psO2 = PS[:, 6:8, :]
        psH = PS[:, 0:4, :]
        psY = PS[:, 4:6, :]
        psW = PS[:, 6:8, :]

        names = """load_x load_cx load_con load_sel load_w0 load_par load_wide load_gate load_mask
            pack0_loaded pack1_loaded consts_ready zeros_ready mbias_ready dve_step
            xn_ready xnT_done xnT_ready bo_added
            k_done v_done kv_ready q_done q_ready km_ready s0_done s_done sub_done exp_done
            pt_done pt_ready pv_done on_ready ot_done ot_ready out_done resid_done
            pn_ready nz_ready ot2_ready ctv_ready k2_done k2_ready q2_done q2_ready va0_done va_done va_ready
            gh_done gh_ready root_ready route_done ex_in ex_done wsplit wT_done wT_ready cum_in cum_done
            y_started wb_done xe_ready gu_done act_done h_done down_done y_done yT_ready xt_done x_ready
            stored""".split()
        s = {n: sem(n) for n in names}

        def c(name, rows=P):
            a, b = CONSTS[name]
            return con[0:rows, a:b]

        def p(name, rows=P):
            a, b = PARAMS[name]
            return par[0:rows, a:b]

        def attn_w(l, i):
            a = PARAMS[f"w{l}"][0] + i * P
            return par[:, a:a + P]

        def tile(ap, t):
            return ap[:, bass.ds(t * P, P)]

        n_attn = (stages + 1) // 2
        n_ffn = stages // 2

        def steps(eng, body):
            body(None, None, 0, 1)
            body(None, 0, 1, 2)
            body(0, 1, 2, 3)
            with eng.Fori(3, T - 1) as i:
                body(i - 2, i - 1, i, i + 1)
            body(T - 3, T - 2, T - 1, None)
            body(T - 2, T - 1, None, None)
            body(T - 1, None, None, None)

        def later(l, t):
            return bool(l) or not isinstance(t, int) or t > 0

        block = ctx.enter_context(nc.Block())

        @block.sync
        def _(sp):
            sp.dma_start(X[:, :, :], x.rearrange("(t p) d -> p t d", p=P)).then_inc(s["load_x"], 16)
            a, b = PARAMS["first"]
            sp.dma_start(par[:, a:b], params[:, a:b]).then_inc(s["load_w0"], 16)
            sp.dma_start(con[:, :], consts).then_inc(s["load_con"], 16)
            sp.dma_start(mrow[:, 0, :], mask0).then_inc(s["load_mask"], 16)
            sp.dma_start(mrow[:, 1, :], mask1).then_inc(s["load_mask"], 16)
            sp.dma_start(sel[:, :], selc).then_inc(s["load_sel"], 16)
            a, b = PARAMS["rest"]
            sp.dma_start(par[:, a:b], params[:, a:b]).then_inc(s["load_par"], 16)
            sp.dma_start(gat[:, :, :], gate.rearrange("(t p) k -> p t k", p=P)).then_inc(s["load_gate"], 16)
            for l in range(LAYERS):
                if l == 1:
                    sp.dma_start(wid[:, :], wide).then_inc(s["load_wide"], 16)
                if l < n_ffn:
                    q0 = CHUNK_BASE[l]

                    def load_pack(e, u):
                        sp.dma_start(pack[u][:, 0:PACK[l]], packs[l][e, :, :]).then_inc(s[f"pack{u}_loaded"], 16)
                    for u in range(2):
                        if l > 0:
                            sp.wait_ge(s["down_done"], q0)
                        load_pack(u, u)
                    with sp.Fori(1, E // 2) as i:
                        for u in range(2):
                            sp.wait_ge(s["down_done"], q0 + (i * 2 + (u - 1)) * CHUNKS[l])
                            load_pack(i * 2 + u, u)
            if stages % 2:
                sp.wait_ge(s["resid_done"], n_attn * T)
            else:
                sp.wait_ge(s["x_ready"], n_ffn * T)
            sp.dma_start(out.rearrange("(t p) d -> p t d", p=P), X[:, :, :]).then_inc(s["stored"], 16)
            sp.wait_ge(s["stored"], 16)

        @block.gpsimd
        def _(pool):
            for dk in (8, 16):
                ins = pool.memset(v2[dk][:, :, :, :].rearrange("p t b c -> p (t b c)"), 0.0)
            ins.then_inc(s["zeros_ready"], 1)
            pool.wait_ge(s["load_con"], 16)
            pool.tensor_copy(identb[:, :], c("ident"))
            pool.tensor_copy(beforeb[:, :], c("before"))
            pool.tensor_copy(bselb[:, :], c("bsel", 2))
            pool.memset(onesb[:, :], 1.0)
            pool.wait_ge(s["load_sel"], 16)
            pool.tensor_copy(selb[:, :], sel[:, :]).then_inc(s["consts_ready"], 1)
            pool.wait_ge(s["load_par"], 16)
            for l in range(n_attn):
                H = HEADS[l]
                n0 = n_small(l)

                def mask_keys(t):
                    hm = c(f"hmask{DK[l]}")
                    for b in range(2):
                        if later(l, t):
                            pool.wait_ge(s["s_done" if b else "s0_done"], (l * T if b else n0) + t)
                        pool.tensor_tensor(
                            km[:, b, 0:H * S].rearrange("p (h k) -> p h k", h=H),
                            kt[:, bass.ds(t * P + b * S, S)].unsqueeze(1).to_broadcast([P, H, S]),
                            hm.unsqueeze(2).to_broadcast([P, H, S]), ALU.mult).then_inc(s["km_ready"], 1)

                def context(t):
                    if later(0, t):
                        pool.wait_ge(s["va_done"], t)
                    pool.tensor_copy(ctv[:, :].rearrange("p (b k) -> p b k", b=2),
                                     cx[:, bass.ds(t, 1), :, 0:S].rearrange("p a b k -> p (a b) k")
                                     ).then_inc(s["ctv_ready"], 1)

                if l != 2:
                    pool.wait_ge(s["kv_ready"], l + 1 if l < 2 else 3)
                    mask_keys(0)
                else:
                    context(0)
                pool.wait_ge(s["xn_ready"], T * (2 * l + 1))
                a = PARAMS["bo"][0] + l * P
                pool.tensor_tensor(X[:, :, :], X[:, :, :],
                                   par[:, a:a + P].unsqueeze(1).to_broadcast([P, T, P]),
                                   ALU.add).then_inc(s["bo_added"], 1)
                with pool.Fori(1, T) as i:
                    if l == 2:
                        context(i)
                    else:
                        mask_keys(i)

        @block.tensor
        def _(pe):
            pe.wait_ge(s["load_con"], 16)
            pe.wait_ge(s["load_w0"], 16)
            pe.wait_ge(s["load_cx"], 16)

            def norm_transpose(k):
                for t in range(T):
                    pe.wait_ge(s["xn_ready"], T * k + t + 1)
                    mm = pe.transpose(psT2[:, t // 4, (t % 4) * P:(t % 4 + 1) * P], XC[:, t, :], c("ident"))
                    if t % 4 == 3:
                        mm.then_inc(s["xnT_done"], 1)

            def keys_values(l):
                for h in range(2):
                    mm = pe.matmul(psW[:, h, :].rearrange("p (t k) -> p t k", k=S), attn_w(l, 1),
                                   cx[:, 4 * h:4 * h + 4, :, 0:S].rearrange("p t b k -> p (t b) k"),
                                   start=True, stop=True)
                mm.then_inc(s["k_done"], 1)
                for t in range(T):
                    for b in range(2):
                        mm = pe.matmul(psH[:, t // 2, (2 * (t % 2) + b) * P:(2 * (t % 2) + b + 1) * P],
                                       cx[:, t, b, :], attn_w(l, 2), start=True, stop=True)
                    if t % 2:
                        mm.then_inc(s["v_done"], 1)

            def small_attention(l):
                H, dk = HEADS[l], DK[l]
                G = H * S // 512
                n0, a0 = n_small(l), l * T

                def queries(t):
                    if later(l, t):
                        pe.wait_ge(s["q_ready"], n0 + t)
                    pe.matmul(psA[:, 0:P], attn_w(l, 0), tile(xnT, t), start=True,
                              stop=True).then_inc(s["q_done"], 1)

                def scores(t, b):
                    n = n0 + t
                    pe.wait_ge(s["km_ready"], 2 * n + 1 + b)
                    if b == 0:
                        pe.wait_ge(s["q_ready"], n + 1)
                        if later(l, t):
                            pe.wait_ge(s["sub_done"], a0 + t)
                    for g in range(G):
                        mm = pe.matmul(psS[b * S:(b + 1) * S, g, :], qt[:, b * S:(b + 1) * S],
                                       km[:, b, g * 512:(g + 1) * 512], start=True, stop=(l == 3),
                                       skip_group_check=True)
                    if b == 0:
                        mm.then_inc(s["s0_done"], 1)
                    if b and l < 3:
                        for g in range(G):
                            mm = pe.matmul(psS[:, g, :].rearrange("p (h k) -> p h k", h=8), bselb[:, :],
                                           mbias[:, l, bass.ds(t, 1), :].to_broadcast([2, 8, S]),
                                           start=False, stop=True, skip_group_check=True)
                    if b:
                        mm.then_inc(s["s_done"], 1)

                def transpose_probs(t):
                    a = a0 + t
                    pe.wait_ge(s["exp_done"], a + 1)
                    if l == 3:
                        pe.wait_ge(s["nz_ready"], t + 1)
                    if l or not isinstance(t, int) or t > 0:
                        pe.wait_ge(s["pt_ready"], 2 * a)
                    src = pnorm if l == 3 else prob
                    for g in range(G):
                        for j in range(4):
                            k = (4 * g + j) * P
                            mm = pe.transpose(psT2[:, g, j * P:(j + 1) * P], src[:, k:k + P], c("ident"))
                        mm.then_inc(s["pt_done"], 2 // G)

                def weigh_values(t):
                    n, a = n0 + t, a0 + t
                    pe.wait_ge(s["pt_ready"], 2 * a + 2)
                    if n0 or not isinstance(t, int) or t > 0:
                        pe.wait_ge(s["on_ready"], n)
                    for j in range(H // 2):
                        mm = pe.matmul(psO[:, 4 * dk * j:4 * dk * (j + 1)].rearrange("p (b c) -> p b c", b=2),
                                       probT[:, j, :],
                                       v2[dk][:, bass.ds(t, 1), :, 2 * dk * j:2 * dk * (j + 1)].rearrange("p a b c -> p (a b) c"),
                                       start=True, stop=True, skip_group_check=True)
                    mm.then_inc(s["pv_done"], 1)

                def turn_output(t):
                    pe.wait_ge(s["on_ready"], n0 + t + 1)
                    if later(l, t):
                        pe.wait_ge(s["resid_done"], a0 + t)
                    pe.transpose(psM[:, 0:P], on[:, :], c("ident")).then_inc(s["ot_done"], 1)

                def output(t):
                    pe.wait_ge(s["ot_ready"], n0 + t + 1)
                    pe.matmul(psM[:, P:2 * P], oT[:, 0, :], attn_w(l, 3), start=True,
                              stop=True).then_inc(s["out_done"], 1)

                def body(out, fin, sc, pre):
                    if sc is not None:
                        scores(sc, 0)
                    if out is not None:
                        turn_output(out)
                    if sc is not None:
                        scores(sc, 1)
                    if fin is not None:
                        transpose_probs(fin)
                    if out is not None:
                        output(out)
                    if pre is not None:
                        queries(pre)
                    if fin is not None:
                        weigh_values(fin)

                pe.wait_ge(s["xnT_ready"], 4 * l + 2)
                queries(0)
                pe.wait_ge(s["consts_ready"], 1)
                if l == 0:
                    pe.wait_ge(s["mbias_ready"], 1)
                steps(pe, body)

            def wide_attention():
                l, a0 = 2, 2 * T

                def keys(t):
                    for g in range(2):
                        if later(0, t):
                            pe.wait_ge(s["q2_ready"], 2 * t - 1 + g)
                        for j in range(4 * g, 4 * g + 4):
                            mm = pe.matmul(psKV[:, g, (j % 4) * P:(j % 4 + 1) * P].rearrange("p (b k) -> p b k", b=2),
                                           wid[:, 1024 + j * P:1024 + (j + 1) * P],
                                           cx[:, bass.ds(t, 1), :, 0:S].rearrange("p a b k -> p (a b) k"),
                                           start=True, stop=True)
                        mm.then_inc(s["k2_done"], 1)

                def queries(t, v_before):
                    for g in range(2):
                        if v_before is None:
                            pe.wait_ge(s["k2_ready"], 2 * t + 1 + g)
                        else:
                            pe.wait_ge(s["va_ready"], 2 * v_before + 1 + g)
                        for j in range(4 * g, 4 * g + 4):
                            mm = pe.matmul(psKV[:, g, (j % 4) * P:(j % 4 + 1) * P],
                                           wid[:, j * P:(j + 1) * P], tile(xnT, t), start=True, stop=True)
                        mm.then_inc(s["q2_done"], 1)

                def values(t, k_before):
                    pe.wait_ge(s["ctv_ready"], t + 1)
                    for b in range(2):
                        if k_before is not None:
                            pe.wait_ge(s["k2_ready"], 2 * k_before + 1 + b)
                        for par_ in range(2):
                            mm = pe.matmul(psKV[par_ * S:(par_ + 1) * S, b, :], ctv[:, b * S:(b + 1) * S],
                                           wid[:, 2048 + par_ * 512:2048 + (par_ + 1) * 512],
                                           start=True, stop=True, skip_group_check=True)
                        mm.then_inc(s["va_done" if b else "va0_done"], 1)

                def scores(t):
                    pe.wait_ge(s["q2_ready"], 2 * t + 2)
                    pe.wait_ge(s["k2_ready"], 2 * t + 2)
                    pe.wait_ge(s["sub_done"], a0 + t)
                    for j in range(8):
                        for b in range(2):
                            for h in range(2):
                                rows = slice(h * S, (h + 1) * S)
                                m = 2 if j == b == h == 0 else 1
                                mm = pe.matmul(psS[b * S:(b + m) * S, h, j * S:(j + 1) * S],
                                               qt2[rows, j, b * S:(b + m) * S],
                                               kt2[rows, j, b * S:(b + 1) * S],
                                               start=True, stop=True, skip_group_check=True)
                    mm.then_inc(s["s_done"], 1)

                def transpose_probs(t):
                    pe.wait_ge(s["pn_ready"], t + 1)
                    pe.wait_ge(s["pt_ready"], 2 * (a0 + t))
                    for g in range(2):
                        for j in range(4):
                            k = (4 * g + j) * P
                            mm = pe.transpose(psT2[:, g, j * P:(j + 1) * P], pnorm[:, k:k + P], c("ident"))
                        mm.then_inc(s["pt_done"], 1)

                def weigh_values(t):
                    pe.wait_ge(s["pt_ready"], 2 * (a0 + t) + 2)
                    pe.wait_ge(s["va_ready"], 2 * t + 2)
                    if not isinstance(t, int) or t > 0:
                        pe.wait_ge(s["resid_done"], a0 + t)
                    for j in range(8):
                        for b in range(2):
                            for h in range(2):
                                rows = slice(h * S, (h + 1) * S)
                                m = 2 if j == b == h == 0 else 1
                                mm = pe.matmul(psO2[h * S:(h + m) * S, b, j * S:(j + 1) * S],
                                               va2[rows, b, j:j + m, :].rearrange("p j d -> p (j d)"), probT[rows, j, b * S:(b + 1) * S],
                                               start=True, stop=True, skip_group_check=True)
                    mm.then_inc(s["pv_done"], 1)

                def output(t):
                    pe.wait_ge(s["ot2_ready"], 2 * t + 2)
                    for j in range(8):
                        mm = pe.matmul(psO2[:, 0, 0:P], oT[:, j, :], wid[:, 3072 + j * P:3072 + (j + 1) * P],
                                       start=(j == 0), stop=(j == 7))
                    mm.then_inc(s["out_done"], 1)

                def body(out, fin, sc, pre):
                    if sc is not None:
                        scores(sc)
                    if out is not None:
                        output(out)
                    if pre is not None:
                        keys(pre)
                    if fin is not None:
                        transpose_probs(fin)
                        values(fin, pre)
                    if pre is not None:
                        queries(pre, fin)
                    if fin is not None:
                        weigh_values(fin)

                pe.wait_ge(s["load_wide"], 16)
                pe.wait_ge(s["x_ready"], 2 * T)
                keys(0)
                norm_transpose(2 * l)
                pe.wait_ge(s["xnT_ready"], 4 * l + 2)
                queries(0, None)
                steps(pe, body)

            def route(l):
                pe.wait_ge(s["xnT_ready"], 4 * l + 4)
                if l == 0:
                    pe.wait_ge(s["load_par"], 16)
                pe.wait_ge(s["resid_done"], (l + 1) * T)
                if l == 0:
                    for k in range(4):
                        if k >= 2:
                            pe.wait_ge(s["gh_ready"], 2 * (k - 1))
                        for h in range(2):
                            a = PARAMS["wa"][0] + k * P
                            mm = pe.matmul(psH[:, (2 * k + h) % 4, :], par[:, a:a + P],
                                           xnT[:, h * HALF:(h + 1) * HALF], start=True, stop=True)
                        mm.then_inc(s["gh_done"], 1)
                    pe.wait_ge(s["gh_ready"], 8)
                    for t in range(T):
                        for k in range(4):
                            mm = pe.matmul(psW[:, 0, t * E + 2 * k:t * E + 2 * k + 2],
                                           ghsq(k)[:, t * P:(t + 1) * P], c("half"), start=True, stop=True)
                    mm.then_inc(s["route_done"], 1)
                else:
                    for t in range(T):
                        mm = pe.matmul(psW[:, 0, t * E:(t + 1) * E], xnT[:, t * P:(t + 1) * P], p(f"wg{l}"),
                                       start=True, stop=True)
                    mm.then_inc(s["route_done"], 1)
                for t in range(T):
                    mm = pe.matmul(psY[:, t // 4, (t % 4) * P:(t % 4 + 1) * P], X[:, t, :], c("ident"),
                                   start=(t % 4 == 0), stop=False, skip_group_check=True)
                mm.then_inc(s["y_started"], 1)
                if l == 3:
                    pe.wait_ge(s["cum_in"], 1)
                    pe.matmul(psW[:, 1, 0:T * E], beforeb[:, :], keepb[:, :, :].rearrange("p t e -> p (t e)"),
                              start=True, stop=False)
                    pe.matmul(psW[:, 1, 0:T * E], onesb[:, :], cumb[:, :, :].rearrange("p t e -> p (t e)"),
                              start=False, stop=True).then_inc(s["cum_done"], 1)
                pe.wait_ge(s["wsplit"], l + 1)
                psWb = psH[:, 0, :].bitcast(BF16)
                for t in range(T):
                    mm = pe.transpose(psWb[0:3 * E, t * P:(t + 1) * P],
                                      w3[:, t, :, :].rearrange("p a e -> p (a e)"), identb[:, :])
                if l == 2:
                    for t in range(T):
                        mm = pe.transpose(psH[0:E, 1 + t // 4, (t % 4) * P:(t % 4 + 1) * P], wts[:, t, :], c("ident"))
                mm.then_inc(s["wT_done"], 1)

            def ghsq(k):
                return [xe[0], xe[1], yT, SQ][k][:, :]

            def experts(l):
                tiles = row_tiles(HIDDEN[l])
                C, bufs, q0 = CHUNKS[l], BUFS[l], CHUNK_BASE[l]
                hidn = HIDDEN[l]
                if l == 0:
                    off = (0, hidn, 2 * hidn)
                elif l == 2:
                    off = (0, None, hidn)
                else:
                    off = (0, hidn, 2 * hidn)

                def spread(e):
                    if not (l == 0 and isinstance(e, int) and e == 0):
                        pe.wait_ge(s["xe_ready"], l * E + e)
                    for h in range(2):
                        mm = pe.matmul(psW[:, h, :], selb[:, bass.ds(e * P, P)], wT3[:, h * HALF:(h + 1) * HALF],
                                       start=True, stop=True)
                    mm.then_inc(s["wb_done"], 1)

                def up(e, u, ch, first):
                    i, h = ch // 2, ch % 2
                    m = tiles[i]
                    q = e * C + (q0 + ch)
                    bank = ch % bufs
                    if ch == 0:
                        done = sum(16 * (E // 2) for _ in range(l))
                        pe.wait_ge(s[f"pack{u}_loaded"], (e - u) * 8 + (done + 16))
                        pe.wait_ge(s["xe_ready"], l * E + e + 1)
                    if not (first and ch < bufs):
                        pe.wait_ge(s["h_done"], q - bufs + 1)
                    if l == 0:
                        mm = pe.matmul(psH[0:m, bank, :], pack[u][:, off[0] + i * P:off[0] + i * P + m],
                                       ghT[:, bass.ds((e - u) // 2 if isinstance(e, int) else pair(e, u), 1),
                                           h * HALF:(h + 1) * HALF],
                                       start=True, stop=True)
                    else:
                        mm = pe.matmul(psH[0:m, bank, :], pack[u][:, off[0] + i * P:off[0] + i * P + m],
                                       xnT[:, h * HALF:(h + 1) * HALF], start=True, stop=True)
                    if l != 2:
                        mm = pe.matmul(psH[0:m, 2 + bank, :], pack[u][:, off[1] + i * P:off[1] + i * P + m],
                                       xe[u][:, h * HALF:(h + 1) * HALF], start=True, stop=True)
                    mm.then_inc(s["gu_done"], 1)

                pairs = {}

                def pair(e, u):
                    return pairs["now"]

                def down(e, u, ch):
                    i, h = ch // 2, ch % 2
                    q = e * C + (q0 + ch)
                    pe.wait_ge(s["h_done"], q + 1)
                    pe.matmul(psY[:, h, :], pack[u][0:tiles[i], off[2] + i * P:off[2] + (i + 1) * P],
                              hid[ch % bufs][0:tiles[i], :], start=False, stop=False,
                              skip_group_check=True).then_inc(s["down_done"], 1)

                lag = bufs - 1

                def expert_pair(i, first=False):
                    pairs["now"] = i
                    for u in range(2):
                        e = i * 2 + u
                        for ch in range(C + lag):
                            if ch < C:
                                up(e, u, ch, first and u == 0)
                            if ch == 1 and not (u == 1 and isinstance(i, int) and i == E // 2 - 1):
                                spread(e + 1)
                            if ch >= lag:
                                down(e, u, ch - lag)

                pe.wait_ge(s["wT_ready"], l + 1)
                spread(0)
                expert_pair(0, True)
                with pe.Fori(1, E // 2 - 1) as i:
                    expert_pair(i)
                expert_pair(E // 2 - 1)
                if l == 2:
                    for h in range(2):
                        mm = pe.matmul(psY[:, h, :], p("b2", E), wT[:, h * HALF:(h + 1) * HALF],
                                       start=False, stop=False, skip_group_check=True)
                    mm.then_inc(s["y_done"], 1)
                if l + 1 < n_attn and l + 1 != 2:
                    keys_values(l + 1)
                for t in range(T):
                    if t % 4 == 0:
                        pe.wait_ge(s["yT_ready"], 2 * l + 1 + t // 4)
                    mm = pe.transpose(psY[:, t // 4, (t % 4) * P:(t % 4 + 1) * P], yT[:, t * P:(t + 1) * P], c("ident"))
                    if t % 4 == 3:
                        mm.then_inc(s["xt_done"], 1)

            for l in range(LAYERS):
                if l < n_attn:
                    if l == 2:
                        wide_attention()
                    else:
                        if l == 0:
                            keys_values(0)
                        pe.wait_ge(s["kv_ready"], l + 1 if l < 2 else 3)
                        norm_transpose(2 * l)
                        small_attention(l)
                if l < n_ffn:
                    norm_transpose(2 * l + 1)
                    route(l)
                    experts(l)

        @block.scalar
        def _(act):
            act.dma_start(cx[:, :, :, :].rearrange("p t b k -> p t (b k)"),
                          ctxT.rearrange("t p k -> p t k")).then_inc(s["load_cx"], 16)
            act.wait_ge(s["load_w0"], 16)

            def norm(k):
                for h in range(2):
                    act.wait_ge(s["xnT_done"], 2 * k + h + 1)
                    act.activation(xnT[:, h * HALF:(h + 1) * HALF], psT2[:, h, :], ACT.Copy).then_inc(s["xnT_ready"], 1)

            def keys_values(l):
                k, dk = (l if l < 2 else 2), DK[l]
                act.wait_ge(s["k_done"], k + 1)
                for h in range(2):
                    cols = slice(h * HALF, (h + 1) * HALF)
                    if l < 3:
                        act.activation(kt[:, cols], psW[:, h, :], ACT.Identity, bias=p(f"bk{l}"))
                    else:
                        act.activation(kt[:, cols], psW[:, h, :], ACT.Copy)
                if l == 0:
                    act.wait_ge(s["zeros_ready"], 1)
                for g in range(4):
                    act.wait_ge(s["v_done"], 4 * k + g + 1)
                    for h in range(2):
                        rows = slice(h * S, (h + 1) * S)
                        a = act.activation(
                            v2[dk][rows, 2 * g:2 * g + 2, :, :].rearrange("p t b (j h d) -> p (t b) j h d", h=2, d=dk)[:, :, :, h, :],
                            psH[rows, g, :].rearrange("p (t j h d) -> p t j h d", t=4, h=2, d=dk)[:, :, :, h, :],
                            ACT.Copy)
                a.then_inc(s["kv_ready"], 1)

            def probs_out(l, t, G):
                a = l * T + t
                for g in range(G):
                    act.wait_ge(s["pt_done"], 2 * a + (g + 1) * (2 // G))
                    if g == 0 and (l or not isinstance(t, int) or t > 0):
                        act.wait_ge(s["pv_done"], a)
                    act.activation(probT[:, 4 * g:4 * g + 4, :].rearrange("p j q -> p (j q)"), psT2[:, g, :],
                                   ACT.Copy).then_inc(s["pt_ready"], 2 // G)

            def small_attention(l):
                H = HEADS[l]
                G = H * S // 512
                n0, a0 = n_small(l), l * T

                def queries(t):
                    act.wait_ge(s["q_done"], n0 + t + 1)
                    if later(l, t):
                        act.wait_ge(s["s_done"], a0 + t)
                    if l < 3:
                        a = act.activation(qt[:, :], psA[:, 0:P], ACT.Identity, bias=p(f"bq{l}"))
                    else:
                        a = act.activation(qt[:, :], psA[:, 0:P], ACT.Copy, scale=Q_SCALE3)
                    a.then_inc(s["q_ready"], 1)

                def exps(t):
                    a = a0 + t
                    act.wait_ge(s["sub_done"], a + 1)
                    if l or not isinstance(t, int) or t > 0:
                        act.wait_ge(s["pt_done"], 2 * a)
                    act.activation(prob[:, 0:H * S], diff[:, 0:H * S], ACT.Exp,
                                   scale=EXP_SCALE[l]).then_inc(s["exp_done"], 1)

                def out_values(t):
                    n = n0 + t
                    act.wait_ge(s["ot_done"], n + 1)
                    if not (l == 0 and isinstance(t, int) and t == 0):
                        act.wait_ge(s["out_done"], a0 + t)
                    if l < 3:
                        act.activation(oT[:, 0, :], psM[:, 0:P], ACT.Identity, bias=p(f"bv{l}")).then_inc(s["ot_ready"], 1)
                    else:
                        act.activation(oT[:, 0, :], psM[:, 0:P], ACT.Copy).then_inc(s["ot_ready"], 1)

                def body(out, fin, sc, pre):
                    if out is not None:
                        out_values(out)
                    if fin is not None:
                        probs_out(l, fin, G)
                    if pre is not None:
                        queries(pre)
                    if sc is not None:
                        exps(sc)

                queries(0)
                steps(act, body)

            def wide_attention():
                a0 = 2 * T

                def exps(t):
                    act.wait_ge(s["sub_done"], a0 + t + 1)
                    act.wait_ge(s["pn_ready"], t)
                    act.activation(prob[:, :].rearrange("p (j h k) -> p h j k", j=8, h=2),
                                   diff[:, :].rearrange("p (h j k) -> p h j k", j=8, h=2), ACT.Exp,
                                   scale=EXP_SCALE[2]).then_inc(s["exp_done"], 1)

                def values_out(t):
                    act.wait_ge(s["pv_done"], a0 + t)
                    for b in range(2):
                        act.wait_ge(s["va_done" if b else "va0_done"], t + 1)
                        act.activation(va2[:, b, :, :].rearrange("p j d -> p (j d)"), psKV[:, b, :],
                                       ACT.Copy).then_inc(s["va_ready"], 1)

                def out_values(t):
                    act.wait_ge(s["pv_done"], a0 + t + 1)
                    act.wait_ge(s["out_done"], a0 + t)
                    src = psO2[:, :, :].rearrange("p b (j q) -> p j b q", j=8)
                    for g in range(2):
                        for j in range(4 * g, 4 * g + 4):
                            bv = PARAMS["bv2"][0] + j
                            a = act.activation(oT[:, j, :].rearrange("p (b q) -> p b q", b=2), src[:, j, :, :],
                                               ACT.Identity, bias=par[:, bv:bv + 1])
                        a.then_inc(s["ot2_ready"], 1)

                def body(out, fin, sc, pre):
                    if out is not None:
                        out_values(out)
                    if sc is not None:
                        exps(sc)
                    if fin is not None:
                        probs_out(2, fin, 2)
                        values_out(fin)

                steps(act, body)

            def route(l):
                if l == 0:
                    for k in range(4):
                        act.wait_ge(s["gh_done"], k + 1)
                        for h in range(2):
                            src = psH[:, (2 * k + h) % 4, :]
                            cols = slice(h * HALF, (h + 1) * HALF)
                            act.activation(ghT[:, k, cols], src, ACT.Copy)
                            act.activation([xe[0], xe[1], yT, SQ][k][:, cols], src,
                                           ACT.Square).then_inc(s["gh_ready"], 1)
                    act.wait_ge(s["route_done"], 1)
                    act.activation(R[2][:, :, :].rearrange("p t e -> p (t e)"), psW[:, 0, 0:T * E],
                                   ACT.Sqrt).then_inc(s["root_ready"], 1)
                act.wait_ge(s["ex_in"], l + 1)
                act.activation(R[1][:, :, :].rearrange("p t e -> p (t e)"), R[0][:, :, :].rearrange("p t e -> p (t e)"),
                               ACT.Exp).then_inc(s["ex_done"], 1)
                act.wait_ge(s["wT_done"], l + 1)
                a = act.activation(wT3[:, :], psH[0:3 * E, 0, :].bitcast(BF16), ACT.Copy)
                if l == 2:
                    for h in range(2):
                        a = act.activation(wT[:, h * HALF:(h + 1) * HALF], psH[0:E, 1 + h, :], ACT.Copy)
                a.then_inc(s["wT_ready"], 1)

            def experts(l):
                tiles = row_tiles(HIDDEN[l])
                C, bufs, q0 = CHUNKS[l], BUFS[l], CHUNK_BASE[l]

                def expert_pair(i, first=False):
                    for u in range(2):
                        e = i * 2 + u
                        for ch in range(C):
                            m = tiles[ch // 2]
                            q = e * C + (q0 + ch)
                            act.wait_ge(s["gu_done"], q + 1)
                            if not (first and u == 0 and ch < bufs):
                                act.wait_ge(s["h_done"], q - bufs + 1)
                            dst = act_s[ch % bufs][0:m, :]
                            src = psH[0:m, ch % bufs, :]
                            if l == 2:
                                b1 = HIDDEN[2] + 4 * P + ch // 2
                                a = act.activation(dst, src, ACT.Relu, bias=pack[u][:, b1:b1 + 1])
                            else:
                                a = act.activation(dst, src, ACT.Silu)
                            a.then_inc(s["act_done"], 1)

                expert_pair(0, True)
                with act.Fori(1, E // 2 - 1) as i:
                    expert_pair(i)
                expert_pair(E // 2 - 1)
                act.wait_ge(s["down_done"], q0 + E * C)
                if l == 2:
                    act.wait_ge(s["y_done"], 1)
                for h in range(2):
                    act.activation(yT[:, h * HALF:(h + 1) * HALF], psY[:, h, :], ACT.Copy).then_inc(s["yT_ready"], 1)
                if l + 1 < n_attn and l + 1 != 2:
                    keys_values(l + 1)

            for l in range(LAYERS):
                if l < n_attn:
                    if l == 0:
                        keys_values(0)
                    norm(2 * l)
                    if l == 2:
                        wide_attention()
                    else:
                        small_attention(l)
                if l < n_ffn:
                    norm(2 * l + 1)
                    route(l)
                    experts(l)

        @block.vector
        def _(dve):
            step = {"n": 0}

            def link(ins):
                step["n"] = step["n"] + 1
                ins.then_inc(s["dve_step"], 1)
                dve.wait_ge(s["dve_step"], step["n"])

            def add_mask_bias():
                dve.wait_ge(s["load_mask"], 32)
                dve.tensor_scalar(mbias[:, :, :, :].rearrange("b l t k -> b (l t k)"),
                                  mrow[:, :, :].rearrange("b l n -> b (l n)"), MASKED, -MASKED,
                                  ALU.mult, ALU.add).then_inc(s["mbias_ready"], 1)

            def add_to_residual(t, product):
                now = X[:, bass.ds(t, 1), :].rearrange("p a d -> p (a d)")
                link(dve.tensor_tensor(xsum[:, :], now, product, ALU.add))
                link(dve.bn_stats(bn[:, :], xsum[:, :]))
                dve.tensor_copy(bns[:, bass.ds(t, 1), :].rearrange("p a s -> p (a s)"), bn[:, :])
                dve.tensor_copy(now, xsum[:, :]).then_inc(s["resid_done"], 1)

            def norm(k):
                var, y, y2, h = root[:, 0, :], root[:, 1, :], root[:, 2, :], root[:, 3, :]
                for t in range(T):
                    ins = dve.bn_aggr(stat[:, t, :], bns[:, t, :])
                link(ins)
                link(dve.tensor_scalar(var, stat[:, :, 1], EPS, None, ALU.add))
                link(dve.tensor_scalar(h.bitcast(I32), var.bitcast(I32), 1, None, ALU.logical_shift_right))
                link(dve.tensor_scalar(y.bitcast(I32), h.bitcast(I32), -1, MAGIC, ALU.mult, ALU.add))
                for _ in range(4):
                    link(dve.tensor_tensor(y2, y, y, ALU.mult))
                    link(dve.scalar_tensor_tensor(h, y2, -0.5, var, ALU.mult, ALU.mult))
                    link(dve.scalar_tensor_tensor(y, h, 1.5, y, ALU.add, ALU.mult))
                if k:
                    dve.wait_ge(s["xnT_done"], 2 * k)
                for t in range(T):
                    dve.tensor_scalar(XC[:, t, :], X[:, t, :], stat[:, t, 0:1], root[:, 1, t:t + 1],
                                      ALU.subtract, ALU.mult).then_inc(s["xn_ready"], 1)

            def loop_steps(body, links):
                body(None, None, 0, 1)
                body(None, 0, 1, 2)
                body(0, 1, 2, 3)
                base = step["n"]
                with dve.Fori(3, T - 1) as i:
                    step["n"] = (i - 3) * links + base
                    body(i - 2, i - 1, i, i + 1)
                step["n"] = base + (T - 4) * links
                body(T - 3, T - 2, T - 1, None)
                body(T - 2, T - 1, None, None)
                body(T - 1, None, None, None)

            def heads(ap, H):
                return ap.rearrange("p (h k) -> p h k", h=H)

            def small_attention(l):
                H, dk = HEADS[l], DK[l]
                G = H * S // 512
                n0, a0 = n_small(l), l * T
                W = H * S
                raw = psS[:, 0:G, :].rearrange("p g n -> p (g n)")

                def softmax_in(t):
                    a = a0 + t
                    dve.wait_ge(s["s_done"], a + 1)
                    src = raw
                    if l == 3:
                        if not isinstance(t, int) or t > 0:
                            dve.wait_ge(s["nz_ready"], t)
                        link(dve.tensor_tensor(heads(gated[:, :], H), heads(raw, H),
                                               gat[:, bass.ds(t, 1), :].to_broadcast([P, H, S]), ALU.mult))
                        src = gated[:, :]
                    link(dve.tensor_reduce(mx[:, 0:H], heads(src, H), AX.X, ALU.max))
                    if l or not isinstance(t, int) or t > 0:
                        dve.wait_ge(s["exp_done"], a)
                    dve.tensor_tensor(heads(diff[:, 0:W], H), heads(src, H),
                                      mx[:, 0:H].unsqueeze(2).to_broadcast([P, H, S]),
                                      ALU.subtract).then_inc(s["sub_done"], 1)

                def normalise_out(t):
                    n = n0 + t
                    dve.wait_ge(s["pv_done"], a0 + t + 1)
                    if not (l == 0 and isinstance(t, int) and t == 0):
                        dve.wait_ge(s["ot_done"], n)
                    for b in range(2):
                        q = slice(b * S, (b + 1) * S)
                        ins = dve.tensor_tensor(
                            on[q, :].rearrange("p (j h d) -> p j h d", h=2, d=dk),
                            psO[q, 0:2 * P].rearrange("p (j b h d) -> p j b h d", b=2, h=2, d=dk)[:, :, b, :, :],
                            sm[q, 1, 0:H].rearrange("p (j h) -> p j h", h=2).unsqueeze(3)
                              .to_broadcast([S, H // 2, 2, dk]), ALU.mult)
                    ins.then_inc(s["on_ready"], 1)

                def sums(t):
                    a = a0 + t
                    dve.wait_ge(s["exp_done"], a + 1)
                    link(dve.tensor_reduce(sm[:, 0, 0:H], heads(prob[:, 0:W], H), AX.X, ALU.add))
                    link(dve.reciprocal(sm[:, 1, 0:H], sm[:, 0, 0:H]))
                    if l == 3:
                        dve.wait_ge(s["pt_done"], 2 * a)
                        dve.scalar_tensor_tensor(pnorm[:, 0:W], gated[:, :], 0.0, prob[:, 0:W],
                                                 ALU.not_equal, ALU.mult).then_inc(s["nz_ready"], 1)

                def residual(t):
                    a = a0 + t
                    dve.wait_ge(s["out_done"], a + 1)
                    add_to_residual(t, psM[:, P:2 * P])

                def body(out, fin, sc, pre):
                    if sc is not None:
                        softmax_in(sc)
                    if out is not None:
                        residual(out)
                    if fin is not None:
                        normalise_out(fin)
                    if sc is not None:
                        sums(sc)

                loop_steps(body, 6 if l == 3 else 5)

            def wide_attention():
                a0 = 2 * T

                def with_bias(dst, bias, g):
                    a = PARAMS[bias][0] + 4 * g
                    return dve.tensor_tensor(dst[:, 4 * g:4 * g + 4, :], psKV[:, g, :].rearrange("p (j q) -> p j q", j=4),
                                             par[:, a:a + 4].unsqueeze(2).to_broadcast([P, 4, P]), ALU.add)

                def keys(t):
                    if later(0, t):
                        dve.wait_ge(s["s_done"], a0 + t)
                    for g in range(2):
                        dve.wait_ge(s["k2_done"], 2 * t + g + 1)
                        with_bias(kt2, "bk2", g).then_inc(s["k2_ready"], 1)

                def queries(t):
                    for g in range(2):
                        dve.wait_ge(s["q2_done"], 2 * t + g + 1)
                        with_bias(qt2, "bq2", g).then_inc(s["q2_ready"], 1)

                keys(0)

                def softmax_in(t):
                    a = a0 + t
                    dve.wait_ge(s["s_done"], a + 1)
                    src = psS[:, :, :].rearrange("p h (j k) -> p (h j) k", j=8)
                    link(dve.tensor_reduce(mx[:, :], src, AX.X, ALU.max))
                    dve.wait_ge(s["exp_done"], a)
                    dve.tensor_tensor(heads(diff[:, :], 16), src, mx[:, :].unsqueeze(2).to_broadcast([P, 16, S]),
                                      ALU.subtract).then_inc(s["sub_done"], 1)

                def normalise(t):
                    a = a0 + t
                    dve.wait_ge(s["exp_done"], a + 1)
                    link(dve.tensor_reduce(sm[:, 0, :], heads(prob[:, :], 16), AX.X, ALU.add))
                    link(dve.reciprocal(sm[:, 1, :], sm[:, 0, :]))
                    dve.wait_ge(s["pt_done"], 2 * a)
                    dve.tensor_tensor(heads(pnorm[:, :], 16), heads(prob[:, :], 16),
                                      sm[:, 1, :].unsqueeze(2).to_broadcast([P, 16, S]),
                                      ALU.mult).then_inc(s["pn_ready"], 1)

                def residual(t):
                    dve.wait_ge(s["out_done"], a0 + t + 1)
                    add_to_residual(t, psO2[:, 0, 0:P])

                def body(out, fin, sc, pre):
                    if sc is not None:
                        softmax_in(sc)
                    if out is not None:
                        residual(out)
                    if pre is not None:
                        keys(pre)
                        queries(pre)
                    if sc is not None:
                        normalise(sc)

                queries(0)
                loop_steps(body, 5)

            def flat(ap):
                return ap[:, :, :].rearrange("p t e -> p (t e)")

            def over_experts(ap):
                return ap.unsqueeze(2).to_broadcast([P, T, E])

            def route(l):
                score, top, keep = R[2], rs[:, 0, :], R[3]
                dve.wait_ge(s["route_done"], l + 1)
                src = psW[:, 0, 0:T * E]
                if l == 0:
                    dve.wait_ge(s["root_ready"], 1)
                elif l == 2:
                    link(dve.tensor_tensor(score[:, :, :], src.rearrange("p (t e) -> p t e", t=T),
                                           p("rb2").unsqueeze(1).to_broadcast([P, T, E]), ALU.add))
                else:
                    link(dve.tensor_copy(flat(score), src))
                link(dve.tensor_reduce(top, score[:, :, :], AX.X, ALU.max))
                dve.tensor_tensor(R[0][:, :, :], score[:, :, :], over_experts(top),
                                  ALU.subtract).then_inc(s["ex_in"], 1)
                dve.wait_ge(s["ex_done"], l + 1)
                ex = R[1]
                if l in (1, 3):
                    link(dve.tensor_reduce(rs[:, 1, :], ex[:, :, :], AX.X, ALU.add))
                    link(dve.reciprocal(rs[:, 1, :], rs[:, 1, :]))
                    link(dve.tensor_tensor(ex[:, :, :], ex[:, :, :], over_experts(rs[:, 1, :]), ALU.mult))
                    score = ex
                other = score[:, :, :].unsqueeze(2).to_broadcast([P, T, E, E])
                own = score[:, :, :].unsqueeze(3).to_broadcast([P, T, E, E])
                dve.tensor_tensor(cmp1[:, :, :, :], other, own, ALU.is_gt)
                link(dve.tensor_tensor(cmp2[:, :, :, :], other, own, ALU.is_equal))
                link(dve.tensor_tensor(cmp2[:, :, :, :].rearrange("p t a b -> p t (a b)"),
                                       cmp2[:, :, :, :].rearrange("p t a b -> p t (a b)"),
                                       c("tri").unsqueeze(1).to_broadcast([P, T, E * E]), ALU.mult))
                link(dve.tensor_tensor(cmp1[:, :, :, :].rearrange("p t a b -> p (t a b)"),
                                       cmp1[:, :, :, :].rearrange("p t a b -> p (t a b)"),
                                       cmp2[:, :, :, :].rearrange("p t a b -> p (t a b)"), ALU.add))
                link(dve.tensor_reduce(flat(R[4]), cmp1[:, :, :, :].rearrange("p t a b -> p (t a) b"), AX.X, ALU.add))
                link(dve.tensor_scalar(flat(keep), flat(R[4]), 1.5, None, ALU.is_lt))
                if l == 3:
                    dve.tensor_copy(keepb[:, :, :], keep[:, :, :])
                    link(dve.memset(cumb[:, 0, :], 0.0))
                    for t in range(1, T):
                        ins = dve.tensor_tensor(cumb[:, t, :], cumb[:, t - 1, :], keep[:, t - 1, :], ALU.add)
                        if t < T - 1:
                            link(ins)
                    ins.then_inc(s["cum_in"], 1)
                if l == 3:
                    link(dve.tensor_tensor(wts[:, :, :], ex[:, :, :], keep[:, :, :], ALU.mult))
                    dve.wait_ge(s["cum_done"], 1)
                    link(dve.scalar_tensor_tensor(flat(wts), psW[:, 1, 0:T * E], CAPACITY - 0.5, flat(wts),
                                                  ALU.is_lt, ALU.mult))
                else:
                    link(dve.tensor_tensor(ex[:, :, :], ex[:, :, :], keep[:, :, :], ALU.mult))
                    link(dve.tensor_reduce(rs[:, 0, :], ex[:, :, :], AX.X, ALU.add))
                    if l == 1:
                        link(dve.tensor_scalar(rs[:, 0, :], rs[:, 0, :], 1e-20, None, ALU.add))
                    link(dve.reciprocal(rs[:, 1, :], rs[:, 0, :]))
                    link(dve.tensor_tensor(wts[:, :, :], ex[:, :, :], over_experts(rs[:, 1, :]), ALU.mult))
                link(dve.tensor_copy(w3[:, :, 0, :], wts[:, :, :]))
                link(dve.tensor_tensor(wres[:, 0, :, :], wts[:, :, :], w3[:, :, 0, :], ALU.subtract))
                link(dve.tensor_copy(w3[:, :, 1, :], wres[:, 0, :, :]))
                link(dve.tensor_tensor(wres[:, 1, :, :], wres[:, 0, :, :], w3[:, :, 1, :], ALU.subtract))
                dve.tensor_copy(w3[:, :, 2, :], wres[:, 1, :, :]).then_inc(s["wsplit"], 1)

            def experts(l):
                tiles = row_tiles(HIDDEN[l])
                C, bufs, q0 = CHUNKS[l], BUFS[l], CHUNK_BASE[l]

                def weighted_input(e, u, first=False):
                    dve.wait_ge(s["wb_done"], l * E + e + 1)
                    if not first:
                        dve.wait_ge(s["down_done"], q0 + (e - 1) * C)
                    w = psW[:, :, :].rearrange("p g n -> p (g n)")
                    if l == 2:
                        link_free = dve.tensor_copy(xe[u][:, :], w)
                    else:
                        link_free = dve.tensor_tensor(xe[u][:, :], xnT[:, :], w, ALU.mult)
                    link_free.then_inc(s["xe_ready"], 1)

                def expert_pair(i, first=False):
                    for u in range(2):
                        e = i * 2 + u
                        for ch in range(C):
                            m = tiles[ch // 2]
                            q = e * C + (q0 + ch)
                            dve.wait_ge(s["act_done"], q + 1)
                            if not (first and u == 0 and ch < bufs):
                                dve.wait_ge(s["down_done"], q - bufs + 1)
                            if l == 2:
                                other = xe[u][0:m, (ch % 2) * HALF:(ch % 2 + 1) * HALF]
                                if ch == 0:
                                    dve.wait_ge(s["xe_ready"], l * E + e + 1)
                            else:
                                other = psH[0:m, 2 + ch % bufs, :]
                            dve.tensor_tensor(hid[ch % bufs][0:m, :], act_s[ch % bufs][0:m, :], other,
                                              ALU.mult).then_inc(s["h_done"], 1)
                            if ch == 1 and not (u == 1 and isinstance(i, int) and i == E // 2 - 1):
                                weighted_input(e + 1, 1 - u, first and u == 0)

                weighted_input(0, 0, True)
                expert_pair(0, True)
                with dve.Fori(1, E // 2 - 1) as i:
                    expert_pair(i)
                expert_pair(E // 2 - 1)
                for t in range(T):
                    dve.wait_ge(s["xt_done"], 2 * l + 1 + t // 4)
                    dve.tensor_copy(X[:, t, :], psY[:, t // 4, (t % 4) * P:(t % 4 + 1) * P]).then_inc(s["x_ready"], 1)
                    if l + 1 < n_attn:
                        dve.wait_ge(s["x_ready"], l * T + t + 1)
                        ins = dve.bn_stats(bns[:, t, :], X[:, t, :])
                if l + 1 < n_attn:
                    link(ins)

            dve.wait_ge(s["load_x"], 16)
            for t in range(T):
                ins = dve.bn_stats(bns[:, t, :], X[:, t, :])
            link(ins)
            for l in range(LAYERS):
                if l < n_attn:
                    norm(2 * l)
                    if l == 0:
                        add_mask_bias()
                    dve.wait_ge(s["bo_added"], l + 1)
                    if l == 2:
                        wide_attention()
                    else:
                        small_attention(l)
                    dve.wait_ge(s["resid_done"], (l + 1) * T)
                if l < n_ffn:
                    norm(2 * l + 1)
                    route(l)
                    experts(l)


def constants():
    con = np.zeros((P, N_CONST), np.float32)
    r = np.arange(P)

    def put(name, value):
        a, b = CONSTS[name]
        con[:value.shape[0], a:b] = value

    put("ident", np.eye(P))
    put("hmask8", (r[:, None] // 8 == np.arange(16)[None]))
    put("hmask16", (r[:, None] // 16 == np.arange(8)[None]))
    e = np.arange(E)
    put("tri", np.broadcast_to((e[None, :] < e[:, None]).reshape(1, E * E), (P, E * E)))
    put("before", (r[:, None] < r[None, :]))
    put("bsel", (np.arange(2)[:, None] == r[None] // S))
    put("half", (r[:, None] // 64 == np.arange(2)[None]))
    return con


def selectors():
    e = np.arange(E)
    sel = (np.arange(3 * E)[:, None, None] % E == e[None, :, None]) * np.ones((1, 1, P))
    return sel.reshape(3 * E, E * P).astype(np.float32)


def kernel(**inputs):
    import concourse.bacc as _bacc
    from concourse.bass_utils import run_bass_kernel_spmd as _run
    i = {k: np.asarray(v) for k, v in inputs.items()}
    stages = STAGES

    par = np.zeros((P, N_PARAM), np.float32)

    def put(name, value):
        a, b = PARAMS[name]
        par[:value.shape[0], a:b] = value

    put("w0", np.concatenate([i["L0_xattn_Wq"], i["L0_xattn_Wk"], i["L0_xattn_Wv"], i["L0_xattn_Wo"]], 1))
    put("w1", np.concatenate([i["L1_xattn_wq_w"].T, i["L1_xattn_wk_w"].T, i["L1_xattn_wv_w"].T,
                              i["L1_xattn_wo_w"].T], 1))
    put("w3", np.concatenate([i["L3_xattn_Wq"].T, i["L3_xattn_Wk"].T, i["L3_xattn_Wv"].T, i["L3_xattn_Wp"].T], 1))
    put("wa", i["L0_ffn_W_A"].reshape(512, P).T)
    for n in "qkv":
        put(f"b{n}0", i[f"L0_xattn_b{n}"].reshape(P, 1))
        put(f"b{n}1", i[f"L1_xattn_w{n}_b"].reshape(P, 1))
        put(f"b{n}2", i[f"L2_xattn_b{n}"].reshape(8, P).T)
    bo = np.stack([i["L0_xattn_bo"], i["L1_xattn_wo_b"], i["L2_xattn_bu"], i["L3_xattn_bp"]]).reshape(1, 4 * P)
    put("bo", np.broadcast_to(bo, (P, 4 * P)))
    put("wg1", i["L1_ffn_Wg"].T)
    put("wg2", i["L2_ffn_router_w"])
    put("wg3", i["L3_ffn_w_gate"])
    put("rb2", np.broadcast_to(i["L2_ffn_router_b"].reshape(1, E), (P, E)))
    put("b2", i["L2_ffn_b2"])

    wide = np.zeros((P, N_WIDE), np.float32)
    wide[:, 0:1024] = i["L2_xattn_Wq"]
    wide[:, 1024:2048] = i["L2_xattn_Wk"]
    wide[:, 2048:3072] = i["L2_xattn_Wv"].reshape(P, 8, 2, 64).transpose(0, 2, 1, 3).reshape(P, 1024)
    wide[:, 3072:4096] = i["L2_xattn_Wu"].reshape(8, P, P).transpose(1, 0, 2).reshape(P, 1024)

    def down_tiles(w):
        e, h, d = w.shape
        t = -(-h // P)
        padded = np.zeros((e, t * P, d), np.float32)
        padded[:, :h] = w
        return padded.reshape(e, t, P, d).transpose(0, 2, 1, 3).reshape(e, P, t * d)

    wb = np.zeros((E, P, HIDDEN[0]), np.float32)
    for e in range(E):
        wb[e, 64 * (e % 2):64 * (e % 2) + 64] = i["L0_ffn_W_B"][e].T
    packs = [
        np.concatenate([wb, i["L0_ffn_W_up"].transpose(0, 2, 1), down_tiles(i["L0_ffn_W_down"].transpose(0, 2, 1))], 2),
        np.concatenate([i["L1_ffn_W1"].transpose(0, 2, 1), i["L1_ffn_W3"].transpose(0, 2, 1),
                        down_tiles(i["L1_ffn_W2"].transpose(0, 2, 1))], 2),
        np.concatenate([i["L2_ffn_w1"], down_tiles(i["L2_ffn_w2"]),
                        i["L2_ffn_b1"].reshape(E, 4, P).transpose(0, 2, 1)], 2),
        np.concatenate([i["L3_ffn_c_fc"], down_tiles(i["L3_ffn_c_proj"])], 2),
    ]
    arrays = {
        "x": i["x"].reshape(N, D),
        "ctxT": np.broadcast_to(i["ctx_1024"].reshape(T, 2, 1, S, D), (T, 2, 2, S, D)).reshape(T, 4 * S, D)
                  .transpose(0, 2, 1),
        "gate": i["fside_BxSxS2_0"].reshape(N, S),
        "mask0": i["mask_Bx1xS2_bf1"].reshape(T, 2, S).transpose(1, 0, 2).reshape(2, T * S).view(np.uint8),
        "mask1": i["mask_BxS2_bf1"].reshape(T, 2, S).transpose(1, 0, 2).reshape(2, T * S).view(np.uint8),
        "consts": constants(),
        "selc": selectors(),
        "params": par,
        "wide": wide,
    }
    for l in range(LAYERS):
        arrays[f"pack{l}"] = packs[l]
    nc = _bacc.Bacc("TRN2", target_bir_lowering=False, num_devices=1)
    feed, aps = {}, {}
    for name, a in arrays.items():
        a = np.ascontiguousarray(a)
        feed[f"in_{name}"] = a
        aps[name] = nc.dram_tensor(f"in_{name}", a.shape, mybir.dt.from_np(a.dtype), kind="ExternalInput").ap()
    out = nc.dram_tensor("out", (N, D), F32, kind="ExternalOutput").ap()
    build(nc, aps["x"], aps["ctxT"], aps["gate"], aps["mask0"], aps["mask1"], aps["consts"], aps["selc"], aps["params"],
          aps["wide"], [aps[f"pack{l}"] for l in range(LAYERS)], out, stages)
    r = _run(nc, [feed], core_ids=[0])
    return r.results[0]["out"].reshape(B, S, D)


STAGES = 8
```

```python
from contextlib import ExitStack

import numpy as np
import concourse.bass as bass
from concourse import mybir

F32 = mybir.dt.float32
BF16 = mybir.dt.bfloat16
I32 = mybir.dt.int32
F32R = mybir.dt.float32r
U8 = mybir.dt.uint8
ALU = mybir.AluOpType
ACT = mybir.ActivationFunctionType
AX = mybir.AxisListType

P = 128
D = 128
B, S = 16, 64
T = B * S // P
N = B * S
HALF = 512
E = 8
CAPACITY = 512
EPS = 1e-5
MAGIC = 0x5F3759DF
MASKED = 2.0 ** 100

LAYERS = 4
HEADS = [16, 16, 16, 8]
DK = [8, 8, 64, 16]
EXP_SCALE = [8 ** -0.5, 8 ** -0.5, 64 ** -0.5, 1.0]
Q_SCALE3 = 16 ** -0.5
PAIR = {8: 2 * 8 + 2, 16: 2 * 16}
HIDDEN = [256, 352, 512, 192]


def row_tiles(h):
    return [min(P, h - r) for r in range(0, h, P)]


CHUNKS = [2 * len(row_tiles(h)) for h in HIDDEN]
CHUNK_BASE = [E * sum(CHUNKS[:l]) for l in range(LAYERS)]
BUFS = [2, 2, 4, 2]
RING = 4
LAG = [2, 3, 3, 2]
PACK = [HIDDEN[0] * 2, HIDDEN[1] * 2 + 3 * P, HIDDEN[2] + 4 * P + 4, HIDDEN[3] * 2 + 2 * P]
CUT = [HIDDEN[0] * 3] + PACK[1:]
PACK_MAX = max(PACK)

CONSTS, PARAMS = {}, {}


def columns(table, items):
    at = 0
    for name, n in items:
        table[name] = (at, at + n)
        at += n
    return at


N_CONST = columns(CONSTS, [("ident", P), ("hmask8", 16), ("hmask16", 8),
                           ("upper", 64), ("limit", E), ("before", P), ("bsel", P), ("half", 2)])
N_PARAM = columns(PARAMS, [("w0", 4 * P), ("bq0", 1), ("bk0", 1), ("bv0", 1),
                           ("w1", 4 * P), ("w3", 4 * P), ("wa", 4 * P), ("wan", 4 * P), ("bq1", 1), ("bk1", 1), ("bv1", 1),
                           ("bq2", 8), ("bk2", 8), ("bv2", 8), ("bo", 4 * P),
                           ("wg1", E), ("wg2", E), ("wg3", E), ("rb2", E), ("b2", P)])
PARAMS["first"] = (0, PARAMS["w1"][0])
PARAMS["rest"] = (PARAMS["w1"][0], N_PARAM)
N_WIDE = 4 * 1024


def n_small(l):
    return T * (l if l < 3 else 2)


def build(nc, x, ctxT, gate, mask0, mask1, consts, selc, params, wb, wide, packs, out):
    with ExitStack() as ctx:
        def sb(name, shape, dt=F32):
            return ctx.enter_context(nc.sbuf_tensor(name, shape, dt))

        def sem(name):
            return ctx.enter_context(nc.semaphore(name))

        X = sb("X", [P, T, D])
        XC = sb("XC", [P, T, D])
        bn = sb("bn", [P, 6])
        bns = sb("bns", [P, T, 6])
        xsum = sb("xsum", [P, P])
        stat = sb("stat", [P, T, 2])
        root = sb("root", [P, 4, T])
        xnT = sb("xnT", [P, N])
        con = sb("con", [P, N_CONST])
        sel = sb("sel", [3 * E, E * P])
        par = sb("par", [P, N_PARAM])
        wid = sb("wid", [P, N_WIDE])
        wb8 = wid[:, 0:2048].rearrange("p (e f) -> p e f", e=E)
        wba = wid[:, 2048:4096].rearrange("p (e f) -> p e f", e=E)
        identb = sb("identb", [P, P], BF16)
        beforeb = sb("beforeb", [P, P], BF16)
        onesb = sb("onesb", [P, P], BF16)
        one = sb("one", [P, 1])
        selb = sb("selb", [3 * E, E * P], BF16)
        bselb = sb("bselb", [2, P], BF16)
        mrow = sb("mrow", [2, 2, T * S], U8)
        mbias = sb("mbias", [2, 2, T, S], BF16)
        gat = sb("gat", [P, T, S])
        cx = sb("cx", [P, T, 2, 2 * S])
        ctv = sb("ctv", [P, P])
        kt = sb("kt", [P, N])
        qt = sb("qt", [P, P])
        km = sb("km", [P, 2, 1024])
        kt2 = km[:, :, :].rearrange("p b n -> p (b n)").rearrange("p (j b h k) -> p j b h k", j=8, b=2, h=2)
        hid = [km[:, i // 2, (i % 2) * HALF:(i % 2 + 1) * HALF] for i in range(RING)]
        v2 = {dk: sb(f"v2_{dk}", [P, T, 2, P // (2 * dk) * PAIR[dk]]) for dk in (8, 16)}
        diff = sb("diff", [P, 1024])
        yT = diff[:, :]
        gated = sb("gated", [P, 512])
        probs = sb("probs", [P, 2, 1024])
        prob, pnorm = probs[:, 0, :], probs[:, 1, :]
        act_s = [probs[:, i // 2, (i % 2) * HALF:(i % 2 + 1) * HALF] for i in range(RING)]
        mx = sb("mx", [P, 16])
        sm = sb("sm", [P, 2, 16])
        probT = sb("probT", [P, 8, P])
        on = sb("on", [P, P])
        oT = sb("oT", [P, 8, P])
        kq2 = sb("kq2", [P, 2, 1024])
        qt2 = kq2[:, 1, :].rearrange("p (j q) -> p j q", j=8)
        cx0 = kq2[:, 0, :]
        xe = [kq2[:, u, :] for u in range(2)]
        va2 = sb("va2", [P, 2, 8, 64])
        below_top, exps_r, score_r, keep_r, rank_r, square_sum = (
            sb(n, [P, T, E]) for n in ("below_top", "exps_r", "score_r", "keep_r", "rank_r", "square_sum"))
        cmp1, cmp2 = (oT[:, 4 * i:4 * i + 4, :].rearrange("p j q -> p (j q)")
                      .rearrange("p (t a b) -> p t a b", a=E, b=E) for i in range(2))
        rs = sb("rs", [P, 2, T])
        wts = sb("wts", [P, T, E])
        wres = sb("wres", [P, T, E])
        w3 = sb("w3", [P, T, 3, E], BF16)
        keepb = sb("keepb", [P, T, E], BF16)
        cumb = sb("cumb", [P, T, E], BF16)
        wT3 = sb("wT3", [3 * E, N], BF16)
        wT = sb("wT", [E, N])
        pack = [sb(f"pack{u}", [P, PACK_MAX]) for u in range(2)]
        whi = [sb(f"whi{u}", [P, PACK_MAX], F32R) for u in range(2)]
        wlo = [sb(f"wlo{u}", [P, PACK_MAX], F32R) for u in range(2)]
        xhi = sb("xhi", [P, N], F32R)
        xlo = sb("xlo", [P, N], F32R)
        xehi = [sb(f"xehi{u}", [P, N], F32R) for u in range(2)]
        xelo = [sb(f"xelo{u}", [P, N], F32R) for u in range(2)]
        hhi = [sb(f"hhi{i}", [P, HALF], F32R) for i in range(RING)]
        hlo = [sb(f"hlo{i}", [P, HALF], F32R) for i in range(RING)]

        PS = ctx.enter_context(nc.psum_tensor("PS", [P, 8, 512], F32))
        psS = PS[:, 0:2, :]
        psT2 = PS[:, 2:4, :]
        psA = PS[:, 4, :]
        psO = PS[:, 6, :]
        psM = PS[:, 7, :]
        psKV = PS[:, 4:6, :]
        psO2 = PS[:, 6:8, :]
        psH = PS[:, 0:4, :]
        psY = PS[:, 4:6, :]
        psW = PS[:, 6:8, :]

        names = """load_x load_cx load_con load_sel load_w0 load_par load_wb load_wide load_gate load_mask
            pack0_loaded pack1_loaded consts_ready zeros_ready cx_ready sel_ready mbias_ready dve_step pool_step
            xn_ready xnT_done xnT_ready bo_added
            k_done v_done k_ready kv_ready q_done q_ready km_ready s0_done s_done sub0_done sub_done exp_done
            pt_done pt_ready pv_done on_ready ot_done ot_ready out_done resid_done
            pn_ready nz_ready ot2_ready ctv_ready k2_zeroed k2_done k2_ready q2_done q2_ready va0_done va_done va_ready
            nat_done sq_ready ssq_ready xhi_ready xlo_ready w_ready xe_step hf_done hhi_done
            wba_done wba_ready root_ready route_done ex_in ex_done wsplit wT_done wT_ready cum_in cum_done
            w2T_done w2T_ready wb0_done wb_done xe0_ready xe_ready gu_done act_done h_done down_done y_done yT_ready xt_done xstat_done x_ready
            stored""".split()
        s = {n: sem(n) for n in names}

        def c(name, rows=P):
            a, b = CONSTS[name]
            return con[0:rows, a:b]

        def p(name, rows=P):
            a, b = PARAMS[name]
            return par[0:rows, a:b]

        def attn_w(l, i):
            a = PARAMS[f"w{l}"][0] + i * P
            return par[:, a:a + P]

        def tile(ap, t):
            return ap[:, bass.ds(t * P, P)]

        def steps(eng, body):
            body(None, None, 0, 1)
            body(None, 0, 1, 2)
            body(0, 1, 2, 3)
            with eng.Fori(3, T - 1) as i:
                body(i - 2, i - 1, i, i + 1)
            body(T - 3, T - 2, T - 1, None)
            body(T - 2, T - 1, None, None)
            body(T - 1, None, None, None)

        def later(l, t):
            return bool(l) or not isinstance(t, int) or t > 0

        block = ctx.enter_context(nc.Block())

        @block.sync
        def _(sp):
            sp.dma_start(X[:, :, :], x).then_inc(s["load_x"], 16)
            a, b = PARAMS["first"]
            sp.dma_start(par[:, a:b], params[:, a:b]).then_inc(s["load_w0"], 16)
            sp.dma_start(con[:, :], consts).then_inc(s["load_con"], 16)
            sp.dma_start(mrow[:, 0, :], mask0).then_inc(s["load_mask"], 16)
            sp.dma_start(mrow[:, 1, :], mask1).then_inc(s["load_mask"], 16)
            sp.dma_start(sel[:, :], selc).then_inc(s["load_sel"], 16)
            a, b = PARAMS["rest"]
            sp.dma_start(par[:, a:b], params[:, a:b]).then_inc(s["load_par"], 16)
            sp.dma_start(gat[:, :, :], gate).then_inc(s["load_gate"], 16)
            sp.dma_start(wid[:, 0:2048], wb).then_inc(s["load_wb"], 16)
            for l in range(LAYERS):
                q0 = CHUNK_BASE[l]

                def load_pack(e, u):
                    sp.dma_start(pack[u][:, 0:PACK[l]], packs[l][e, :, :]).then_inc(s[f"pack{u}_loaded"], 16)
                for u in range(2):
                    if l == 3:
                        sp.wait_ge(s["act_done"], q0 - (1 - u) * CHUNKS[2])
                    elif l > 0:
                        sp.wait_ge(s["w_ready"], l * E - 1 + u)
                    load_pack(u, u)
                if l == 1:
                    sp.wait_ge(s["w_ready"], E)
                    sp.dma_start(wid[:, :], wide).then_inc(s["load_wide"], 16)
                with sp.Fori(1, E // 2) as i:
                    for u in range(2):
                        if l == 2:
                            sp.wait_ge(s["act_done"], (i * 2 + (u - 1)) * CHUNKS[2] + q0)
                        else:
                            sp.wait_ge(s["w_ready"], i * 2 + (u + l * E - 1))
                        load_pack(i * 2 + u, u)
            for h in range(2):
                tiles = slice(h * T // 2, (h + 1) * T // 2)
                sp.wait_ge(s["x_ready"], LAYERS * T - (1 - h) * T // 2)
                sp.dma_start(out[:, tiles, :], X[:, tiles, :]).then_inc(s["stored"], 16)
            sp.wait_ge(s["stored"], 32)

        @block.gpsimd
        def _(pool):
            for dk in (8, 16):
                pool.memset(v2[dk][:, :, :, :].rearrange("p t b c -> p (t b c)"), 0.0).then_inc(s["zeros_ready"], 1)
            pool.wait_ge(s["zeros_ready"], 2)
            pool.wait_ge(s["load_con"], 16)
            pool.tensor_copy(v2[8][:, :, :, :].rearrange("p t b (j c) -> p (t b) j c", c=PAIR[8])[:, :, :, 16:18],
                             c("half").unsqueeze(1).unsqueeze(1).to_broadcast([P, 2 * T, 8, 2])
                             ).then_inc(s["zeros_ready"], 1)
            pool.tensor_copy(identb[:, :], c("ident"))
            pool.tensor_copy(beforeb[:, :], c("before"))
            pool.tensor_copy(bselb[:, :], c("bsel", 2))
            pool.memset(onesb[:, :], 1.0)
            pool.memset(one[:, :], 1.0).then_inc(s["consts_ready"], 1)
            pool.wait_ge(s["load_par"], 16)
            for l in range(LAYERS):
                H = HEADS[l]
                n0 = n_small(l)

                def mask_keys(t):
                    hm = c(f"hmask{DK[l]}")
                    for g in range(H // 8):
                        if later(l, t):
                            pool.wait_ge(s["s_done"], l * T + t) if g == H // 8 - 1 else pool.wait_ge(s["s0_done"], n0 + t)
                        for b in range(2):
                            at = t * P + b * S if g == 0 else (t * 2 + b) * S
                            ins = pool.tensor_tensor(
                                km[:, b, g * 512:(g + 1) * 512].rearrange("p (h k) -> p h k", h=8),
                                kt[:, bass.ds(at, S)].unsqueeze(1).to_broadcast([P, 8, S]),
                                hm[:, 8 * g:8 * g + 8].unsqueeze(2).to_broadcast([P, 8, S]), ALU.mult)
                        ins.then_inc(s["km_ready"], 16 // H)

                def context(t):
                    if later(0, t):
                        pool.wait_ge(s["va_done"], t)
                    pool.tensor_copy(ctv[:, :].rearrange("p (b k) -> p b k", b=2),
                                     cx[:, bass.ds(t, 1), :, 0:S].rearrange("p a b k -> p (a b) k")
                                     ).then_inc(s["ctv_ready"], 1)

                if l != 2:
                    pool.wait_ge(s["k_ready"], l + 1 if l < 2 else 3)
                    mask_keys(0)
                    mask_keys(1)
                else:
                    pool.wait_ge(s["x_ready"], 2 * T)
                    pool.memset(km[:, :, :].rearrange("p b n -> p (b n)"), 0.0).then_inc(s["k2_zeroed"], 1)
                    context(0)
                pool.wait_ge(s["xn_ready"], T * (2 * l + 1))
                a = PARAMS["bo"][0] + l * P
                pool.tensor_tensor(X[:, :, :], X[:, :, :],
                                   par[:, a:a + P].unsqueeze(1).to_broadcast([P, T, P]),
                                   ALU.add).then_inc(s["bo_added"], 1)
                with pool.Fori(1 if l == 2 else 2, T) as i:
                    if l == 2:
                        context(i)
                    else:
                        mask_keys(i)
                def cut_weights(e, u):
                    pool.wait_ge(s[f"pack{u}_loaded"], (e - u) * 8 + 16 * (E // 2 * l + 1))
                    if l or not isinstance(e, int) or e > 1:
                        pool.wait_ge(s["down_done"], e * CHUNKS[l] + (CHUNK_BASE[l] - CHUNKS[l])
                                     if not isinstance(e, int) or e > 1 else CHUNK_BASE[l])
                    W, M = PACK[l], CUT[l] - PACK[l]
                    ins = pool.tensor_tensor(whi[u][:, M:M + W], pack[u][:, 0:W], one[:, :].to_broadcast([P, W]),
                                             ALU.mult)
                    if M:
                        made = wba[:, bass.ds(e, 1), :].rearrange("p a f -> p (a f)")
                        ins = pool.tensor_tensor(whi[u][:, 0:M], made, one[:, :].to_broadcast([P, M]), ALU.mult)
                    ins.then_inc(s["pool_step"], 1)
                    pool.wait_ge(s["pool_step"], e + (l * E + 1))
                    ins = pool.tensor_tensor(wlo[u][:, M:M + W], pack[u][:, 0:W], whi[u][:, M:M + W].bitcast(F32),
                                             ALU.subtract)
                    if M:
                        ins = pool.tensor_tensor(wlo[u][:, 0:M], made, whi[u][:, 0:M].bitcast(F32), ALU.subtract)
                    ins.then_inc(s["w_ready"], 1)

                if l == 0:
                    pool.wait_ge(s["wba_ready"], 4)
                for u in range(2):
                    cut_weights(u, u)
                if l:
                    pool.wait_ge(s["gu_done"], CHUNK_BASE[l])
                pool.wait_ge(s["xhi_ready"], l + 1)
                pool.tensor_tensor(xlo[:, :], xnT[:, :], xhi[:, :].bitcast(F32),
                                   ALU.subtract).then_inc(s["xlo_ready"], 1)
                with pool.Fori(1, E // 2) as i:
                    for u in range(2):
                        cut_weights(i * 2 + u, u)

        @block.tensor
        def _(pe):
            pe.wait_ge(s["load_con"], 16)
            pe.wait_ge(s["load_w0"], 16)
            pe.wait_ge(s["load_cx"], 16)

            def norm_transpose(k):
                for t in range(T):
                    pe.wait_ge(s["xn_ready"], T * k + t + 1)
                    mm = pe.transpose(psT2[:, t // 4, (t % 4) * P:(t % 4 + 1) * P], XC[:, t, :], c("ident"))
                    if t % 4 == 3:
                        mm.then_inc(s["xnT_done"], 1)

            def keys_values(l):
                for h in range(2):
                    if l == 0:
                        src = cx0[:, h * HALF:(h + 1) * HALF].rearrange("p (t k) -> p t k", k=S)
                    else:
                        src = cx[:, 4 * h:4 * h + 4, :, 0:S].rearrange("p t b k -> p (t b) k")
                    mm = pe.matmul(psW[:, h, :].rearrange("p (t k) -> p t k", k=S), attn_w(l, 1), src,
                                   start=True, stop=True)
                mm.then_inc(s["k_done"], 1)
                if l == 0:
                    pe.wait_ge(s["cx_ready"], 1)
                for t in range(T):
                    for b in range(2):
                        mm = pe.matmul(psH[:, t // 2, (2 * (t % 2) + b) * P:(2 * (t % 2) + b + 1) * P],
                                       cx[:, t, b, :], attn_w(l, 2), start=True, stop=True)
                    if t % 2:
                        mm.then_inc(s["v_done"], 1)

            def small_attention(l):
                H, dk = HEADS[l], DK[l]
                G = H * S // 512
                n0, a0 = n_small(l), l * T

                def queries(t):
                    if isinstance(t, int) and t == 2:
                        pe.wait_ge(s["xnT_ready"], 4 * l + 2)
                    if later(l, t):
                        pe.wait_ge(s["q_ready"], n0 + t)
                    pe.matmul(psA[:, 0:P], attn_w(l, 0), tile(xnT, t), start=True,
                              stop=True).then_inc(s["q_done"], 1)

                def scores(t, g):
                    n, last = n0 + t, g == G - 1
                    pe.wait_ge(s["km_ready"], 2 * n + (g + 1) * (2 // G))
                    if g == 0:
                        pe.wait_ge(s["q_ready"], n + 1)
                    if later(l, t):
                        pe.wait_ge(s["sub_done"], a0 + t) if last else pe.wait_ge(s["sub0_done"], n)
                    for b in range(2):
                        mm = pe.matmul(psS[b * S:(b + 1) * S, g, :], qt[:, b * S:(b + 1) * S],
                                       km[:, b, g * 512:(g + 1) * 512], start=True, stop=(l == 3),
                                       skip_group_check=True)
                    if l < 3:
                        mm = pe.matmul(psS[:, g, :].rearrange("p (h k) -> p h k", h=8), bselb[:, :],
                                       mbias[:, l, bass.ds(t, 1), :].to_broadcast([2, 8, S]),
                                       start=False, stop=True, skip_group_check=True)
                    mm.then_inc(s["s_done" if last else "s0_done"], 1)

                def transpose_probs(t):
                    a = a0 + t
                    pe.wait_ge(s["exp_done"], a + 1)
                    if l == 3:
                        pe.wait_ge(s["nz_ready"], t + 1)
                    if l or not isinstance(t, int) or t > 0:
                        pe.wait_ge(s["pt_ready"], 2 * a)
                    src = pnorm if l == 3 else prob
                    for g in range(G):
                        for j in range(4):
                            k = (4 * g + j) * P
                            mm = pe.transpose(psT2[:, g, j * P:(j + 1) * P], src[:, k:k + P], c("ident"))
                        mm.then_inc(s["pt_done"], 2 // G)

                def weigh_values(t):
                    n, a = n0 + t, a0 + t
                    if n0 or not isinstance(t, int) or t > 0:
                        pe.wait_ge(s["on_ready"], n)
                    for j in range(H // 2):
                        w = PAIR[dk]
                        if j % 4 == 0:
                            pe.wait_ge(s["pt_ready"], 2 * a + (j // 4 + 1) * (2 // G))
                        mm = pe.matmul(psO[:, 2 * w * j:2 * w * (j + 1)].rearrange("p (b c) -> p b c", b=2),
                                       probT[:, j, :],
                                       v2[dk][:, bass.ds(t, 1), :, w * j:w * (j + 1)].rearrange("p a b c -> p (a b) c"),
                                       start=True, stop=True, skip_group_check=True)
                    mm.then_inc(s["pv_done"], 1)

                def turn_output(t):
                    pe.wait_ge(s["on_ready"], n0 + t + 1)
                    if later(l, t):
                        pe.wait_ge(s["resid_done"], a0 + t)
                    pe.transpose(psM[:, 0:P], on[:, :], c("ident")).then_inc(s["ot_done"], 1)

                def output(t):
                    pe.wait_ge(s["ot_ready"], n0 + t + 1)
                    pe.matmul(psM[:, P:2 * P], oT[:, 0, :], attn_w(l, 3), start=True,
                              stop=True).then_inc(s["out_done"], 1)

                def body(out, fin, sc, pre):
                    if sc is not None:
                        scores(sc, 0)
                    if sc is not None and G == 2:
                        scores(sc, 1)
                    if out is not None:
                        turn_output(out)
                    if fin is not None:
                        transpose_probs(fin)
                    if pre is not None:
                        queries(pre)
                    if out is not None:
                        output(out)
                    if fin is not None:
                        weigh_values(fin)

                pe.wait_ge(s["xnT_ready"], 4 * l + 1)
                queries(0)
                pe.wait_ge(s["consts_ready"], 1)
                if l == 0:
                    pe.wait_ge(s["mbias_ready"], 1)
                steps(pe, body)

            def wide_attention():
                l, a0 = 2, 2 * T

                def keys(t):
                    for g in range(2):
                        if later(0, t):
                            pe.wait_ge(s["q2_ready"], 2 * t - 1 + g)
                        for j in range(4 * g, 4 * g + 4):
                            mm = pe.matmul(psKV[:, g, (j % 4) * P:(j % 4 + 1) * P].rearrange("p (b k) -> p b k", b=2),
                                           wid[:, 1024 + j * P:1024 + (j + 1) * P],
                                           cx[:, bass.ds(t, 1), :, 0:S].rearrange("p a b k -> p (a b) k"),
                                           start=True, stop=True)
                        mm.then_inc(s["k2_done"], 1)

                def queries(t, v_before):
                    for g in range(2):
                        if v_before is None:
                            pe.wait_ge(s["k2_ready"], 2 * t + 1 + g)
                        else:
                            pe.wait_ge(s["va_ready"], 2 * v_before + 1 + g)
                        for j in range(4 * g, 4 * g + 4):
                            mm = pe.matmul(psKV[:, g, (j % 4) * P:(j % 4 + 1) * P],
                                           wid[:, j * P:(j + 1) * P], tile(xnT, t), start=True, stop=True)
                        mm.then_inc(s["q2_done"], 1)

                def values(t, k_before):
                    pe.wait_ge(s["ctv_ready"], t + 1)
                    for b in range(2):
                        if k_before is not None:
                            pe.wait_ge(s["k2_ready"], 2 * k_before + 1 + b)
                        for par_ in range(2):
                            mm = pe.matmul(psKV[par_ * S:(par_ + 1) * S, b, :], ctv[:, b * S:(b + 1) * S],
                                           wid[:, 2048 + par_ * 512:2048 + (par_ + 1) * 512],
                                           start=True, stop=True, skip_group_check=True)
                        mm.then_inc(s["va_done" if b else "va0_done"], 1)

                def scores(t):
                    pe.wait_ge(s["q2_ready"], 2 * t + 2)
                    pe.wait_ge(s["k2_ready"], 2 * t + 2)
                    pe.wait_ge(s["sub_done"], a0 + t)
                    for j in range(8):
                        for b in range(2):
                            mm = pe.matmul(psS[b * S:(b + 1) * S, j // 4, (j % 4) * P:(j % 4 + 1) * P],
                                           qt2[:, j, b * S:(b + 1) * S],
                                           kt2[:, j, b, :, :].rearrange("p h k -> p (h k)"),
                                           start=True, stop=True, skip_group_check=True)
                    mm.then_inc(s["s_done"], 1)

                def transpose_probs(t):
                    pe.wait_ge(s["pn_ready"], t + 1)
                    pe.wait_ge(s["pt_ready"], 2 * (a0 + t))
                    for g in range(2):
                        for j in range(4):
                            k = (4 * g + j) * P
                            mm = pe.transpose(psT2[:, g, j * P:(j + 1) * P], pnorm[:, k:k + P], c("ident"))
                        mm.then_inc(s["pt_done"], 1)

                def weigh_values(t):
                    pe.wait_ge(s["pt_ready"], 2 * (a0 + t) + 2)
                    pe.wait_ge(s["va_ready"], 2 * t + 2)
                    if not isinstance(t, int) or t > 0:
                        pe.wait_ge(s["resid_done"], a0 + t)
                    for j in range(8):
                        for b in range(2):
                            for h in range(2):
                                rows = slice(h * S, (h + 1) * S)
                                m = 2 if j == b == h == 0 else 1
                                mm = pe.matmul(psO2[h * S:(h + m) * S, b, j * S:(j + 1) * S],
                                               va2[rows, b, j:j + m, :].rearrange("p j d -> p (j d)"),
                                               probT[rows, j, b * S:(b + 1) * S],
                                               start=True, stop=True, skip_group_check=True)
                    mm.then_inc(s["pv_done"], 1)

                def output(t):
                    pe.wait_ge(s["ot2_ready"], 2 * t + 2)
                    for j in range(8):
                        mm = pe.matmul(psO2[:, 0, 0:P], oT[:, j, :], wid[:, 3072 + j * P:3072 + (j + 1) * P],
                                       start=(j == 0), stop=(j == 7))
                    mm.then_inc(s["out_done"], 1)

                def body(out, fin, sc, pre):
                    if sc is not None:
                        scores(sc)
                    if pre is not None:
                        keys(pre)
                        if out is not None:
                            output(out)
                    if fin is not None:
                        transpose_probs(fin)
                        values(fin, pre)
                    if out is not None and pre is None:
                        output(out)
                    if pre is not None:
                        queries(pre, fin)
                    if fin is not None:
                        weigh_values(fin)

                pe.wait_ge(s["load_wide"], 16)
                pe.wait_ge(s["x_ready"], 2 * T)
                keys(0)
                norm_transpose(2 * l)
                pe.wait_ge(s["xnT_ready"], 4 * l + 1)
                queries(0, None)
                pe.wait_ge(s["xnT_ready"], 4 * l + 2)
                steps(pe, body)

            def route(l):
                pe.wait_ge(s["xnT_ready"], 4 * l + 3)
                pe.wait_ge(s["resid_done"], (l + 1) * T)
                if l == 0:
                    a, b = PARAMS["wa"]
                    for t in range(T):
                        if t == 4:
                            pe.wait_ge(s["xnT_ready"], 4)
                        if t == 2:
                            pe.wait_ge(s["xhi_ready"], 1)
                        if t >= 4:
                            pe.wait_ge(s["sq_ready"], t - 3)
                        pe.matmul(psH[:, t % 4, :], xnT[:, t * P:(t + 1) * P], par[:, a:b],
                                  start=True, stop=True).then_inc(s["nat_done"], 1)
                else:
                    for t in range(T):
                        if t == 4:
                            pe.wait_ge(s["xnT_ready"], 4 * l + 4)
                        mm = pe.matmul(psW[:, 0, t * E:(t + 1) * E], xnT[:, t * P:(t + 1) * P], p(f"wg{l}"),
                                       start=True, stop=True)
                    mm.then_inc(s["route_done"], 1)
                for t in range(T):
                    mm = pe.matmul(psY[:, t // 4, (t % 4) * P:(t % 4 + 1) * P], X[:, t, :], c("ident"),
                                   start=(t % 4 == 0), stop=False, skip_group_check=True)
                if l == 3:
                    pe.wait_ge(s["cum_in"], 1)
                    pe.matmul(psW[:, 1, 0:T * E], beforeb[:, :], keepb[:, :, :].rearrange("p t e -> p (t e)"),
                              start=True, stop=False)
                    pe.matmul(psW[:, 1, 0:T * E], onesb[:, :], cumb[:, :, :].rearrange("p t e -> p (t e)"),
                              start=False, stop=True).then_inc(s["cum_done"], 1)

            def gate_factors():
                pe.wait_ge(s["load_wb"], 16)
                pe.wait_ge(s["load_par"], 16)
                pe.wait_ge(s["sub0_done"], T)
                pe.wait_ge(s["sub_done"], T)
                pe.wait_ge(s["q_ready"], T)
                a = PARAMS["wan"][0]
                for e in range(E):
                    mm = pe.matmul(PS[:, (0, 1, 4, 5)[e // 2], (e % 2) * 256:(e % 2 + 1) * 256],
                                   par[:, a + e // 2 * P:a + (e // 2 + 1) * P], wb8[:, e, :], start=True, stop=True)
                    if e % 2:
                        mm.then_inc(s["wba_done"], 1)

            def experts(l):
                tiles = row_tiles(HIDDEN[l])
                C, bufs, q0 = CHUNKS[l], BUFS[l], CHUNK_BASE[l]
                hidn = HIDDEN[l]
                if l == 0:
                    off = (0, hidn, 2 * hidn)
                elif l == 2:
                    off = (0, None, hidn)
                else:
                    off = (0, hidn, 2 * hidn)

                def spread(e):
                    start = isinstance(e, int) and e == 0
                    if not start:
                        pe.wait_ge(s["xe_ready"], l * E + e)
                    for h in range(2):
                        if start:
                            pe.wait_ge(s["wT_ready"], 2 * l + 1 + h)
                            if h == 1:
                                mm.then_inc(s["wb0_done"], 1)
                        mm = pe.matmul(psW[:, h, :], selb[:, bass.ds(e * P, P)], wT3[:, h * HALF:(h + 1) * HALF],
                                       start=True, stop=True)
                    mm.then_inc(s["wb_done"], 1)

                def three(out, hi, lo, xh, xl, **flags):
                    pe.matmul(out, hi, xh, start=flags["start"], stop=False, skip_group_check=True)
                    pe.matmul(out, hi, xl, start=False, stop=False, skip_group_check=True)
                    return pe.matmul(out, lo, xh, start=False, stop=flags["stop"], skip_group_check=True)

                def gate_product(i, k):
                    u, r, h = k // C, k % C // 2, k % 2
                    w = slice(r * P, (r + 1) * P)
                    cols = slice(h * HALF, (h + 1) * HALF)
                    return three(psH[:, k % bufs, :], whi[u][:, w], wlo[u][:, w], xhi[:, cols], xlo[:, cols],
                                 start=True, stop=True)

                def linear_product(i, k):
                    u, r, h = k // C, k % C // 2, k % 2
                    w = slice(hidn + r * P, hidn + (r + 1) * P)
                    cols = slice(h * HALF, (h + 1) * HALF)
                    return three(psH[:, 2 + k % bufs, :], whi[u][:, w], wlo[u][:, w], xehi[u][:, cols],
                                 xelo[u][:, cols], start=True, stop=True)

                def up(i, k, first):
                    u, ch = k // C, k % C
                    e = i * 2 + u
                    q = e * C + (q0 + ch)
                    early = first and k < bufs
                    if not early:
                        if ch == 0:
                            pe.wait_ge(s["w_ready"], l * E + e + 1)
                        pe.wait_ge(s["hf_done"], q - bufs + 1)
                        mm = gate_product(i, k)
                    if l != 2:
                        if first and k == 0:
                            pe.wait_ge(s["xe0_ready"], l + 1)
                        elif ch == 0 or (first and k == 1):
                            pe.wait_ge(s["xe_ready"], l * E + e + 1)
                        mm = linear_product(i, k)
                    if l != 2 or not early:
                        mm.then_inc(s["gu_done"], 1)

                def down(i, k):
                    q = (i * 2) * C + (q0 + k)
                    k = k % (2 * C)
                    u, ch = k // C, k % C
                    r, h = ch // 2, ch % 2
                    m = tiles[r]
                    pe.wait_ge(s["h_done"], q + 1)
                    w = slice(off[2] + r * P, off[2] + (r + 1) * P)
                    three(psY[:, h, :], whi[u][0:m, w], wlo[u][0:m, w], hhi[k % RING][0:m, :], hlo[k % RING][0:m, :],
                          start=False, stop=False).then_inc(s["down_done"], 1)

                def expert_pair(i, first=False):
                    for k in range(2 * C):
                        up(i, k, first)
                        if k % C == 0 and not (k and isinstance(i, int) and i == E // 2 - 1):
                            spread(i * 2 + k // C + 1)
                        if not first or k >= LAG[l]:
                            down(i, k - LAG[l])

                pe.wait_ge(s["w_ready"], l * E + 1)
                pe.wait_ge(s["xlo_ready"], l + 1)
                if l == 0:
                    pe.wait_ge(s["sel_ready"], 1)
                    pe.wait_ge(s["sq_ready"], T)
                for k in range(bufs):
                    mm = gate_product(0, k)
                    if l == 2:
                        mm.then_inc(s["gu_done"], 1)
                pe.wait_ge(s["wsplit"], l + 1)
                for t in range(T):
                    mm = pe.transpose(psW[:, t // 4, :].bitcast(BF16)[0:3 * E, (t % 4) * P:(t % 4 + 1) * P],
                                      w3[:, t, :, :].rearrange("p a e -> p (a e)"), identb[:, :])
                    if t % 4 == 3:
                        mm.then_inc(s["wT_done"], 1)
                spread(0)
                expert_pair(0, True)
                with pe.Fori(1, E // 2 - 1) as i:
                    expert_pair(i)
                expert_pair(E // 2 - 1)
                if l == 2:
                    for t in range(T):
                        mm = pe.transpose(psW[0:E, t // 4, (t % 4) * P:(t % 4 + 1) * P], wts[:, t, :], c("ident"))
                    mm.then_inc(s["w2T_done"], 1)
                for k in range(-LAG[l], 0):
                    down(E // 2, k)
                if l == 2:
                    pe.wait_ge(s["w2T_ready"], 1)
                    for h in range(2):
                        pe.matmul(psY[:, h, :], p("b2", E), wT[:, h * HALF:(h + 1) * HALF],
                                  start=False, stop=False, skip_group_check=True).then_inc(s["y_done"], 1)
                for t in range(T):
                    if t % 4 == 0:
                        pe.wait_ge(s["yT_ready"], 2 * l + 1 + t // 4)
                    mm = pe.transpose(psY[:, t // 4, (t % 4) * P:(t % 4 + 1) * P], yT[:, t * P:(t + 1) * P], c("ident"))
                    if t % 4 == 3:
                        mm.then_inc(s["xt_done"], 1)
                if l + 1 in (1, 3):
                    keys_values(l + 1)

            for l in range(LAYERS):
                if l == 2:
                    wide_attention()
                else:
                    if l == 0:
                        keys_values(0)
                    pe.wait_ge(s["kv_ready"], l + 1 if l < 2 else 3)
                    norm_transpose(2 * l)
                    small_attention(l)
                if l == 0:
                    gate_factors()
                norm_transpose(2 * l + 1)
                route(l)
                experts(l)

        @block.scalar
        def _(act):
            act.dma_start(cx0, ctxT).then_inc(s["load_cx"], 16)
            act.wait_ge(s["load_w0"], 16)

            def norm(k):
                for h in range(2):
                    act.wait_ge(s["xnT_done"], 2 * k + h + 1)
                    act.activation(xnT[:, h * HALF:(h + 1) * HALF], psT2[:, h, :], ACT.Copy).then_inc(s["xnT_ready"], 1)
                if k % 2:
                    for h in range(2):
                        a = act.activation(xhi[:, h * HALF:(h + 1) * HALF], psT2[:, h, :], ACT.Copy)
                    a.then_inc(s["xhi_ready"], 1)

            def keys_values(l):
                k, dk = (l if l < 2 else 2), DK[l]
                act.wait_ge(s["k_done"], k + 1)
                for h in range(2):
                    cols = slice(h * HALF, (h + 1) * HALF)
                    if l < 3:
                        a = act.activation(kt[:, cols], psW[:, h, :], ACT.Identity, bias=p(f"bk{l}"))
                    else:
                        a = act.activation(kt[:, cols], psW[:, h, :], ACT.Copy)
                a.then_inc(s["k_ready"], 1)
                if l == 0:
                    act.wait_ge(s["zeros_ready"], 3)
                for g in range(4):
                    act.wait_ge(s["v_done"], 4 * k + g + 1)
                    for h in range(2):
                        rows = slice(h * S, (h + 1) * S)
                        a = act.activation(
                            v2[dk][rows, 2 * g:2 * g + 2, :, :].rearrange("p t b (j c) -> p (t b) j c", c=PAIR[dk])
                            [:, :, :, h * dk:(h + 1) * dk],
                            psH[rows, g, :].rearrange("p (t j h d) -> p t j h d", t=4, h=2, d=dk)[:, :, :, h, :],
                            ACT.Copy)
                a.then_inc(s["kv_ready"], 1)

            def probs_out(l, t, G):
                a = l * T + t
                for g in range(G):
                    act.wait_ge(s["pt_done"], 2 * a + (g + 1) * (2 // G))
                    if g == 0 and (l or not isinstance(t, int) or t > 0):
                        act.wait_ge(s["pv_done"], a)
                    act.activation(probT[:, 4 * g:4 * g + 4, :].rearrange("p j q -> p (j q)"), psT2[:, g, :],
                                   ACT.Copy).then_inc(s["pt_ready"], 2 // G)

            def small_attention(l):
                H = HEADS[l]
                G = H * S // 512
                n0, a0 = n_small(l), l * T

                def queries(t):
                    act.wait_ge(s["q_done"], n0 + t + 1)
                    if later(l, t):
                        act.wait_ge(s["s_done"], a0 + t)
                    if l < 3:
                        a = act.activation(qt[:, :], psA[:, 0:P], ACT.Identity, bias=p(f"bq{l}"))
                    else:
                        a = act.activation(qt[:, :], psA[:, 0:P], ACT.Copy, scale=Q_SCALE3)
                    a.then_inc(s["q_ready"], 1)

                def exps(t):
                    a = a0 + t
                    act.wait_ge(s["sub_done"], a + 1)
                    if l or not isinstance(t, int) or t > 0:
                        act.wait_ge(s["pt_done"], 2 * a)
                    act.activation(prob[:, 0:H * S], diff[:, 0:H * S], ACT.Exp,
                                   scale=EXP_SCALE[l]).then_inc(s["exp_done"], 1)

                def out_values(t):
                    n = n0 + t
                    act.wait_ge(s["ot_done"], n + 1)
                    if not (l == 0 and isinstance(t, int) and t == 0):
                        act.wait_ge(s["out_done"], a0 + t)
                    if l < 3:
                        act.activation(oT[:, 0, :], psM[:, 0:P], ACT.Identity, bias=p(f"bv{l}")).then_inc(s["ot_ready"], 1)
                    else:
                        act.activation(oT[:, 0, :], psM[:, 0:P], ACT.Copy).then_inc(s["ot_ready"], 1)

                def body(out, fin, sc, pre):
                    if out is not None:
                        out_values(out)
                    if fin is not None:
                        probs_out(l, fin, G)
                    if pre is not None:
                        queries(pre)
                    if sc is not None:
                        exps(sc)

                queries(0)
                steps(act, body)

            def wide_attention():
                a0 = 2 * T

                def exps(t):
                    act.wait_ge(s["sub_done"], a0 + t + 1)
                    act.wait_ge(s["pn_ready"], t)
                    act.activation(prob[:, :], diff[:, :], ACT.Exp, scale=EXP_SCALE[2]).then_inc(s["exp_done"], 1)

                def values_out(t):
                    act.wait_ge(s["pv_done"], a0 + t)
                    for b in range(2):
                        act.wait_ge(s["va_done" if b else "va0_done"], t + 1)
                        act.activation(va2[:, b, :, :].rearrange("p j d -> p (j d)"), psKV[:, b, :],
                                       ACT.Copy).then_inc(s["va_ready"], 1)

                def out_values(t):
                    act.wait_ge(s["pv_done"], a0 + t + 1)
                    act.wait_ge(s["out_done"], a0 + t)
                    src = psO2[:, :, :].rearrange("p b (j q) -> p j b q", j=8)
                    for g in range(2):
                        for j in range(4 * g, 4 * g + 4):
                            bv = PARAMS["bv2"][0] + j
                            a = act.activation(oT[:, j, :].rearrange("p (b q) -> p b q", b=2), src[:, j, :, :],
                                               ACT.Identity, bias=par[:, bv:bv + 1])
                        a.then_inc(s["ot2_ready"], 1)

                def body(out, fin, sc, pre):
                    if out is not None:
                        out_values(out)
                    if sc is not None:
                        exps(sc)
                    if fin is not None:
                        probs_out(2, fin, 2)
                        values_out(fin)

                steps(act, body)

            def route(l):
                if l == 0:
                    for t in range(T):
                        act.wait_ge(s["nat_done"], t + 1)
                        if t >= RING:
                            act.wait_ge(s["ssq_ready"], t - RING + 1)
                        act.activation(act_s[t % RING][:, :], psH[:, t % 4, :], ACT.Square).then_inc(s["sq_ready"], 1)
                    act.wait_ge(s["ssq_ready"], T)
                    act.activation(score_r[:, :, :].rearrange("p t e -> p (t e)"),
                                   square_sum[:, :, :].rearrange("p t e -> p (t e)"), ACT.Sqrt).then_inc(s["root_ready"], 1)
                act.wait_ge(s["ex_in"], l + 1)
                act.activation(exps_r[:, :, :].rearrange("p t e -> p (t e)"), below_top[:, :, :].rearrange("p t e -> p (t e)"),
                               ACT.Exp).then_inc(s["ex_done"], 1)
                for h in range(2):
                    act.wait_ge(s["wT_done"], 2 * l + 1 + h)
                    act.activation(wT3[:, h * HALF:(h + 1) * HALF], psW[0:3 * E, h, :].bitcast(BF16)[:, 0:HALF],
                                   ACT.Copy).then_inc(s["wT_ready"], 1)

            def experts(l):
                tiles = row_tiles(HIDDEN[l])
                C, bufs, q0 = CHUNKS[l], BUFS[l], CHUNK_BASE[l]

                def activate(i, k, first):
                    u, ch = k // C, k % C
                    m = tiles[ch // 2]
                    q = (i * 2) * C + (q0 + k)
                    if l == 2 and ch == 0:
                        act.wait_ge(s[f"pack{u}_loaded"], i * 16 + 16 * (E // 2 * l + 1))
                    act.wait_ge(s["gu_done"], q + 1)
                    if not (first and k < RING):
                        act.wait_ge(s["hf_done"], q - RING + 1)
                    dst = act_s[k % RING][0:m, :]
                    src = psH[0:m, k % bufs, :]
                    if l == 2:
                        b1 = HIDDEN[2] + 4 * P + ch // 2
                        a = act.activation(dst, src, ACT.Relu, bias=pack[u][:, b1:b1 + 1])
                    else:
                        a = act.activation(dst, src, ACT.Silu)
                    a.then_inc(s["act_done"], 1)

                def hidden_hi(i, k, first):
                    m = tiles[(k % C) // 2]
                    q = (i * 2) * C + (q0 + k)
                    k = k % (2 * C)
                    act.wait_ge(s["hf_done"], q + 1)
                    if not (first and k < RING):
                        act.wait_ge(s["down_done"], q - RING + 1)
                    act.activation(hhi[k % RING][0:m, :], hid[k % RING][0:m, :], ACT.Copy).then_inc(s["hhi_done"], 1)

                def expert_pair(i, first=False):
                    for k in range(2 * C):
                        activate(i, k, first)
                        if not first or k >= 1:
                            hidden_hi(i, k - 1, first)

                expert_pair(0, True)
                with act.Fori(1, E // 2 - 1) as i:
                    expert_pair(i)
                expert_pair(E // 2 - 1)
                hidden_hi(E // 2, -1, False)
                if l == 2:
                    act.wait_ge(s["w2T_done"], 1)
                    for h in range(2):
                        a = act.activation(wT[:, h * HALF:(h + 1) * HALF], psW[0:E, h, :], ACT.Copy)
                    a.then_inc(s["w2T_ready"], 1)
                for h in range(2):
                    act.wait_ge(s["down_done"], q0 + E * C - 1 + h)
                    if l == 2:
                        act.wait_ge(s["y_done"], 1 + h)
                    act.activation(yT[:, h * HALF:(h + 1) * HALF], psY[:, h, :], ACT.Copy).then_inc(s["yT_ready"], 1)
                for h in range(2):
                    act.wait_ge(s["xt_done"], 2 * l + 1 + h)
                    if l + 1 < LAYERS:
                        act.wait_ge(s["xstat_done"], 2 * l + 1 + h)
                    act.activation(X[:, 4 * h:4 * h + 4, :].rearrange("p t d -> p (t d)"), psY[:, h, :],
                                   ACT.Copy).then_inc(s["x_ready"], T // 2)
                if l + 1 in (1, 3):
                    keys_values(l + 1)

            for l in range(LAYERS):
                if l == 0:
                    keys_values(0)
                norm(2 * l)
                if l == 2:
                    wide_attention()
                else:
                    small_attention(l)
                if l == 0:
                    for k in range(4):
                        act.wait_ge(s["wba_done"], k + 1)
                        act.activation(wba[:, 2 * k:2 * k + 2, :].rearrange("p e f -> p (e f)"),
                                       PS[:, (0, 1, 4, 5)[k], :], ACT.Copy).then_inc(s["wba_ready"], 1)
                norm(2 * l + 1)
                route(l)
                experts(l)

        @block.vector
        def _(dve):
            step = {"n": 0}

            def link(ins):
                step["n"] = step["n"] + 1
                ins.then_inc(s["dve_step"], 1)
                dve.wait_ge(s["dve_step"], step["n"])

            def add_mask_bias():
                dve.wait_ge(s["load_mask"], 32)
                dve.tensor_scalar(mbias[:, :, :, :].rearrange("b l t k -> b (l t k)"),
                                  mrow[:, :, :].rearrange("b l n -> b (l n)"), MASKED, -MASKED,
                                  ALU.mult, ALU.add).then_inc(s["mbias_ready"], 1)

            def add_to_residual(t, product):
                now = X[:, bass.ds(t, 1), :].rearrange("p a d -> p (a d)")
                link(dve.tensor_tensor(xsum[:, :], now, product, ALU.add))
                link(dve.bn_stats(bn[:, :], xsum[:, :]))
                dve.tensor_copy(bns[:, bass.ds(t, 1), :].rearrange("p a s -> p (a s)"), bn[:, :])
                dve.tensor_copy(now, xsum[:, :]).then_inc(s["resid_done"], 1)

            def norm(k):
                var, y, y2, h = root[:, 0, :], root[:, 1, :], root[:, 2, :], root[:, 3, :]
                for t in range(T):
                    ins = dve.bn_aggr(stat[:, t, :], bns[:, t, :])
                link(ins)
                link(dve.tensor_scalar(var, stat[:, :, 1], EPS, None, ALU.add))
                link(dve.tensor_scalar(h.bitcast(I32), var.bitcast(I32), 1, None, ALU.logical_shift_right))
                link(dve.tensor_scalar(y.bitcast(I32), h.bitcast(I32), -1, MAGIC, ALU.mult, ALU.add))
                for _ in range(3):
                    link(dve.tensor_tensor(y2, y, y, ALU.mult))
                    link(dve.scalar_tensor_tensor(h, y2, -0.5, var, ALU.mult, ALU.mult))
                    link(dve.scalar_tensor_tensor(y, h, 1.5, y, ALU.add, ALU.mult))
                if k:
                    dve.wait_ge(s["xnT_done"], 2 * k)
                    if k % 2 == 0:
                        dve.wait_ge(s["x_ready"], k // 2 * T)
                for t in range(T):
                    dve.tensor_scalar(XC[:, t, :], X[:, t, :], stat[:, t, 0:1], root[:, 1, t:t + 1],
                                      ALU.subtract, ALU.mult).then_inc(s["xn_ready"], 1)

            def loop_steps(body, links):
                body(None, None, 0, 1)
                body(None, 0, 1, 2)
                body(0, 1, 2, 3)
                base = step["n"]
                with dve.Fori(3, T - 1) as i:
                    step["n"] = (i - 3) * links + base
                    body(i - 2, i - 1, i, i + 1)
                step["n"] = base + (T - 4) * links
                body(T - 3, T - 2, T - 1, None)
                body(T - 2, T - 1, None, None)
                body(T - 1, None, None, None)

            def heads(ap, H):
                return ap.rearrange("p (h k) -> p h k", h=H)

            def small_attention(l):
                H, dk = HEADS[l], DK[l]
                G = H * S // 512
                n0, a0 = n_small(l), l * T
                W = H * S
                if l == 3:
                    dve.wait_ge(s["load_gate"], 16)

                def softmax_in(t):
                    a, n = a0 + t, n0 + t
                    for g in range(G):
                        last = g == G - 1
                        dve.wait_ge(s["s_done"], a + 1) if last else dve.wait_ge(s["s0_done"], n + 1)
                        src, hs = psS[:, g, :], slice(8 * g, 8 * g + 8)
                        if l == 3:
                            if not isinstance(t, int) or t > 0:
                                dve.wait_ge(s["nz_ready"], t)
                            link(dve.tensor_tensor(heads(gated[:, :], 8), heads(src, 8),
                                                   gat[:, bass.ds(t, 1), :].to_broadcast([P, 8, S]), ALU.mult))
                            src = gated[:, :]
                        link(dve.tensor_reduce(mx[:, hs], heads(src, 8), AX.X, ALU.max))
                        if g == 0 and (l or not isinstance(t, int) or t > 0):
                            dve.wait_ge(s["exp_done"], a)
                        dve.tensor_tensor(heads(diff[:, g * 512:(g + 1) * 512], 8), heads(src, 8),
                                          mx[:, hs].unsqueeze(2).to_broadcast([P, 8, S]),
                                          ALU.subtract).then_inc(s["sub_done" if last else "sub0_done"], 1)

                def normalise_out(t):
                    n = n0 + t
                    dve.wait_ge(s["pv_done"], a0 + t + 1)
                    w = PAIR[dk]
                    blocks = psO[:, 0:w * H].rearrange("p (j b c) -> p j b c", b=2, c=w)
                    if l < 3:
                        for b in range(2):
                            q = slice(b * S, (b + 1) * S)
                            ins = dve.reciprocal(sm[q, 1, 0:H].rearrange("p (j h) -> p j h", h=2),
                                                 blocks[q, :, b, 2 * dk:2 * dk + 2])
                        link(ins)
                    if not (l == 0 and isinstance(t, int) and t == 0):
                        dve.wait_ge(s["ot_done"], n)
                    for b in range(2):
                        q = slice(b * S, (b + 1) * S)
                        ins = dve.tensor_tensor(
                            on[q, :].rearrange("p (j h d) -> p j h d", h=2, d=dk),
                            blocks[q, :, b, 0:2 * dk].rearrange("p j (h d) -> p j h d", h=2),
                            sm[q, 1, 0:H].rearrange("p (j h) -> p j h", h=2).unsqueeze(3)
                              .to_broadcast([S, H // 2, 2, dk]), ALU.mult)
                    ins.then_inc(s["on_ready"], 1)

                def sums(t):
                    a = a0 + t
                    dve.wait_ge(s["exp_done"], a + 1)
                    link(dve.tensor_reduce(sm[:, 0, 0:H], heads(prob[:, 0:W], H), AX.X, ALU.add))
                    link(dve.reciprocal(sm[:, 1, 0:H], sm[:, 0, 0:H]))
                    dve.wait_ge(s["pt_done"], 2 * a)
                    dve.scalar_tensor_tensor(pnorm[:, 0:W], gated[:, :], 0.0, prob[:, 0:W],
                                             ALU.not_equal, ALU.mult).then_inc(s["nz_ready"], 1)

                def residual(t):
                    if isinstance(t, int) and t == 0:
                        dve.wait_ge(s["bo_added"], l + 1)
                    a = a0 + t
                    dve.wait_ge(s["out_done"], a + 1)
                    add_to_residual(t, psM[:, P:2 * P])

                def body(out, fin, sc, pre):
                    if sc is not None:
                        softmax_in(sc)
                    if out is not None:
                        residual(out)
                    if fin is not None:
                        normalise_out(fin)
                    if sc is not None and l == 3:
                        sums(sc)

                loop_steps(body, 6 if l == 3 else 5)

            def wide_attention():
                a0 = 2 * T

                def keys(t):
                    if later(0, t):
                        dve.wait_ge(s["s_done"], a0 + t)
                    for g in range(2):
                        dve.wait_ge(s["k2_done"], 2 * t + g + 1)
                        a = PARAMS["bk2"][0] + 4 * g
                        for h in range(2):
                            rows = slice(h * S, (h + 1) * S)
                            ins = dve.tensor_tensor(kt2[rows, 4 * g:4 * g + 4, :, h, :],
                                                    psKV[rows, g, :].rearrange("p (j b k) -> p j b k", j=4, b=2),
                                                    par[rows, a:a + 4].unsqueeze(2).unsqueeze(3)
                                                      .to_broadcast([S, 4, 2, S]), ALU.add)
                        ins.then_inc(s["k2_ready"], 1)

                def queries(t):
                    for g in range(2):
                        dve.wait_ge(s["q2_done"], 2 * t + g + 1)
                        a = PARAMS["bq2"][0] + 4 * g
                        dve.tensor_tensor(qt2[:, 4 * g:4 * g + 4, :], psKV[:, g, :].rearrange("p (j q) -> p j q", j=4),
                                          par[:, a:a + 4].unsqueeze(2).to_broadcast([P, 4, P]),
                                          ALU.add).then_inc(s["q2_ready"], 1)

                dve.wait_ge(s["k2_zeroed"], 1)
                keys(0)

                def softmax_in(t):
                    a = a0 + t
                    dve.wait_ge(s["s_done"], a + 1)
                    src = heads(psS[:, :, :].rearrange("p g n -> p (g n)"), 16)
                    link(dve.tensor_reduce(mx[:, :], src, AX.X, ALU.max))
                    dve.wait_ge(s["exp_done"], a)
                    dve.tensor_tensor(heads(diff[:, :], 16), src, mx[:, :].unsqueeze(2).to_broadcast([P, 16, S]),
                                      ALU.subtract).then_inc(s["sub_done"], 1)

                def normalise(t):
                    a = a0 + t
                    dve.wait_ge(s["exp_done"], a + 1)
                    link(dve.tensor_reduce(sm[:, 0, :], heads(prob[:, :], 16), AX.X, ALU.add))
                    link(dve.reciprocal(sm[:, 1, :], sm[:, 0, :]))
                    dve.wait_ge(s["pt_done"], 2 * a)
                    dve.tensor_tensor(heads(pnorm[:, :], 16), heads(prob[:, :], 16),
                                      sm[:, 1, :].unsqueeze(2).to_broadcast([P, 16, S]),
                                      ALU.mult).then_inc(s["pn_ready"], 1)

                def residual(t):
                    if isinstance(t, int) and t == 0:
                        dve.wait_ge(s["bo_added"], l + 1)
                    dve.wait_ge(s["out_done"], a0 + t + 1)
                    add_to_residual(t, psO2[:, 0, 0:P])

                def body(out, fin, sc, pre):
                    if sc is not None:
                        softmax_in(sc)
                    if pre is not None:
                        keys(pre)
                    if out is not None:
                        residual(out)
                    if pre is not None:
                        queries(pre)
                    if sc is not None:
                        normalise(sc)

                queries(0)
                loop_steps(body, 5)

            def flat(ap):
                return ap[:, :, :].rearrange("p t e -> p (t e)")

            def over_experts(ap):
                return ap.unsqueeze(2).to_broadcast([P, T, E])

            def route(l):
                score, top, keep = score_r, rs[:, 0, :], keep_r
                if l:
                    dve.wait_ge(s["route_done"], l)
                src = psW[:, 0, 0:T * E]
                if l == 0:
                    for t in range(T):
                        dve.wait_ge(s["sq_ready"], t + 1)
                        dve.tensor_reduce(square_sum[:, t, :], act_s[t % RING][:, :].rearrange("p (e r) -> p e r", e=E),
                                          AX.X, ALU.add).then_inc(s["ssq_ready"], 1)
                    dve.wait_ge(s["root_ready"], 1)
                elif l == 2:
                    link(dve.tensor_tensor(score[:, :, :], src.rearrange("p (t e) -> p t e", t=T),
                                           p("rb2").unsqueeze(1).to_broadcast([P, T, E]), ALU.add))
                else:
                    link(dve.tensor_copy(flat(score), src))
                link(dve.tensor_reduce(top, score[:, :, :], AX.X, ALU.max))
                dve.tensor_tensor(below_top[:, :, :], score[:, :, :], over_experts(top),
                                  ALU.subtract).then_inc(s["ex_in"], 1)
                dve.wait_ge(s["ex_done"], l + 1)
                ex = exps_r
                if l in (1, 3):
                    link(dve.tensor_reduce(rs[:, 1, :], ex[:, :, :], AX.X, ALU.add))
                    link(dve.reciprocal(rs[:, 1, :], rs[:, 1, :]))
                    link(dve.tensor_tensor(ex[:, :, :], ex[:, :, :], over_experts(rs[:, 1, :]), ALU.mult))
                    score = ex
                other = score[:, :, :].unsqueeze(2).to_broadcast([P, T, E, E])
                own = score[:, :, :].unsqueeze(3).to_broadcast([P, T, E, E])
                link(dve.tensor_tensor(cmp1[:, :, :, :], other, own, ALU.is_gt))
                link(dve.tensor_tensor(cmp1[:, :, :, :].rearrange("p t a b -> p t (a b)"),
                                       cmp1[:, :, :, :].rearrange("p t a b -> p t (a b)"),
                                       c("upper").unsqueeze(1).to_broadcast([P, T, E * E]), ALU.mult))
                link(dve.tensor_tensor(cmp2[:, :, :, :], cmp1[:, :, :, :],
                                       cmp1[:, :, :, :].rearrange("p t a b -> p t b a"), ALU.subtract))
                link(dve.tensor_reduce(flat(rank_r), cmp2[:, :, :, :].rearrange("p t a b -> p (t a) b"), AX.X, ALU.add))
                link(dve.tensor_tensor(keep[:, :, :], rank_r[:, :, :], c("limit").unsqueeze(1).to_broadcast([P, T, E]),
                                       ALU.is_lt))
                if l == 3:
                    dve.tensor_copy(keepb[:, :, :], keep[:, :, :])
                    link(dve.memset(cumb[:, 0, :], 0.0))
                    for t in range(1, T):
                        ins = dve.tensor_tensor(cumb[:, t, :], cumb[:, t - 1, :], keep[:, t - 1, :], ALU.add)
                        if t < T - 1:
                            link(ins)
                    ins.then_inc(s["cum_in"], 1)
                if l == 3:
                    link(dve.tensor_tensor(wts[:, :, :], ex[:, :, :], keep[:, :, :], ALU.mult))
                    dve.wait_ge(s["cum_done"], 1)
                    link(dve.scalar_tensor_tensor(flat(wts), psW[:, 1, 0:T * E], CAPACITY - 0.5, flat(wts),
                                                  ALU.is_lt, ALU.mult))
                else:
                    link(dve.tensor_tensor(ex[:, :, :], ex[:, :, :], keep[:, :, :], ALU.mult))
                    link(dve.tensor_reduce(rs[:, 0, :], ex[:, :, :], AX.X, ALU.add))
                    if l == 1:
                        link(dve.tensor_scalar(rs[:, 0, :], rs[:, 0, :], 1e-20, None, ALU.add))
                    link(dve.reciprocal(rs[:, 1, :], rs[:, 0, :]))
                    link(dve.tensor_tensor(wts[:, :, :], ex[:, :, :], over_experts(rs[:, 1, :]), ALU.mult))
                link(dve.tensor_copy(w3[:, :, 0, :], wts[:, :, :]))
                dve.tensor_tensor(w3[:, :, 1, :], wts[:, :, :], w3[:, :, 0, :], ALU.subtract)
                link(dve.tensor_tensor(wres[:, :, :], wts[:, :, :], w3[:, :, 0, :], ALU.subtract))
                dve.tensor_tensor(w3[:, :, 2, :], wres[:, :, :], w3[:, :, 1, :],
                                  ALU.subtract).then_inc(s["wsplit"], 1)

            def experts(l):
                tiles = row_tiles(HIDDEN[l])
                C, bufs, q0 = CHUNKS[l], BUFS[l], CHUNK_BASE[l]

                def weighted_input(i, k, part, first=False):
                    u = k % 2
                    e = i * 2 + k
                    w = psW[:, :, :].rearrange("p g n -> p (g n)")
                    if part == 0:
                        dve.wait_ge(s["wb_done"], l * E + e + 1)
                        if l == 2:
                            if not first:
                                dve.wait_ge(s["hf_done"], q0 + (e - 1) * C)
                            dve.tensor_copy(xe[u][:, :], w).then_inc(s["xe_ready"], 1)
                        else:
                            dve.tensor_tensor(xe[u][:, :], xnT[:, :], w, ALU.mult).then_inc(s["xe_step"], 1)
                    elif l != 2 and part == 1:
                        dve.wait_ge(s["xe_step"], 2 * (e - 1 + (E - 1) * (l if l < 3 else 2)) + 1)
                        if not first:
                            dve.wait_ge(s["gu_done"], q0 + (e - 1) * C)
                        dve.tensor_copy(xehi[u][:, :], xe[u][:, :]).then_inc(s["xe_step"], 1)
                    elif l != 2 and part == 2:
                        dve.wait_ge(s["xe_step"], 2 * (e - 1 + (E - 1) * (l if l < 3 else 2)) + 2)
                        dve.tensor_tensor(xelo[u][:, :], xe[u][:, :], xehi[u][:, :].bitcast(F32),
                                          ALU.subtract).then_inc(s["xe_ready"], 1)

                def first_input():
                    for h in range(2):
                        cols = slice(h * HALF, (h + 1) * HALF)
                        dve.wait_ge(s["wb_done"], l * E + 1) if h else dve.wait_ge(s["wb0_done"], l + 1)
                        if l == 2:
                            ins = dve.tensor_copy(xe[0][:, cols], psW[:, h, :])
                        else:
                            link(dve.tensor_tensor(xe[0][:, cols], xnT[:, cols], psW[:, h, :], ALU.mult))
                            link(dve.tensor_copy(xehi[0][:, cols], xe[0][:, cols]))
                            ins = dve.tensor_tensor(xelo[0][:, cols], xe[0][:, cols], xehi[0][:, cols].bitcast(F32),
                                                    ALU.subtract)
                        ins.then_inc(s["xe_ready" if h else "xe0_ready"], 1)

                def hidden(i, k, first):
                    u, ch = k // C, k % C
                    m = tiles[ch // 2]
                    q = (i * 2) * C + (q0 + k)
                    dve.wait_ge(s["act_done"], q + 1)
                    if not (first and k < RING):
                        dve.wait_ge(s["h_done"], q - RING + 1)
                    if l == 2:
                        other = xe[u][0:m, (ch % 2) * HALF:(ch % 2 + 1) * HALF]
                        if ch == 0:
                            dve.wait_ge(s["xe_ready"], l * E + i * 2 + u + 1)
                    else:
                        other = psH[0:m, 2 + k % bufs, :]
                    dve.tensor_tensor(hid[k % RING][0:m, :], act_s[k % RING][0:m, :], other,
                                      ALU.mult).then_inc(s["hf_done"], 1)

                def hidden_lo(i, k, first):
                    m = tiles[(k % C) // 2]
                    q = (i * 2) * C + (q0 + k)
                    k = k % (2 * C)
                    dve.wait_ge(s["hhi_done"], q + 1)
                    if not (first and k < RING):
                        dve.wait_ge(s["down_done"], q - RING + 1)
                    dve.tensor_tensor(hlo[k % RING][0:m, :], hid[k % RING][0:m, :], hhi[k % RING][0:m, :].bitcast(F32),
                                      ALU.subtract).then_inc(s["h_done"], 1)

                def expert_pair(i, first=False):
                    last = isinstance(i, int) and i == E // 2 - 1
                    for k in range(2 * C):
                        hidden(i, k, first)
                        if not first or k >= 1:
                            hidden_lo(i, k - 1, first)
                        ch = k % C
                        if ch < 3 and not (k >= C and last):
                            weighted_input(i, k // C + 1, ch, first and k < C)

                first_input()
                expert_pair(0, True)
                with dve.Fori(1, E // 2 - 1) as i:
                    expert_pair(i)
                expert_pair(E // 2 - 1)
                hidden_lo(E // 2, -1, False)
                if l + 1 < LAYERS:
                    for t in range(T):
                        if t % 4 == 0:
                            dve.wait_ge(s["xt_done"], 2 * l + 1 + t // 4)
                        ins = dve.bn_stats(bns[:, t, :], psY[:, t // 4, (t % 4) * P:(t % 4 + 1) * P])
                        if t % 4 == 3:
                            ins.then_inc(s["xstat_done"], 1)
                    dve.wait_ge(s["xstat_done"], 2 * l + 2)

            dve.wait_ge(s["load_x"], 16)
            for t in range(T):
                ins = dve.bn_stats(bns[:, t, :], X[:, t, :])
            link(ins)
            dve.wait_ge(s["load_cx"], 16)
            dve.tensor_copy(cx[:, :, :, :].rearrange("p t b (u k) -> p (t b) u k", u=2),
                            cx0.rearrange("p (n k) -> p n k", k=S).unsqueeze(2).to_broadcast([P, 2 * T, 2, S])
                            ).then_inc(s["cx_ready"], 1)
            for l in range(LAYERS):
                norm(2 * l)
                if l == 0:
                    add_mask_bias()
                    dve.wait_ge(s["load_sel"], 16)
                    dve.tensor_copy(selb[:, :], sel[:, :]).then_inc(s["sel_ready"], 1)
                if l == 2:
                    wide_attention()
                else:
                    small_attention(l)
                dve.wait_ge(s["resid_done"], (l + 1) * T)
                norm(2 * l + 1)
                route(l)
                experts(l)


def constants():
    con = np.zeros((P, N_CONST), np.float32)
    r = np.arange(P)

    def put(name, value):
        a, b = CONSTS[name]
        con[:value.shape[0], a:b] = value

    put("ident", np.eye(P))
    put("hmask8", (r[:, None] // 8 == np.arange(16)[None]))
    put("hmask16", (r[:, None] // 16 == np.arange(8)[None]))
    e = np.arange(E)
    put("upper", np.broadcast_to((e[None, :] > e[:, None]).reshape(1, E * E), (P, E * E)))
    put("limit", np.broadcast_to(1.5 - e, (P, E)))
    put("before", (r[:, None] < r[None, :]))
    put("bsel", (np.arange(2)[:, None] == r[None] // S))
    put("half", (r[:, None] // 64 == np.arange(2)[None]))
    return con


def selectors():
    e = np.arange(E)
    sel = (np.arange(3 * E)[:, None, None] % E == e[None, :, None]) * np.ones((1, 1, P))
    return sel.reshape(3 * E, E * P).astype(np.float32)


def kernel(**inputs):
    import concourse.bacc as _bacc
    from concourse.bass_utils import run_bass_kernel_spmd as _run
    i = {k: np.asarray(v) for k, v in inputs.items()}

    par = np.zeros((P, N_PARAM), np.float32)

    def put(name, value):
        a, b = PARAMS[name]
        par[:value.shape[0], a:b] = value

    put("w0", np.concatenate([i["L0_xattn_Wq"], i["L0_xattn_Wk"], i["L0_xattn_Wv"], i["L0_xattn_Wo"]], 1))
    put("w1", np.concatenate([i["L1_xattn_wq_w"].T, i["L1_xattn_wk_w"].T, i["L1_xattn_wv_w"].T,
                              i["L1_xattn_wo_w"].T], 1))
    put("w3", np.concatenate([i["L3_xattn_Wq"].T, i["L3_xattn_Wk"].T, i["L3_xattn_Wv"].T, i["L3_xattn_Wp"].T], 1))
    put("wa", i["L0_ffn_W_A"].reshape(512, P).T)
    put("wan", i["L0_ffn_W_A"].reshape(4, P, P).transpose(1, 0, 2).reshape(P, 4 * P))
    for n in "qkv":
        put(f"b{n}0", i[f"L0_xattn_b{n}"].reshape(P, 1))
        put(f"b{n}1", i[f"L1_xattn_w{n}_b"].reshape(P, 1))
        put(f"b{n}2", i[f"L2_xattn_b{n}"].reshape(8, P).T)
    bo = np.stack([i["L0_xattn_bo"], i["L1_xattn_wo_b"], i["L2_xattn_bu"], i["L3_xattn_bp"]]).reshape(1, 4 * P)
    put("bo", np.broadcast_to(bo, (P, 4 * P)))
    put("wg1", i["L1_ffn_Wg"].T)
    put("wg2", i["L2_ffn_router_w"])
    put("wg3", i["L3_ffn_w_gate"])
    put("rb2", np.broadcast_to(i["L2_ffn_router_b"].reshape(1, E), (P, E)))
    put("b2", i["L2_ffn_b2"])

    wide = np.zeros((P, N_WIDE), np.float32)
    wide[:, 0:1024] = i["L2_xattn_Wq"]
    wide[:, 1024:2048] = i["L2_xattn_Wk"]
    wide[:, 2048:3072] = i["L2_xattn_Wv"].reshape(P, 8, 2, 64).transpose(0, 2, 1, 3).reshape(P, 1024)
    wide[:, 3072:4096] = i["L2_xattn_Wu"].reshape(8, P, P).transpose(1, 0, 2).reshape(P, 1024)

    def down_tiles(w):
        e, h, d = w.shape
        t = -(-h // P)
        padded = np.zeros((e, t * P, d), np.float32)
        padded[:, :h] = w
        return padded.reshape(e, t, P, d).transpose(0, 2, 1, 3).reshape(e, P, t * d)

    wb = np.zeros((E, P, HIDDEN[0]), np.float32)
    for e in range(E):
        wb[e, 64 * (e % 2):64 * (e % 2) + 64] = i["L0_ffn_W_B"][e].T
    packs = [
        np.concatenate([i["L0_ffn_W_up"].transpose(0, 2, 1), down_tiles(i["L0_ffn_W_down"].transpose(0, 2, 1))], 2),
        np.concatenate([i["L1_ffn_W1"].transpose(0, 2, 1), i["L1_ffn_W3"].transpose(0, 2, 1),
                        down_tiles(i["L1_ffn_W2"].transpose(0, 2, 1))], 2),
        np.concatenate([i["L2_ffn_w1"], down_tiles(i["L2_ffn_w2"]),
                        i["L2_ffn_b1"].reshape(E, 4, P).transpose(0, 2, 1)], 2),
        np.concatenate([i["L3_ffn_c_fc"], down_tiles(i["L3_ffn_c_proj"])], 2),
    ]
    arrays = {
        "x": i["x"].reshape(T, P, D).transpose(1, 0, 2),
        "ctxT": i["ctx_1024"].reshape(N, D).T,
        "gate": i["fside_BxSxS2_0"].reshape(T, P, S).transpose(1, 0, 2),
        "mask0": i["mask_Bx1xS2_bf1"].reshape(T, 2, S).transpose(1, 0, 2).reshape(2, T * S).view(np.uint8),
        "mask1": i["mask_BxS2_bf1"].reshape(T, 2, S).transpose(1, 0, 2).reshape(2, T * S).view(np.uint8),
        "consts": constants(),
        "selc": selectors(),
        "params": par,
        "wb": wb.transpose(1, 0, 2).reshape(P, E * HIDDEN[0]),
        "wide": wide,
    }
    for l in range(LAYERS):
        arrays[f"pack{l}"] = packs[l]
    nc = _bacc.Bacc("TRN2", target_bir_lowering=False, num_devices=1)
    feed, aps = {}, {}
    for name, a in arrays.items():
        a = np.ascontiguousarray(a)
        feed[f"in_{name}"] = a
        aps[name] = nc.dram_tensor(f"in_{name}", a.shape, mybir.dt.from_np(a.dtype), kind="ExternalInput").ap()
    out = nc.dram_tensor("out", (P, T, D), F32, kind="ExternalOutput").ap()
    build(nc, aps["x"], aps["ctxT"], aps["gate"], aps["mask0"], aps["mask1"], aps["consts"], aps["selc"], aps["params"],
          aps["wb"], aps["wide"], [aps[f"pack{l}"] for l in range(LAYERS)], out)
    r = _run(nc, [feed], core_ids=[0])
    return r.results[0]["out"].transpose(1, 0, 2).reshape(B, S, D)
```
